# Optimizing a Trainium2 kernel written in Bass

```python
import numpy as np
import jax
import jax.numpy as jnp

def _softmax(x, axis=-1):
    return jax.nn.softmax(x, axis=axis)

def _gelu(x):
    return jax.nn.gelu(x, approximate=True)

def _silu(x):
    return jax.nn.silu(x)

def _sigmoid(x):
    return jax.nn.sigmoid(x)

def _layernorm(x, axis=-1, eps=1e-05):
    m = jnp.mean(x, axis=axis, keepdims=True)
    v = jnp.var(x, axis=axis, keepdims=True)
    return (x - m) / jnp.sqrt(v + eps)

def _scatter_add(tgt, idx, src, axis=0):
    return tgt.at[idx].add(src)

def _segment_sum(src, seg, n):
    return jax.ops.segment_sum(src, seg, n)
kernel_name = 'mk_hybrid_d1_jaxref_r8_f10d19'

def setup_inputs(seed: int=0):
    np.random.seed(seed)
    _w = jnp.asarray

    def _L0_attn_a_setup():
        import jax, jax.numpy as jnp
        import numpy as np
        NHEAD = 8
        ATTN_EPS = 1e-06
        LN_EPS = 1e-05

        def _layernorm(y, g, b):
            mu = jnp.mean(y, axis=-1, keepdims=True)
            var = jnp.var(y, axis=-1, keepdims=True)
            return (y - mu) * jax.lax.rsqrt(var + LN_EPS) * g + b
        key = jax.random.key(seed)
        ks = jax.random.split(key, 6)
        B, L, D = (2, 1024, 128)
        s = 1.0 / np.sqrt(D)
        return {'x': jax.random.normal(ks[0], (B, L, D), jnp.float32), 'Wq': jax.random.normal(ks[1], (D, D), jnp.float32) * s, 'Wm': jax.random.normal(ks[2], (D, D), jnp.float32) * s, 'W1': jax.random.normal(ks[3], (D, 2 * D), jnp.float32) * s, 'W2': jax.random.normal(ks[4], (2 * D, D), jnp.float32) * (1.0 / np.sqrt(2 * D)), 'g1': jnp.ones((D,), jnp.float32), 'b1': jnp.zeros((D,), jnp.float32), 'g2': jnp.ones((D,), jnp.float32), 'b2': jnp.zeros((D,), jnp.float32)}
    _L0_attn_a_in = _L0_attn_a_setup()

    def _L0_attn_b_setup():
        import jax, jax.numpy as jnp
        import numpy as np
        H = 16
        BUCKETS = 32
        MAX_REL = 64

        def _log_bucket(rel, bucket_size, max_position):
            mid = bucket_size // 2
            sign = jnp.sign(rel).astype(jnp.float32)
            abs_pos = jnp.where((rel < mid) & (rel > -mid), mid - 1, jnp.abs(rel)).astype(jnp.float32)
            log_pos = jnp.ceil(jnp.log(abs_pos / mid) / np.log((max_position - 1) / mid) * (mid - 1)) + mid
            bucket = jnp.where(abs_pos <= mid, rel.astype(jnp.float32), log_pos * sign)
            return bucket.astype(jnp.int32)

        def _rel_pos(seq_len):
            ids = jnp.arange(seq_len)
            rel = ids[:, None] - ids[None, :]
            return _log_bucket(rel, BUCKETS, MAX_REL)
        key = jax.random.key(seed)
        ks = jax.random.split(key, 16)
        B, S, D = (4, 128, 128)
        K2 = 2 * BUCKETS
        s = 0.02

        def lin(k, din, dout):
            return jax.random.normal(k, (din, dout), jnp.float32) * s
        return {'hidden_states': jax.random.normal(ks[0], (B, S, D), jnp.float32), 'Wq': lin(ks[1], D, D), 'bq': jnp.zeros((D,), jnp.float32), 'Wk': lin(ks[2], D, D), 'bk': jnp.zeros((D,), jnp.float32), 'Wv': lin(ks[3], D, D), 'bv': jnp.zeros((D,), jnp.float32), 'Wo': lin(ks[4], D, D), 'bo': jnp.zeros((D,), jnp.float32), 'rel_emb': jax.random.normal(ks[5], (K2, D), jnp.float32) * s, 'ln_g': jnp.ones((D,), jnp.float32), 'ln_b': jnp.zeros((D,), jnp.float32), 'Wpk': lin(ks[6], D, D), 'bpk': jnp.zeros((D,), jnp.float32), 'Wpq': lin(ks[7], D, D), 'bpq': jnp.zeros((D,), jnp.float32)}
    _L0_attn_b_in = _L0_attn_b_setup()

    def _L0_ffn_setup():
        import jax, jax.numpy as jnp
        import numpy as np
        B, S, D = (4, 256, 128)
        E, F = (8, 512)
        key = jax.random.key(seed)
        ks = jax.random.split(key, 5)
        x = jax.random.normal(ks[0], (B, S, D), dtype=jnp.float32)
        switch_w = jax.random.normal(ks[1], (D, E), dtype=jnp.float32) * D ** (-0.5)
        switch_b = jnp.zeros((E,), dtype=jnp.float32)
        w1 = jax.random.normal(ks[2], (E, D, F), dtype=jnp.float32) * D ** (-0.5)
        b1 = jnp.zeros((E, F), dtype=jnp.float32)
        w2 = jax.random.normal(ks[3], (E, F, D), dtype=jnp.float32) * F ** (-0.5)
        b2 = jnp.zeros((E, D), dtype=jnp.float32)
        return {'x': x, 'switch_w': switch_w, 'switch_b': switch_b, 'w1': w1, 'b1': b1, 'w2': w2, 'b2': b2}
    _L0_ffn_in = _L0_ffn_setup()
    _d = {'L0_attn_a_x': _L0_attn_a_in['x'], 'L0_attn_a_Wq': _L0_attn_a_in['Wq'], 'L0_attn_a_Wm': _L0_attn_a_in['Wm'], 'L0_attn_a_W1': _L0_attn_a_in['W1'], 'L0_attn_a_W2': _L0_attn_a_in['W2'], 'L0_attn_a_g1': _L0_attn_a_in['g1'], 'L0_attn_a_b1': _L0_attn_a_in['b1'], 'L0_attn_a_g2': _L0_attn_a_in['g2'], 'L0_attn_a_b2': _L0_attn_a_in['b2'], 'L0_attn_b_Wq': _L0_attn_b_in['Wq'], 'L0_attn_b_bq': _L0_attn_b_in['bq'], 'L0_attn_b_Wk': _L0_attn_b_in['Wk'], 'L0_attn_b_bk': _L0_attn_b_in['bk'], 'L0_attn_b_Wv': _L0_attn_b_in['Wv'], 'L0_attn_b_bv': _L0_attn_b_in['bv'], 'L0_attn_b_Wo': _L0_attn_b_in['Wo'], 'L0_attn_b_bo': _L0_attn_b_in['bo'], 'L0_attn_b_rel_emb': _L0_attn_b_in['rel_emb'], 'L0_attn_b_ln_g': _L0_attn_b_in['ln_g'], 'L0_attn_b_ln_b': _L0_attn_b_in['ln_b'], 'L0_attn_b_Wpk': _L0_attn_b_in['Wpk'], 'L0_attn_b_bpk': _L0_attn_b_in['bpk'], 'L0_attn_b_Wpq': _L0_attn_b_in['Wpq'], 'L0_attn_b_bpq': _L0_attn_b_in['bpq'], 'L0_ffn_switch_w': _L0_ffn_in['switch_w'], 'L0_ffn_switch_b': _L0_ffn_in['switch_b'], 'L0_ffn_w1': _L0_ffn_in['w1'], 'L0_ffn_b1': _L0_ffn_in['b1'], 'L0_ffn_w2': _L0_ffn_in['w2'], 'L0_ffn_b2': _L0_ffn_in['b2']}
    _x0 = _d['L0_attn_a_x']
    _d['L0_attn_a_x'] = jax.random.normal(jax.random.fold_in(jax.random.key(seed), 1), (16, 256, 128), dtype=_x0.dtype)
    del _x0
    return _d

def reference(L0_attn_a_x, L0_attn_a_Wq, L0_attn_a_Wm, L0_attn_a_W1, L0_attn_a_W2, L0_attn_a_g1, L0_attn_a_b1, L0_attn_a_g2, L0_attn_a_b2, L0_attn_b_Wq, L0_attn_b_bq, L0_attn_b_Wk, L0_attn_b_bk, L0_attn_b_Wv, L0_attn_b_bv, L0_attn_b_Wo, L0_attn_b_bo, L0_attn_b_rel_emb, L0_attn_b_ln_g, L0_attn_b_ln_b, L0_attn_b_Wpk, L0_attn_b_bpk, L0_attn_b_Wpq, L0_attn_b_bpq, L0_ffn_switch_w, L0_ffn_switch_b, L0_ffn_w1, L0_ffn_b1, L0_ffn_w2, L0_ffn_b2):

    def _L0_attn_a_ref(x, Wq, Wm, W1, W2, g1, b1, g2, b2):
        import jax, jax.numpy as jnp
        import numpy as np
        NHEAD = 8
        ATTN_EPS = 1e-06
        LN_EPS = 1e-05

        def _layernorm(y, g, b):
            mu = jnp.mean(y, axis=-1, keepdims=True)
            var = jnp.var(y, axis=-1, keepdims=True)
            return (y - mu) * jax.lax.rsqrt(var + LN_EPS) * g + b
        B, L, D = x.shape
        H = NHEAD
        d = D // H
        q = (x @ Wq).reshape(B, L, H, d)
        feat = jax.nn.elu(q) + 1.0
        Q = feat
        K = feat
        V = q / L
        KV = jnp.einsum('nshd,nshv->nhdv', K, V)
        Ksum = K.sum(axis=1)
        Z = 1.0 / (jnp.einsum('nlhd,nhd->nlh', Q, Ksum) + ATTN_EPS)
        msg = jnp.einsum('nlhd,nhdv,nlh->nlhv', Q, KV, Z) * L
        msg = msg.reshape(B, L, D) @ Wm
        x = x + _layernorm(msg, g1, b1)
        mlp = jax.nn.relu(msg @ W1) @ W2
        x = x + _layernorm(mlp, g2, b2)
        return x

    def _L0_attn_b_ref(hidden_states, Wq, bq, Wk, bk, Wv, bv, Wo, bo, rel_emb, ln_g, ln_b, Wpk, bpk, Wpq, bpq):
        import jax, jax.numpy as jnp
        import numpy as np
        H = 16
        BUCKETS = 32
        MAX_REL = 64

        def _log_bucket(rel, bucket_size, max_position):
            mid = bucket_size // 2
            sign = jnp.sign(rel).astype(jnp.float32)
            abs_pos = jnp.where((rel < mid) & (rel > -mid), mid - 1, jnp.abs(rel)).astype(jnp.float32)
            log_pos = jnp.ceil(jnp.log(abs_pos / mid) / np.log((max_position - 1) / mid) * (mid - 1)) + mid
            bucket = jnp.where(abs_pos <= mid, rel.astype(jnp.float32), log_pos * sign)
            return bucket.astype(jnp.int32)

        def _rel_pos(seq_len):
            ids = jnp.arange(seq_len)
            rel = ids[:, None] - ids[None, :]
            return _log_bucket(rel, BUCKETS, MAX_REL)
        B, S, D = hidden_states.shape
        hd = D // H
        span = BUCKETS

        def shape_heads(x):
            return x.reshape(*x.shape[:-1], H, hd).swapaxes(-2, -3)
        q = shape_heads(hidden_states @ Wq + bq)
        k = shape_heads(hidden_states @ Wk + bk)
        v = shape_heads(hidden_states @ Wv + bv)
        scale_factor = 3
        scores = jnp.einsum('bhsd,bhkd->bhsk', q, k) / jnp.sqrt(jnp.float32(hd * scale_factor))
        mu = rel_emb.mean(-1, keepdims=True)
        var = rel_emb.var(-1, keepdims=True)
        re = (rel_emb - mu) / jnp.sqrt(var + 1e-05) * ln_g + ln_b
        pos_k = shape_heads(re @ Wpk + bpk)
        pos_q = shape_heads(re @ Wpq + bpq)
        rel = _rel_pos(S)
        bias_scale = jnp.sqrt(jnp.float32(hd * 2))
        c2p = jnp.einsum('bhsd,hkd->bhsk', q, pos_k)
        c2p_idx = jnp.clip(rel + span, 0, 2 * span - 1)
        c2p = jnp.take_along_axis(c2p, jnp.broadcast_to(c2p_idx[None, None], (B, H, S, S)), axis=-1)
        scores = scores + c2p / bias_scale
        p2c = jnp.einsum('bhsd,hkd->bhsk', k, pos_q)
        p2c_idx = jnp.clip(-rel + span, 0, 2 * span - 1)
        p2c = jnp.take_along_axis(p2c, jnp.broadcast_to(p2c_idx[None, None], (B, H, S, S)), axis=-1)
        scores = scores + p2c.swapaxes(-1, -2) / bias_scale
        probs = jax.nn.softmax(scores.astype(jnp.float32), axis=-1).astype(q.dtype)
        ctx = jnp.einsum('bhsk,bhkd->bhsd', probs, v)
        ctx = ctx.swapaxes(1, 2).reshape(B, S, D)
        return ctx @ Wo + bo

    def _L0_ffn_ref(x, switch_w, switch_b, w1, b1, w2, b2):
        import jax, jax.numpy as jnp
        import numpy as np
        B, S, D = (4, 256, 128)
        E, F = (8, 512)
        b, s, d = x.shape
        t = x.reshape(-1, d)
        logits = t @ switch_w + switch_b
        route_prob = jax.nn.softmax(logits, axis=-1)
        route_prob_max = jnp.max(route_prob, axis=-1)
        routes = jnp.argmax(route_prob, axis=-1)
        out = jnp.zeros_like(t)
        n_experts = w1.shape[0]
        for e in range(n_experts):
            h = jax.nn.gelu(t @ w1[e] + b1[e])
            y = h @ w2[e] + b2[e]
            mask = (routes == e)[:, None]
            out = jnp.where(mask, y, out)
        out = out * route_prob_max[:, None]
        return out.reshape(b, s, d)
    x = L0_attn_a_x
    x = x + _L0_attn_a_ref(_layernorm(x, axis=-1), L0_attn_a_Wq, L0_attn_a_Wm, L0_attn_a_W1, L0_attn_a_W2, L0_attn_a_g1, L0_attn_a_b1, L0_attn_a_g2, L0_attn_a_b2)
    x = x + _L0_ffn_ref(_layernorm(x, axis=-1), L0_ffn_switch_w, L0_ffn_switch_b, L0_ffn_w1, L0_ffn_b1, L0_ffn_w2, L0_ffn_b2)
    x = x + _L0_attn_b_ref(_layernorm(x, axis=-1), L0_attn_b_Wq, L0_attn_b_bq, L0_attn_b_Wk, L0_attn_b_bk, L0_attn_b_Wv, L0_attn_b_bv, L0_attn_b_Wo, L0_attn_b_bo, L0_attn_b_rel_emb, L0_attn_b_ln_g, L0_attn_b_ln_b, L0_attn_b_Wpk, L0_attn_b_bpk, L0_attn_b_Wpq, L0_attn_b_bpq)
    x = x + _L0_ffn_ref(_layernorm(x, axis=-1), L0_ffn_switch_w, L0_ffn_switch_b, L0_ffn_w1, L0_ffn_b1, L0_ffn_w2, L0_ffn_b2)
    return x

_drawn_inputs = setup_inputs


def setup_inputs(seed=0):
    import zlib

    import numpy as np

    out = dict(_drawn_inputs(seed))
    spreads = {'L0_attn_a_g1': (1.0, 0.2),
     'L0_attn_a_b1': (0.0, 0.1),
     'L0_attn_a_g2': (1.0, 0.2),
     'L0_attn_a_b2': (0.0, 0.1),
     'L0_attn_b_bq': (0.0, 0.8),
     'L0_attn_b_bk': (0.0, 0.8),
     'L0_attn_b_bv': (0.0, 0.608),
     'L0_attn_b_bo': (0.0, 0.1),
     'L0_attn_b_ln_g': (1.0, 0.6),
     'L0_attn_b_ln_b': (0.0, 0.8),
     'L0_attn_b_bpk': (0.0, 0.8),
     'L0_attn_b_bpq': (0.0, 0.8),
     'L0_ffn_switch_b': (0.0, 0.1),
     'L0_ffn_b1': (0.0, 0.359),
     'L0_ffn_b2': (0.0, 0.1)}
    factors = {'L0_attn_b_Wq': 8.0,
     'L0_attn_b_Wk': 8.0,
     'L0_attn_b_Wv': 4.107,
     'L0_attn_b_Wo': 3.532,
     'L0_attn_b_rel_emb': 8.0,
     'L0_attn_b_Wpk': 8.0,
     'L0_attn_b_Wpq': 8.0}
    for name, (base, spread) in spreads.items():
        noise = np.random.default_rng([zlib.crc32(name.encode()), seed]).standard_normal(out[name].shape)
        drawn = base * np.exp(spread * noise) if base else spread * noise
        out[name] = jnp.asarray(drawn.astype(out[name].dtype))
    for name, factor in factors.items():
        out[name] = (out[name] * factor).astype(out[name].dtype)
    return out
```

```python
from contextlib import ExitStack

import numpy as np

import concourse.bass as bass
from concourse import mybir

FP32 = mybir.dt.float32
BF16 = mybir.dt.bfloat16
I32 = mybir.dt.int32
U32 = mybir.dt.uint32
ALU = mybir.AluOpType
ACT = mybir.ActivationFunctionType
AX = mybir.AxisListType

P = 128
BATCH, SEQ, D = 16, 256, 128
TOKENS = BATCH * SEQ
TILES = TOKENS // P
EPS = 1e-5
E, F = 8, 512
FC = F // P
BLOCKS = TOKENS // P + E
SLOTS = BLOCKS * P


class Mem:

    whole = None
    sems = {}

    def __init__(self, nc, stack, prefix):
        self.nc, self.stack, self.prefix = nc, stack, prefix

    def sb(self, name, shape, dt=FP32):
        return self.stack.enter_context(self.nc.sbuf_tensor(f"{self.prefix}_{name}", shape, dt))

    def sem(self, name, own=False):
        key = f"{self.prefix if own else self.prefix.strip('01')}_{name}"
        if key not in Mem.sems:
            Mem.sems[key] = Mem.whole.enter_context(self.nc.semaphore(key))
        return Mem.sems[key]

    def banks(self, n):
        return [self.stack.enter_context(self.nc.psum_tensor(f"{self.prefix}_bank{i}", [P, 512], FP32)) for i in range(n)]


def clear_semaphores(nc, handles):
    with nc.Block() as block:
        for n, engine in enumerate((block.sync, block.gpsimd, block.scalar, block.vector)):
            @engine
            def _(eng, n=n):
                for handle in handles[n::4]:
                    eng.sem_clear(handle)


def layernorm_transposed(nc, prefix, X, ident, XN, XT):
    with ExitStack() as stack:
        m = Mem(nc, stack, prefix)
        stats = m.sb("stats", [P, TILES, 6])
        mv = m.sb("mean_var", [P, TILES, 2])
        std = m.sb("std", [P, TILES])
        rstd = m.sb("rstd", [P, TILES])
        bank = m.banks(4)
        s_stats, s_mv, s_vareps, s_std, s_rstd, s_xn, s_xt_ps, s_xt = (
            m.sem(n) for n in ("stats", "mv", "vareps", "std", "rstd", "xn", "xt_ps", "xt"))
        block = stack.enter_context(nc.Block())

        @block.vector
        def _(dve):
            for t in range(TILES):
                dve.bn_stats(stats[:, t, :], X[:, t, :]).then_inc(s_stats, 1)
            for t in range(TILES):
                dve.wait_ge(s_stats, t + 1)
                dve.bn_aggr(mv[:, t, :], stats[:, t, :]).then_inc(s_mv, 1)
            dve.wait_ge(s_mv, TILES)
            dve.tensor_scalar(std[:, :], mv[:, :, 1], EPS, None, ALU.add).then_inc(s_vareps, 1)
            dve.wait_ge(s_std, 1)
            dve.reciprocal(rstd[:, :], std[:, :]).then_inc(s_rstd, 1)
            dve.wait_ge(s_rstd, 1)
            for t in range(TILES):
                dve.tensor_scalar(XN[:, t, :], X[:, t, :], mv[:, t, 0:1], rstd[:, t:t + 1],
                                  ALU.subtract, ALU.mult).then_inc(s_xn, 1)

        @block.tensor
        def _(pe):
            for t in range(TILES):
                g = t // 4
                pe.wait_ge(s_xn, t + 1)
                if t % 4 == 0 and g >= 4:
                    pe.wait_ge(s_xt, g - 3)
                pe.transpose(bank[g % 4][:, (t % 4) * P:(t % 4 + 1) * P], XN[:, t, :], ident).then_inc(s_xt_ps, 1)

        @block.scalar
        def _(act):
            act.wait_ge(s_vareps, 1)
            act.activation(std[:, :], std[:, :], ACT.Sqrt).then_inc(s_std, 1)
            for g in range(TILES // 4):
                act.wait_ge(s_xt_ps, 4 * g + 4)
                act.activation(XT[:, g * 512:(g + 1) * 512], bank[g % 4][:, :], ACT.Copy).then_inc(s_xt, 1)


def experts_layer(nc, prefix, X, con, w, slots_in, slots_out):
    with ExitStack() as stack:
        m = Mem(nc, stack, prefix)
        XN = m.sb("xn", [P, TILES, D])
        prob = m.sb("prob", [P, TILES])
        slot = m.sb("slot", [P, TILES], U32)
        bexp = m.sb("block_expert", [P, BLOCKS], I32)
        route_tokens(nc, prefix + "r", X, con, w, XN, prob, slot, bexp)
        run_experts(nc, prefix + "e", X, con, w, XN, prob, slot, bexp, slots_in, slots_out)


def route_tokens(nc, prefix, X, con, w, XN, prob, slot, bexp):
    with ExitStack() as stack:
        m = Mem(nc, stack, prefix)
        XT = m.sb("xt", [P, TOKENS])
        layernorm_transposed(nc, prefix + "n", X, con["ident"], XN, XT)
        PAD = 16
        sw = m.sb("switch_w", [P, E])
        sbias = m.sb("switch_b", [P, E])
        L = m.sb("logits", [P, TILES, E])
        mx = m.sb("max", [P, TILES])
        ex = m.sb("exp", [P, TILES, E])
        es = m.sb("expsum", [P, TILES])
        cand = m.sb("cand", [P, TILES, E])
        ridx = m.sb("route", [P, TILES])
        hot = m.sb("onehot", [P, TILES, E])
        cnt = [m.sb(f"count{i}", [P, PAD + TILES, E]) for i in range(2)]
        cfirst = m.sb("counts", [P, TILES, E])
        nblk_i = m.sb("nblocks_i", [P, E], I32)
        pre = [m.sb(f"blockprefix{i}", [P, 4 + E]) for i in range(2)]
        pos = m.sb("pos", [P, TILES, E])
        offs = m.sb("offs", [P, E])
        slotf = m.sb("slotf", [P, TILES])
        ge = m.sb("ge", [P, BLOCKS, E])
        bexpf = m.sb("bexpf", [P, BLOCKS])
        bank = m.banks(3)
        s_w, s_logit, s_d, s_exp, s_hot, s_rank, s_v = (m.sem(n) for n in ("w", "logit", "d", "exp", "hot", "rank", "v"))
        block = stack.enter_context(nc.Block())
        psl, psr, psc = (bank[i][:, 0:TILES * E].rearrange("p (t e) -> p t e", e=E) for i in range(3))

        @block.sync
        def _(sp):
            sp.dma_start(sw[:, :], w["switch_w"]).then_inc(s_w, 16)
            sp.dma_start(sbias[:, :], w["switch_b"].partition_broadcast(P)).then_inc(s_w, 16)

        @block.tensor
        def _(pe):
            pe.wait_ge(s_w, 32)
            for t in range(TILES):
                last = pe.matmul(bank[0][:, t * E:(t + 1) * E], XT[:, t * P:(t + 1) * P], sw[:, :], start=True, stop=True)
            last.then_inc(s_logit, 1)
            pe.wait_ge(s_hot, 1)
            pe.matmul(bank[1][:, 0:TILES * E], con["below"], hot[:, :, :].rearrange("p t e -> p (t e)"), start=True, stop=True)
            pe.matmul(bank[2][:, 0:TILES * E], con["ones"], hot[:, :, :].rearrange("p t e -> p (t e)"), start=True, stop=True).then_inc(s_rank, 1)

        @block.scalar
        def _(act):
            act.wait_ge(s_d, 1)
            act.activation(ex[:, :, :], L[:, :, :], ACT.Exp).then_inc(s_exp, 1)

        @block.vector
        def _(dve):
            done = [0]

            def then(ins):
                done[0] += 1
                ins.then_inc(s_v, 1)
                dve.wait_ge(s_v, done[0])

            TE = [P, TILES, E]
            dve.wait_ge(s_w, 32)
            dve.wait_ge(s_logit, 1)
            then(dve.tensor_tensor(L[:, :, :], psl, sbias[:, :].unsqueeze(1).to_broadcast(TE), ALU.add))
            then(dve.tensor_reduce(mx[:, :], L[:, :, :], AX.X, ALU.max))
            dve.tensor_tensor(L[:, :, :], L[:, :, :], mx[:, :].unsqueeze(2).to_broadcast(TE), ALU.subtract).then_inc(s_d, 1)
            dve.wait_ge(s_d, 1)
            then(dve.tensor_scalar(cand[:, :, :], L[:, :, :], 0.0, float(E), ALU.is_lt, ALU.mult))
            then(dve.tensor_tensor(cand[:, :, :], cand[:, :, :], con["iota_e"].unsqueeze(1).to_broadcast(TE), ALU.add))
            then(dve.tensor_reduce(ridx[:, :], cand[:, :, :], AX.X, ALU.min))
            dve.tensor_tensor(hot[:, :, :], con["iota_e"].unsqueeze(1).to_broadcast(TE),
                              ridx[:, :].unsqueeze(2).to_broadcast(TE), ALU.is_equal).then_inc(s_hot, 1)
            dve.wait_ge(s_exp, 1)
            then(dve.tensor_reduce(es[:, :], ex[:, :, :], AX.X, ALU.add))
            dve.reciprocal(prob[:, :], es[:, :])
            dve.memset(cnt[0][:, 0:PAD, :], 0.0)
            dve.memset(cnt[1][:, 0:PAD, :], 0.0)
            dve.memset(pre[0][:, 0:4], 0.0)
            then(dve.memset(pre[1][:, 0:4], 0.0))
            dve.wait_ge(s_rank, 1)
            then(dve.tensor_copy(cfirst[:, :, :], psc))
            then(dve.tensor_copy(cnt[0][:, PAD:, :], cfirst[:, :, :]))
            for k in range(5):
                a, b = cnt[k % 2], cnt[(k + 1) % 2]
                then(dve.tensor_tensor(b[:, PAD:, :], a[:, PAD:, :], a[:, PAD - (1 << k):PAD + TILES - (1 << k), :], ALU.add))
            tot = cnt[1]
            then(dve.tensor_scalar(nblk_i[:, :], tot[:, PAD + TILES - 1, :], float(P - 1), None, ALU.add))
            then(dve.tensor_scalar(nblk_i[:, :], nblk_i[:, :], 7, None, ALU.arith_shift_right))
            then(dve.tensor_copy(pre[0][:, 4:], nblk_i[:, :]))
            for k in range(3):
                a, b = pre[k % 2], pre[(k + 1) % 2]
                then(dve.tensor_tensor(b[:, 4:], a[:, 4:], a[:, 4 - (1 << k):4 + E - (1 << k)], ALU.add))
            bend = pre[1]
            then(dve.tensor_scalar(offs[:, :], bend[:, 3:3 + E], float(P), None, ALU.mult))
            then(dve.tensor_tensor(pos[:, :, :], tot[:, PAD:, :], cfirst[:, :, :], ALU.subtract))
            then(dve.tensor_tensor(pos[:, :, :], psr, pos[:, :, :], ALU.add))
            then(dve.tensor_tensor(pos[:, :, :], pos[:, :, :], offs[:, :].unsqueeze(1).to_broadcast(TE), ALU.add))
            then(dve.tensor_tensor(pos[:, :, :], pos[:, :, :], hot[:, :, :], ALU.mult))
            then(dve.tensor_reduce(slotf[:, :], pos[:, :, :], AX.X, ALU.add))
            then(dve.tensor_copy(slot[:, :], slotf[:, :]))
            BE = [P, BLOCKS, E]
            then(dve.tensor_tensor(ge[:, :, :], con["iota_b"].unsqueeze(2).to_broadcast(BE),
                                   bend[:, 4:].unsqueeze(1).to_broadcast(BE), ALU.is_ge))
            then(dve.tensor_reduce(bexpf[:, :], ge[:, :, :], AX.X, ALU.add))
            then(dve.tensor_scalar(bexp[:, :], bexpf[:, :], float(E - 1), None, ALU.min))


def run_experts(nc, prefix, X, con, w, XN, prob, slot, bexp, slots_in, slots_out):
    with ExitStack() as stack:
        m = Mem(nc, stack, prefix)
        W1 = [m.sb(f"w1_{i}", [P, F]) for i in range(2)]
        W2 = [m.sb(f"w2_{i}", [P, FC, D]) for i in range(2)]
        B1 = [m.sb(f"b1_{i}", [P, FC]) for i in range(2)]
        B2 = [m.sb(f"b2_{i}", [1, D]) for i in range(2)]
        xb = [m.sb(f"xb_{i}", [P, D]) for i in range(2)]
        xbt = [m.sb(f"xbt_{i}", [P, P]) for i in range(2)]
        h = [m.sb(f"h_{i}", [P, FC, P]) for i in range(2)]
        y = [m.sb(f"y_{i}", [P, D]) for i in range(2)]
        G = m.sb("gathered", [P, TILES, D])
        ZB = 8
        zero = m.sb("zero", [P, ZB, D])
        bank = m.banks(6)
        px, ph, py = bank[0:2], bank[2:4], bank[4:6]
        s_zero, s_xt, s_xtc, s_h, s_g, s_yp, s_y = (m.sem(n) for n in ("zero", "xt", "xtc", "h", "gelu", "yp", "y"))
        s_clear, s_scat = m.sem("clear", own=True), m.sem("scattered", own=True)
        GQ = 8
        s_gath = [m.sem(f"gathered{q}", own=True) for q in range(TILES // GQ)]
        s_w = [m.sem(f"w{i}") for i in range(2)]
        s_x = [m.sem(f"x{i}") for i in range(2)]
        s_out = [m.sem(f"out{i}", own=True) for i in range(2)]
        PAIRS = BLOCKS // 2
        block = stack.enter_context(nc.Block())


        @block.gpsimd
        def _(pool):
            pool.memset(zero[:, :, :], 0.0).then_inc(s_zero, 1)
            pool.wait_ge(s_zero, 1)
            for z in range(BLOCKS // ZB):
                pool.dma_start(slots_in[z * ZB * P:(z + 1) * ZB * P, :].rearrange("(p b) d -> p b d", p=P),
                               zero[:, :, :]).then_inc(s_clear, 16)
            pool.wait_ge(s_clear, 16 * (BLOCKS // ZB))
            for t in range(TILES):
                pool.indirect_dma_start(slots_in, bass.IndirectOffsetOnAxis(ap=slot[:, t:t + 1], axis=0),
                                        XN[:, t, :], None).then_inc(s_scat, 16)

            def store(g, i):
                pool.wait_ge(s_y, 2 * g + i + 1)
                pool.dma_start(slots_out[bass.ds((2 * g + i) * P, P), :], y[i][:, :]).then_inc(s_out[i], 16)

            with pool.Fori(0, PAIRS) as g:
                for i in range(2):
                    store(g, i)
            for i in range(2):
                pool.wait_ge(s_out[i], 16 * PAIRS)
            for t in range(TILES):
                pool.indirect_dma_start(G[:, t, :], None, slots_out,
                                        bass.IndirectOffsetOnAxis(ap=slot[:, t:t + 1], axis=0)).then_inc(s_gath[t // GQ], 16)

        @block.sync
        def _(sp):
            def rows(g, i):
                sp.dma_start(xb[i][:, :], slots_in[bass.ds((2 * g + i) * P, P), :]).then_inc(s_x[i], 16)

            def weights(g, i):
                e = sp.value_load(bexp[0:1, bass.ds(2 * g + i, 1)], min_val=0, max_val=E - 1)
                sp.dma_start(W1[i][:, :], w["w1"][bass.ds(e, 1), :, :].rearrange("a d f -> (a d) f")).then_inc(s_w[i], 16)
                sp.dma_start(B1[i][:, :], w["b1"][bass.ds(e, 1), :].rearrange("a (p c) -> (a p) c", c=FC)).then_inc(s_w[i], 16)
                sp.dma_start(W2[i][:, :, :], w["w2"][bass.ds(e, 1), :, :].rearrange("a (p c) d -> (a p) c d", c=FC)).then_inc(s_w[i], 16)
                sp.dma_start(B2[i][:, :], w["b2"][bass.ds(e, 1), :]).then_inc(s_w[i], 16)

            for i in range(2):
                weights(0, i)
            sp.wait_ge(s_scat, 16 * TILES)
            for i in range(2):
                rows(0, i)
            with sp.Fori(1, PAIRS) as g:
                for i in range(2):
                    sp.wait_ge(s_xt, 2 * g + i - 1)
                    rows(g, i)
                    sp.wait_ge(s_yp, 2 * g + i - 1)
                    weights(g, i)

        @block.tensor
        def _(pe):
            def transposed(g, i, first):
                pe.wait_ge(s_x[i], 16 * (g + 1))
                if not first:
                    pe.wait_ge(s_xtc, 2 * g + i - 1)
                pe.transpose(px[i][:, 0:P], xb[i][:, :], con["ident"]).then_inc(s_xt, 1)

            def up(g, i, first):
                pe.wait_ge(s_w[i], 64 * (g + 1))
                pe.wait_ge(s_xtc, 2 * g + i + 1)
                if not first:
                    pe.wait_ge(s_g, FC * (2 * g + i - 1))
                for c in range(FC):
                    last = pe.matmul(ph[i][:, c * P:(c + 1) * P], W1[i][:, c::FC], xbt[i][:, :], start=True, stop=True)
                last.then_inc(s_h, 1)

            def down(g, i, first):
                if not first:
                    pe.wait_ge(s_y, 2 * g + i - 1)
                pe.matmul(py[i][:, 0:D], con["ones"][0:1, :], B2[i][:, :], start=True, stop=False)
                for c in range(FC):
                    pe.wait_ge(s_g, FC * (2 * g + i) + c + 1)
                    last = pe.matmul(py[i][:, 0:D], h[i][:, c, :], W2[i][:, c, :], start=False, stop=(c == FC - 1))
                last.then_inc(s_yp, 1)

            transposed(0, 0, True)
            up(0, 0, True)
            transposed(0, 1, True)
            up(0, 1, True)
            transposed(1, 0, False)
            down(0, 0, True)

            def pair(g, last, second=False):
                up(g, 0, False)
                transposed(g, 1, False)
                down(g - 1, 1, second)
                up(g, 1, False)
                if not last:
                    transposed(g + 1, 0, False)
                down(g, 0, False)

            pair(1, False, True)
            with pe.Fori(2, PAIRS - 1) as g:
                pair(g, False)
            pair(PAIRS - 1, True)
            down(PAIRS - 1, 1, False)

        @block.scalar
        def _(act):
            def gelu(g, i, first):
                act.wait_ge(s_h, 2 * g + i + 1)
                if not first:
                    act.wait_ge(s_yp, 2 * g + i - 1)
                for c in range(FC):
                    act.activation(h[i][:, c, :], ph[i][:, c * P:(c + 1) * P], ACT.Gelu_apprx_tanh,
                                   bias=B1[i][:, c:c + 1]).then_inc(s_g, 1)

            for i in range(2):
                gelu(0, i, True)
            with act.Fori(1, PAIRS) as g:
                for i in range(2):
                    gelu(g, i, False)

        @block.vector
        def _(dve):
            def rows(g, i, first):
                dve.wait_ge(s_xt, 2 * g + i + 1)
                if not first:
                    dve.wait_ge(s_h, 2 * g + i - 1)
                dve.tensor_copy(xbt[i][:, :], px[i][:, 0:P]).then_inc(s_xtc, 1)

            def result(g, i, first):
                dve.wait_ge(s_yp, 2 * g + i + 1)
                if not first:
                    dve.wait_ge(s_out[i], 16 * g)
                dve.tensor_copy(y[i][:, :], py[i][:, 0:D]).then_inc(s_y, 1)

            rows(0, 0, True)
            rows(0, 1, True)
            rows(1, 0, False)
            result(0, 0, True)

            def pair(g, last, second=False):
                rows(g, 1, False)
                result(g - 1, 1, second)
                if not last:
                    rows(g + 1, 0, False)
                result(g, 0, False)

            pair(1, False, True)
            with dve.Fori(2, PAIRS - 1) as g:
                pair(g, False)
            pair(PAIRS - 1, True)
            result(PAIRS - 1, 1, False)
            for t in range(TILES):
                if t % GQ == 0:
                    dve.wait_ge(s_gath[t // GQ], 16 * GQ)
                dve.scalar_tensor_tensor(X[:, t, :], G[:, t, :], prob[:, t:t + 1], X[:, t, :], ALU.mult, ALU.add)


HA, DA = 8, D // 8
ATTN_EPS = 1e-6


def linear_attention_layer(nc, prefix, X, con, w):
    with ExitStack() as stack:
        m = Mem(nc, stack, prefix)
        XN = m.sb("xn", [P, TILES, D])
        M2 = m.sb("msg", [P, TILES, D])
        ML = m.sb("mlp", [P, TILES, D])
        with ExitStack() as inner:
            XT = Mem(nc, inner, prefix).sb("xt", [P, TOKENS])
            layernorm_transposed(nc, prefix + "n", X, con["ident"], XN, XT)
            linear_attention(nc, prefix + "l", con, w, XT, M2, ML)
        add_normalised(nc, prefix + "a", X, w, XN, M2, ML)


def linear_attention(nc, prefix, con, w, XT, M2, ML):
    with ExitStack() as stack:
        m = Mem(nc, stack, prefix)
        Wq, Wm = m.sb("wq", [P, D]), m.sb("wm", [P, D])
        W1, W2 = m.sb("w1", [P, 2 * D]), m.sb("w2", [P, 2, D])
        xt = m.sb("xt", [P, SEQ])
        q = m.sb("q", [P, 2, D + 1])
        neg = m.sb("neg", [P, 2, D])
        feat = m.sb("feat", [P, 2, D])
        featT = m.sb("featT", [P, SEQ])
        kv = m.sb("kv", [P, D + HA])
        den = m.sb("den", [P, 2, HA])
        msg = m.sb("msg", [P, 2, D])
        msgT = m.sb("msgT", [P, SEQ])
        m2T = m.sb("m2T", [P, SEQ])
        h1 = m.sb("h1", [P, 2, SEQ])
        bank = m.banks(8)
        (s_w, s_one, s_xt, s_q, s_qc, s_neg, s_exp, s_feat, s_kv, s_ft, s_kvm, s_ftc, s_un, s_den, s_rec, s_msg,
         s_mt, s_mtc, s_m2, s_m2t, s_m2c, s_h, s_relu, s_ml, s_mlc, s_m2s) = (m.sem(n) for n in (
             "w", "one", "xtc", "q", "qc", "neg", "exp", "feat", "kvp", "ft", "kvm", "ftc", "un", "denom", "rec", "msgs",
             "mt", "mtc", "m2", "m2t", "m2c", "h", "relu", "ml", "mlc", "m2s"))
        block = stack.enter_context(nc.Block())
        pq, pkv, pft, pun, pmt, pm2t, pm2, ph = bank
        pml = pq

        @block.sync
        def _(sp):
            sp.dma_start(Wq[:, :], w["Wq"]).then_inc(s_w, 16)
            sp.dma_start(Wm[:, :], w["Wm"]).then_inc(s_w, 16)
            sp.dma_start(W1[:, :], w["W1"]).then_inc(s_w, 16)
            sp.dma_start(W2[:, :, :], w["W2"].rearrange("(c p) d -> p c d", p=P)).then_inc(s_w, 16)

        @block.tensor
        def _(pe):
            pe.wait_ge(s_w, 64)
            with pe.Fori(0, BATCH) as b:
                pe.wait_ge(s_xt, b + 1)
                for u in range(2):
                    last = pe.matmul(pq[:, u * D:(u + 1) * D], xt[:, u * P:(u + 1) * P], Wq[:, :], start=True, stop=True)
                last.then_inc(s_q, 1)
                pe.wait_ge(s_qc, b + 1)
                pe.wait_ge(s_feat, b + 1)
                for u in range(2):
                    last = pe.matmul(pkv[:, 0:D + 1], feat[:, u, :], q[:, u, :], start=(u == 0), stop=(u == 1))
                last.then_inc(s_kv, 1)
                for u in range(2):
                    last = pe.transpose(pft[:, u * P:(u + 1) * P], feat[:, u, :], con["ident"])
                last.then_inc(s_ft, 1)
                pe.wait_ge(s_kvm, b + 1)
                pe.wait_ge(s_ftc, b + 1)
                for u in range(2):
                    last = pe.matmul(pun[:, u * (D + HA):(u + 1) * (D + HA)], featT[:, u * P:(u + 1) * P], kv[:, :], start=True, stop=True)
                last.then_inc(s_un, 1)
                pe.wait_ge(s_msg, b + 1)
                for u in range(2):
                    last = pe.transpose(pmt[:, u * P:(u + 1) * P], msg[:, u, :], con["ident"])
                last.then_inc(s_mt, 1)
                pe.wait_ge(s_mtc, b + 1)
                pe.matmul(pm2t[:, 0:SEQ], Wm[:, :], msgT[:, :], start=True, stop=True).then_inc(s_m2t, 1)
                for u in range(2):
                    last = pe.matmul(pm2[:, u * D:(u + 1) * D], msgT[:, u * P:(u + 1) * P], Wm[:, :], start=True, stop=True)
                last.then_inc(s_m2, 1)
                pe.wait_ge(s_m2c, b + 1)
                for c in range(2):
                    last = pe.matmul(ph[:, c * SEQ:(c + 1) * SEQ], W1[:, c * P:(c + 1) * P], m2T[:, :], start=True, stop=True)
                last.then_inc(s_h, 1)
                pe.wait_ge(s_relu, b + 1)
                for u in range(2):
                    for c in range(2):
                        last = pe.matmul(pml[:, u * D:(u + 1) * D], h1[:, c, u * P:(u + 1) * P], W2[:, c, :], start=(c == 0), stop=(c == 1))
                last.then_inc(s_ml, 1)
                pe.wait_ge(s_mlc, b + 1)

        @block.scalar
        def _(act):
            with act.Fori(0, BATCH) as b:
                act.wait_ge(s_neg, b + 1)
                act.activation(neg[:, :, :], neg[:, :, :], ACT.Exp).then_inc(s_exp, 1)
                act.wait_ge(s_ft, b + 1)
                act.activation(featT[:, :], pft[:, 0:SEQ], ACT.Copy).then_inc(s_ftc, 1)
                act.wait_ge(s_mt, b + 1)
                act.activation(msgT[:, :], pmt[:, 0:SEQ], ACT.Copy).then_inc(s_mtc, 1)
                act.wait_ge(s_m2t, b + 1)
                act.activation(m2T[:, :], pm2t[:, 0:SEQ], ACT.Copy).then_inc(s_m2c, 1)
                act.wait_ge(s_h, b + 1)
                act.activation(h1[:, :, :], ph[:, :].rearrange("p (c s) -> p c s", c=2), ACT.Relu).then_inc(s_relu, 1)

        @block.vector
        def _(dve):
            dve.memset(q[:, :, D:D + 1], 1.0).then_inc(s_one, 1)
            dve.wait_ge(s_one, 1)
            with dve.Fori(0, BATCH) as b:
                dve.tensor_copy(xt[:, :], XT[:, bass.ds(b * SEQ, SEQ)]).then_inc(s_xt, 1)
                dve.wait_ge(s_q, b + 1)
                pq3 = pq[:, 0:SEQ].rearrange("p (u d) -> p u d", u=2)
                dve.tensor_scalar(neg[:, :, :], pq3, 0.0, None, ALU.min).then_inc(s_neg, 1)
                dve.tensor_copy(q[:, :, 0:D], pq3).then_inc(s_qc, 1)
                dve.wait_ge(s_exp, b + 1)
                dve.scalar_tensor_tensor(feat[:, :, :], pq3, 0.0, neg[:, :, :], ALU.max, ALU.add).then_inc(s_feat, 1)
                dve.wait_ge(s_kv, b + 1)
                dve.tensor_tensor(kv[:, 0:D], pkv[:, 0:D], con["head_block"], ALU.mult)
                dve.tensor_scalar(kv[:, D:D + HA], con["head_of"], pkv[:, D:D + 1], None, ALU.mult).then_inc(s_kvm, 1)
                dve.wait_ge(s_un, b + 1)
                un = pun[:, 0:2 * (D + HA)].rearrange("p (u n) -> p u n", u=2)
                dve.tensor_scalar(den[:, :, :], un[:, :, D:], ATTN_EPS, None, ALU.add).then_inc(s_den, 1)
                dve.wait_ge(s_den, b + 1)
                dve.reciprocal(den[:, :, :], den[:, :, :]).then_inc(s_rec, 1)
                dve.wait_ge(s_rec, b + 1)
                for u in range(2):
                    last = dve.tensor_tensor(msg[:, u, :].rearrange("p (h v) -> p h v", h=HA), un[:, u, 0:D].rearrange("p (h v) -> p h v", h=HA),
                                             den[:, u, :].unsqueeze(2).to_broadcast([P, HA, DA]), ALU.mult)
                last.then_inc(s_msg, 1)
                dve.wait_ge(s_m2, b + 1)
                dve.tensor_copy(M2[:, bass.ds(2 * b, 2), :], pm2[:, 0:SEQ].rearrange("p (u d) -> p u d", u=2)).then_inc(s_m2s, 1)
                dve.wait_ge(s_ml, b + 1)
                dve.tensor_copy(ML[:, bass.ds(2 * b, 2), :], pml[:, 0:SEQ].rearrange("p (u d) -> p u d", u=2)).then_inc(s_mlc, 1)


def add_normalised(nc, prefix, X, w, XN, M2, ML):
    with ExitStack() as stack:
        m = Mem(nc, stack, prefix)
        gain = m.sb("gain", [P, 2, D])
        bias = m.sb("bias", [P, 2, D])
        stats = m.sb("stats", [P, 2 * TILES, 6])
        mv = m.sb("mean_var", [P, 2 * TILES, 2])
        std = m.sb("std", [P, 2 * TILES])
        rstd = m.sb("rstd", [P, 2 * TILES])
        s_w, s_stats, s_mv, s_ve, s_std, s_rstd, s_norm, s_gain, s_x, s_b = (m.sem(n) for n in (
            "w", "stats", "mv", "vareps", "std", "rstd", "norm", "gain", "x", "b"))
        block = stack.enter_context(nc.Block())

        @block.sync
        def _(sp):
            for j, n in enumerate(("g1", "g2")):
                sp.dma_start(gain[:, j, :], w[n].partition_broadcast(P)).then_inc(s_w, 16)
            for j, n in enumerate(("b1", "b2")):
                sp.dma_start(bias[:, j, :], w[n].partition_broadcast(P)).then_inc(s_w, 16)

        @block.scalar
        def _(act):
            act.wait_ge(s_ve, 1)
            act.activation(std[:, :], std[:, :], ACT.Sqrt).then_inc(s_std, 1)

        @block.gpsimd
        def _(pool):
            pool.tensor_tensor(X[:, :, :], X[:, :, :], XN[:, :, :], ALU.add).then_inc(s_x, 1)
            pool.wait_ge(s_x, 1)
            pool.wait_ge(s_w, 64)
            n = 1
            for j in range(2):
                pool.tensor_tensor(X[:, :, :], X[:, :, :], bias[:, j, :].unsqueeze(1).to_broadcast([P, TILES, D]), ALU.add).then_inc(s_x, 1)
                n += 1
                pool.wait_ge(s_x, n)
            for j, Y in enumerate((M2, ML)):
                pool.wait_ge(s_gain, 4 * (j + 1))
                pool.tensor_tensor(X[:, :, :], X[:, :, :], Y[:, :, :], ALU.add).then_inc(s_x, 1)
                n += 1
                pool.wait_ge(s_x, n)

        @block.vector
        def _(dve):
            for j, Y in enumerate((M2, ML)):
                for t in range(TILES):
                    dve.bn_stats(stats[:, j * TILES + t, :], Y[:, t, :]).then_inc(s_stats, 1)
            for t in range(2 * TILES):
                dve.wait_ge(s_stats, t + 1)
                dve.bn_aggr(mv[:, t, :], stats[:, t, :]).then_inc(s_mv, 1)
            dve.wait_ge(s_mv, 2 * TILES)
            dve.tensor_scalar(std[:, :], mv[:, :, 1], EPS, None, ALU.add).then_inc(s_ve, 1)
            dve.wait_ge(s_std, 1)
            dve.reciprocal(rstd[:, :], std[:, :]).then_inc(s_rstd, 1)
            dve.wait_ge(s_rstd, 1)
            dve.wait_ge(s_w, 64)
            for j, Y in enumerate((M2, ML)):
                for t in range(TILES):
                    n = j * TILES + t
                    dve.tensor_scalar(Y[:, t, :], Y[:, t, :], mv[:, n, 0:1], rstd[:, n:n + 1], ALU.subtract, ALU.mult).then_inc(s_norm, 1)
                for g in range(4):
                    dve.wait_ge(s_norm, j * TILES + 8 * g + 8)
                    part = Y[:, 8 * g:8 * g + 8, :]
                    dve.tensor_tensor(part, part, gain[:, j, :].unsqueeze(1).to_broadcast([P, 8, D]), ALU.mult).then_inc(s_gain, 1)


HB, DB = 16, D // 16
NB16 = SEQ // 16
BUCKETS, MAX_REL = 32, 64
OFFS = 2 * SEQ
TABLE = OFFS - 16
VW = DB + 1
NEG_HUGE = -3.0e38


def disentangled_attention_layer(nc, prefix, X, con, w, dram):
    with ExitStack() as stack:
        m = Mem(nc, stack, prefix)
        V = m.sb("v", [P, TILES, HB, VW])
        with ExitStack() as inner:
            mi = Mem(nc, inner, prefix)
            XT = mi.sb("xt", [P, TOKENS])
            XN = mi.sb("xn", [P, TILES, D])
            layernorm_transposed(nc, prefix + "n", X, con["ident"], XN, XT)
            project_qkv(nc, prefix + "p", X, con, w, XT, V, dram)
        position_tables(nc, prefix + "t", con, w, dram)
        attend(nc, prefix + "s", con, V, X, dram)
        return_context(nc, prefix + "o", X, con, w, dram)


def project_qkv(nc, prefix, X, con, w, XT, V, dram):
    with ExitStack() as stack:
        m = Mem(nc, stack, prefix)
        W = m.sb("w", [P, 3, D])
        b_col = m.sb("b_col", [P, 2])
        bv = m.sb("bv", [P, D])
        QT = [m.sb(f"qt{i}", [P, TOKENS]) for i in range(2)]
        part = [m.sb(f"part{i}", [P, 3, TOKENS], BF16) for i in range(2)]
        rest = [m.sb(f"rest{i}", [P, 512]) for i in range(3)]
        s_p1, s_rest, s_p2, s_p3 = m.sem("part1"), m.sem("rest"), m.sem("part2"), m.sem("part3")
        bank = m.banks(6)
        s_w, s_bs, s_q, s_qe, s_v, s_ve, s_one, s_out = (m.sem(n) for n in ("w", "bs", "q", "qe", "v", "ve", "one", "out"))
        scale = (1.0 / np.sqrt(3.0 * DB), 1.0)
        G = TOKENS // 512
        block = stack.enter_context(nc.Block())

        @block.sync
        def _(sp):
            for j, n in enumerate(("Wq", "Wk", "Wv")):
                sp.dma_start(W[:, j, :], w[n]).then_inc(s_w, 16)
            for j, n in enumerate(("bq", "bk")):
                sp.dma_start(b_col[:, j:j + 1], w[n].rearrange("(p o) -> p o", o=1)).then_inc(s_w, 16)
            sp.dma_start(bv[:, :], w["bv"].partition_broadcast(P)).then_inc(s_w, 16)
            sp.dma_start(dram["x"], X[:, :, :].rearrange("p t d -> p (t d)")).then_inc(s_out, 16)
            for j in range(2):
                sp.wait_ge(s_qe, G * (j + 1))
                sp.dma_start(dram["qk"][j], QT[j][:, :]).then_inc(s_out, 16)
            for j in range(2):
                sp.wait_ge(s_p3, G * (j + 1))
                sp.dma_start(dram["parts"][j].rearrange("i p n -> p i n"), part[j][:, :, :]).then_inc(s_out, 16)
            sp.wait_ge(s_out, 80)

        @block.tensor
        def _(pe):
            pe.wait_ge(s_w, 96)
            for n in range(2 * G):
                j, g = n // G, n % G
                if n >= 4:
                    pe.wait_ge(s_p1, n - 3)
                pe.matmul(bank[n % 4][:, :], W[:, j, :], XT[:, g * 512:(g + 1) * 512], start=True, stop=True).then_inc(s_q, 1)
            for t in range(TILES):
                if t % 4 == 0 and t >= 8:
                    pe.wait_ge(s_ve, t // 4 - 1)
                pe.matmul(bank[4 + t // 4 % 2][:, t % 4 * D:(t % 4 + 1) * D], XT[:, t * P:(t + 1) * P], W[:, 2, :], start=True, stop=True).then_inc(s_v, 1)

        @block.scalar
        def _(act):
            act.wait_ge(s_bs, 1)
            for n in range(2 * G):
                j, g = n // G, n % G
                act.wait_ge(s_q, n + 1)
                act.activation(QT[j][:, g * 512:(g + 1) * 512], bank[n % 4][:, :], ACT.Identity,
                               bias=b_col[:, j:j + 1], scale=float(scale[j])).then_inc(s_qe, 1)
                act.activation(part[j][:, 0, g * 512:(g + 1) * 512], bank[n % 4][:, :], ACT.Identity,
                               bias=b_col[:, j:j + 1], scale=float(scale[j])).then_inc(s_p1, 1)

        @block.vector
        def _(dve):
            dve.wait_ge(s_w, 96)
            dve.tensor_scalar(b_col[:, 0:1], b_col[:, 0:1], float(scale[0]), None, ALU.mult).then_inc(s_bs, 1)
            dve.memset(V[:, :, :, DB:], 1.0).then_inc(s_one, 1)
            for g in range(TILES // 4):
                dve.wait_ge(s_v, 4 * g + 4)
                for j in range(4):
                    last = dve.tensor_tensor(V[:, 4 * g + j, :, 0:DB], bank[4 + g % 2][:, j * D:(j + 1) * D].rearrange("p (h d) -> p h d", h=HB),
                                             bv[:, :].rearrange("p (h d) -> p h d", h=HB), ALU.add)
                last.then_inc(s_ve, 1)
            for n in range(2 * G + 1):
                if n < 2 * G:
                    j, g = n // G, n % G
                    cols = slice(g * 512, (g + 1) * 512)
                    dve.wait_ge(s_p1, n + 1)
                    dve.wait_ge(s_qe, n + 1)
                    if n >= 3:
                        dve.wait_ge(s_p3, n - 2)
                    dve.tensor_tensor(rest[n % 3][:, :], QT[j][:, cols], part[j][:, 0, cols], ALU.subtract).then_inc(s_rest, 1)
                if n >= 1:
                    j, g = (n - 1) // G, (n - 1) % G
                    cols = slice(g * 512, (g + 1) * 512)
                    dve.wait_ge(s_p2, n)
                    dve.tensor_tensor(part[j][:, 2, cols], rest[(n - 1) % 3][:, :], part[j][:, 1, cols], ALU.subtract).then_inc(s_p3, 1)

        @block.gpsimd
        def _(pool):
            for n in range(2 * G):
                j, g = n // G, n % G
                pool.wait_ge(s_rest, n + 1)
                pool.tensor_copy(part[j][:, 1, g * 512:(g + 1) * 512], rest[n % 3][:, :]).then_inc(s_p2, 1)


def position_tables(nc, prefix, con, w, dram):
    with ExitStack() as stack:
        m = Mem(nc, stack, prefix)
        R = m.sb("rel", [2 * BUCKETS, D])
        gb = m.sb("gb", [2 * BUCKETS, 2, D])
        Wp = m.sb("wp", [P, 2, D])
        bp = m.sb("bp", [2 * BUCKETS, 2, D])
        onehot = m.sb("onehot", [2 * BUCKETS, 2, OFFS])
        RT = m.sb("relt", [P, 2 * BUCKETS])
        PK = m.sb("pk", [2 * BUCKETS, 2, D])
        T = m.sb("tables", [P, 2, OFFS])
        stats, mv, std = m.sb("stats", [2 * BUCKETS, 6]), m.sb("mv", [2 * BUCKETS, 2]), m.sb("std", [2 * BUCKETS, 1])
        bank = m.banks(4)
        s_w, s_v, s_std, s_ve, s_re, s_rt, s_rtc, s_pk, s_pkc, s_t, s_tc, s_out = (m.sem(n) for n in (
            "w", "v", "std", "vareps", "re", "rt", "rtc", "pk", "pkc", "t", "tc", "out"))
        scale = (np.sqrt(3.0 * DB) / np.sqrt(2.0 * DB), 1.0 / np.sqrt(2.0 * DB))
        NBK = 2 * BUCKETS
        block = stack.enter_context(nc.Block())

        @block.sync
        def _(sp):
            sp.dma_start(R[:, :], w["rel_emb"]).then_inc(s_w, 16)
            for j, n in enumerate(("ln_g", "ln_b")):
                sp.dma_start(gb[:, j, :], w[n].partition_broadcast(NBK)).then_inc(s_w, 16)
            for j, n in enumerate(("k", "q")):
                sp.dma_start(Wp[:, j, :], w["Wp" + n]).then_inc(s_w, 16)
                sp.dma_start(bp[:, j, :], w["bp" + n].partition_broadcast(NBK)).then_inc(s_w, 16)
            sp.dma_start(onehot[:, :, :], dram["onehot"].rearrange("a (j x) -> a j x", j=2)).then_inc(s_w, 16)
            sp.wait_ge(s_tc, 1)
            sp.dma_start(dram["tables"].rearrange("j p x -> p j x"), T[:, :, :]).then_inc(s_out, 16)
            sp.wait_ge(s_out, 16)

        @block.scalar
        def _(act):
            act.wait_ge(s_ve, 1)
            act.activation(std[:, :], std[:, :], ACT.Sqrt).then_inc(s_std, 1)

        @block.vector
        def _(dve):
            done = [0]

            def then(ins):
                done[0] += 1
                ins.then_inc(s_v, 1)
                dve.wait_ge(s_v, done[0])

            dve.wait_ge(s_w, 128)
            then(dve.bn_stats(stats[:, :], R[:, :]))
            then(dve.bn_aggr(mv[:, :], stats[:, :]))
            dve.tensor_scalar(std[:, :], mv[:, 1:2], EPS, None, ALU.add).then_inc(s_ve, 1)
            dve.wait_ge(s_std, 1)
            then(dve.reciprocal(std[:, :], std[:, :]))
            then(dve.tensor_scalar(R[:, :], R[:, :], mv[:, 0:1], std[:, :], ALU.subtract, ALU.mult))
            then(dve.tensor_tensor(R[:, :], R[:, :], gb[:, 0, :], ALU.mult))
            dve.tensor_tensor(R[:, :], R[:, :], gb[:, 1, :], ALU.add).then_inc(s_re, 1)
            dve.wait_ge(s_rt, 1)
            dve.tensor_copy(RT[:, :], bank[0][:, 0:NBK]).then_inc(s_rtc, 1)
            dve.wait_ge(s_pk, 1)
            then(dve.tensor_tensor(PK[:, :, :], bank[1][0:NBK, 0:2 * D].rearrange("p (j d) -> p j d", j=2), bp[:, :, :], ALU.add))
            for j in range(2):
                last = dve.tensor_scalar(PK[:, j, :], PK[:, j, :], float(scale[j]), None, ALU.mult)
            last.then_inc(s_pkc, 1)
            dve.wait_ge(s_t, 1)
            for j in range(2):
                last = dve.tensor_copy(T[:, j, :], bank[2 + j][:, :])
            last.then_inc(s_tc, 1)

        @block.tensor
        def _(pe):
            pe.wait_ge(s_re, 1)
            pe.transpose(bank[0][:, 0:NBK], R[:, :], con["ident"][0:NBK, 0:NBK]).then_inc(s_rt, 1)
            pe.wait_ge(s_rtc, 1)
            for j in range(2):
                last = pe.matmul(bank[1][0:NBK, j * D:(j + 1) * D], RT[:, :], Wp[:, j, :], start=True, stop=True)
            last.then_inc(s_pk, 1)
            pe.wait_ge(s_pkc, 1)
            for j in range(2):
                last = pe.matmul(bank[2 + j][:, :], PK[:, j, :], onehot[:, j, :], start=True, stop=True)
            last.then_inc(s_t, 1)


def stacked_views(dram):
    n, part = TOKENS, P * TOKENS
    tab, qk, parts = (dram[name].tensor for name in ("tables", "qk", "parts"))
    return {
        "tables": [bass.AP(tensor=tab, offset=j * P * OFFS, ap=[[1, 16], [OFFS, P], [1, TABLE]]) for j in range(2)],
        "qk": [bass.AP(tensor=qk, offset=j * P * n, ap=[[0, 16], [n, P], [1, n]]) for j in range(2)],
        "q_parts": [bass.AP(tensor=parts, offset=i * part, ap=[[0, 3], [n, P], [1, n]]) for i in range(3)],
        "k_parts": bass.AP(tensor=parts, offset=3 * part, ap=[[part, 3], [n, P], [1, n]]),
    }


def attend(nc, prefix, con, V, CTX, dram):
    with ExitStack() as stack:
        m = Mem(nc, stack, prefix)
        QR = m.sb("qr", [P, TOKENS])
        KR = m.sb("kr", [P, TOKENS])
        QS = m.sb("qs", [9 * DB, TOKENS], BF16)
        KS = m.sb("ks", [9 * DB, TOKENS], BF16)
        TAB = m.sb("tab", [P, 2, TABLE])
        CT = m.sb("c2p_t", [P, 2, BATCH, SEQ])
        PC = m.sb("p2c", [P, 2, BATCH, SEQ])
        NS = 4
        S = [m.sb(f"scores{i}", [P, 2, SEQ]) for i in range(NS)]
        PT = [m.sb(f"probs_t{i}", [P, 2, SEQ]) for i in range(2)]
        mx = m.sb("max", [P, 2 * BATCH])
        rec = m.sb("rec", [P, 2 * BATCH])
        bank = m.banks(8)
        pb, pt1, pqk, pt2, pav = bank[0:2], bank[2:4], bank[4:6], bank[6], bank[7]
        (s_masked, s_bm, s_be, s_t1, s_z, s_qk, s_sc, s_sub0, s_sub1, s_t2, s_exp, s_av, s_rec, s_ctx,
         s_q, s_tab, s_stack, s_go_dve, s_go_pool, s_go_sp) = (m.sem(n) for n in (
             "masked", "bias_mm", "bias_copied", "t1", "z", "qk", "scores", "shifted0", "shifted1", "t2", "exp", "av", "rec", "ctx",
             "q", "tab", "stack", "go_dve", "go_pool", "go_sp"))
        PAIRS = NB16 // 2
        BM = 2 * PAIRS * 2
        views = stacked_views(dram)
        LAG = 3
        block = stack.enter_context(nc.Block())

        @block.sync
        def _(sp):
            with sp.Fori(0, HB) as head:
                rows = bass.ds(head * DB, DB)
                sp.wait_ge(s_be, head * BM + 2)
                sp.sem_inc(s_go_sp, 1)
                for j in range(2):
                    sp.dma_start(TAB[:, j, :], views["tables"][j][:, rows, :]).then_inc(s_tab, 16)
                for j, R in enumerate((QR, KR)):
                    sp.dma_start(R[:, :], views["qk"][j][:, rows, :]).then_inc(s_q, 16)
                sp.wait_ge(s_sc, head * BATCH + 2)
                sp.sem_inc(s_go_sp, 1)
                for i in range(3):
                    three = slice(i * 3 * DB, (i + 1) * 3 * DB)
                    sp.dma_start(QS[three, :], views["q_parts"][i][:, rows, :]).then_inc(s_stack, 16)
                    sp.dma_start(KS[three, :], views["k_parts"][:, rows, :]).then_inc(s_stack, 16)

        @block.gpsimd
        def _(pool):
            with pool.Fori(0, HB) as head:
                for b in range(BATCH):
                    pool.wait_ge(s_sc, head * BATCH + b + 3)
                    pool.sem_inc(s_go_pool, 1)
                    pool.tensor_scalar(S[b % NS][:, 1, :], S[b % NS][:, 1, :], mx[:, 2 * b + 1:2 * b + 2], None,
                                       ALU.subtract).then_inc(s_sub1, 1)

        @block.tensor
        def _(pe):
            pe.sem_inc(s_t2, NS)
            pe.sem_inc(s_av, 2)
            with pe.Fori(0, HB) as head:
                pe.wait_ge(s_tab, 16 * 2 * (head + 1))
                n = 0
                for kind, mov in ((0, QR), (1, KR)):
                    for pair in range(PAIRS):
                        pe.wait_ge(s_masked, head * 2 * PAIRS + kind * PAIRS + pair + 1)
                        for side in range(2):
                            pe.wait_ge(s_be, head * BM + n + 1)
                            for a in range(2):
                                grp = 2 * pair + a
                                c = TABLE - SEQ + P * side - 16 * grp
                                last = pe.matmul(pb[n % 2][:, a * 256:(a + 1) * 256], TAB[:, kind, c:c + P],
                                                 mov[:, :].rearrange("p (b g s) -> p g b s", b=BATCH, s=16)[:, grp, :, :],
                                                 start=True, stop=True)
                            last.then_inc(s_bm, 1)
                            n += 1
                pe.wait_ge(s_be, head * BM + BM + 2)
                pe.wait_ge(s_stack, 16 * 6 * (head + 1))

                def t1(b):
                    pe.wait_ge(s_z, head * BATCH + b + 1)
                    for st in range(2):
                        for kt in range(2):
                            last = pe.transpose(pt1[b % 2][:, st * SEQ + kt * P:st * SEQ + (kt + 1) * P],
                                                CT[:, kt, b, st * P:(st + 1) * P], con["ident"])
                    last.then_inc(s_t1, 1)

                def qk(b):
                    pe.wait_ge(s_sc, head * BATCH + b + 1)
                    for st in range(2):
                        last = pe.matmul(pqk[b % 2][:, st * SEQ:(st + 1) * SEQ], QS[:, b * SEQ + st * P:b * SEQ + (st + 1) * P],
                                         KS[:, b * SEQ:(b + 1) * SEQ], start=True, stop=True)
                    last.then_inc(s_qk, 1)

                def t2(b):
                    pe.wait_ge(s_sub0, head * BATCH + b + 1)
                    pe.wait_ge(s_sub1, head * BATCH + b + 1)
                    pe.wait_ge(s_exp, head * BATCH + b + 1)
                    for kt in range(2):
                        for st in range(2):
                            last = pe.transpose(pt2[:, kt * SEQ + st * P:kt * SEQ + (st + 1) * P],
                                                S[b % NS][:, st, kt * P:(kt + 1) * P], con["ident"])
                    last.then_inc(s_t2, 1)

                def av(b):
                    pe.wait_ge(s_exp, head * BATCH + b + 2)
                    if b == 0:
                        pe.wait_ge(s_ctx, head + 1)
                    for st in range(2):
                        for kt in range(2):
                            last = pe.matmul(pav[:, (2 * b + st) * VW:(2 * b + st + 1) * VW], PT[b % 2][:, kt, st * P:(st + 1) * P],
                                             V[:, 2 * b + kt, bass.ds(head, 1), :].rearrange("p a v -> p (a v)"),
                                             start=(kt == 0), stop=(kt == 1))
                    last.then_inc(s_av, 1)

                for n in range(BATCH + LAG + 1):
                    if n < BATCH:
                        t1(n)
                        qk(n)
                    if LAG <= n < BATCH + LAG:
                        t2(n - LAG)
                    if n >= LAG + 1:
                        av(n - LAG - 1)

        @block.scalar
        def _(act):
            act.sem_inc(s_be, 2)
            act.sem_inc(s_exp, 1)
            with act.Fori(0, HB) as head:
                n = 0
                for dst in (CT, PC):
                    for pair in range(PAIRS):
                        for side in range(2):
                            act.wait_ge(s_bm, head * BM + n + 1)
                            o = dst[:, side, :, pair * 32:(pair + 1) * 32].rearrange("p b (a s) -> p a b s", a=2)
                            act.activation(o, pb[n % 2][:, :].rearrange("p (a b s) -> p a b s", a=2, b=BATCH), ACT.Copy).then_inc(s_be, 1)
                            n += 1
                for b in range(BATCH):
                    act.wait_ge(s_t2, head * BATCH + b + NS + 1)
                    act.wait_ge(s_av, head * BATCH + b + 1)
                    act.activation(PT[b % 2][:, :, :], pt2[:, :].rearrange("p (k s) -> p k s", k=2), ACT.Exp).then_inc(s_exp, 1)

        @block.vector
        def _(dve):
            dve.sem_inc(s_z, 2)
            dve.sem_inc(s_sc, 2)
            dve.sem_inc(s_ctx, 1)
            with dve.Fori(0, HB) as head:
                dve.wait_ge(s_q, 16 * 2 * (head + 1))
                for R in (QR, KR):
                    for pair in range(PAIRS):
                        for a in range(2):
                            part = R[:, :].rearrange("p (b g s) -> p g b s", b=BATCH, s=16)[:, 2 * pair + a, :, :]
                            last = dve.tensor_tensor(part, part, con["own_pos"].unsqueeze(1).to_broadcast([P, BATCH, 16]), ALU.mult)
                        last.then_inc(s_masked, 1)
                dve.wait_ge(s_be, head * BM + BM + 2)
                for b in range(BATCH):
                    dve.wait_ge(s_t1, head * BATCH + b + 1)
                    z = PC[:, :, b, :]
                    dve.tensor_tensor(z, pt1[b % 2][:, :].rearrange("p (a k) -> p a k", a=2), z, ALU.add).then_inc(s_z, 1)
                    dve.wait_ge(s_z, head * BATCH + b + 3)
                    dve.wait_ge(s_qk, head * BATCH + b + 1)
                    dve.wait_ge(s_t2, head * BATCH + b + 1)
                    dve.sem_inc(s_go_dve, 1)
                    for st in range(2):
                        last = dve.tensor_tensor_reduce(out=S[b % NS][:, st, :], in0=pqk[b % 2][:, st * SEQ:(st + 1) * SEQ], in1=PC[:, st, b, :],
                                                        scale=1.0, scalar=NEG_HUGE, op0=ALU.add, op1=ALU.max,
                                                        accum_out=mx[:, 2 * b + st:2 * b + st + 1])
                    last.then_inc(s_sc, 1)
                    dve.wait_ge(s_sc, head * BATCH + b + 3)
                    dve.tensor_scalar(S[b % NS][:, 0, :], S[b % NS][:, 0, :], mx[:, 2 * b:2 * b + 1], None, ALU.subtract).then_inc(s_sub0, 1)
                dve.wait_ge(s_av, head * BATCH + BATCH + 2)
                o = pav[:, 0:2 * BATCH * VW].rearrange("p (t v) -> p t v", v=VW)
                dve.reciprocal(rec[:, :], o[:, :, DB]).then_inc(s_rec, 1)
                dve.wait_ge(s_rec, head + 1)
                dve.tensor_tensor(CTX[:, :, bass.ds(head * DB, DB)], o[:, :, 0:DB],
                                  rec[:, :].unsqueeze(2).to_broadcast([P, TILES, DB]), ALU.mult).then_inc(s_ctx, 1)


def return_context(nc, prefix, X, con, w, dram):
    with ExitStack() as stack:
        m = Mem(nc, stack, prefix)
        Wo = m.sb("wo", [P, D])
        bo = m.sb("bo", [P, D])
        XR = m.sb("x", [P, TILES, D])
        CXT = m.sb("ctx_t", [P, TOKENS])
        bank = m.banks(4)
        s_w, s_t, s_tc, s_o, s_x, s_b = (m.sem(n) for n in ("w", "t", "tc", "o", "x", "b"))
        block = stack.enter_context(nc.Block())

        @block.sync
        def _(sp):
            sp.dma_start(Wo[:, :], w["Wo"]).then_inc(s_w, 16)
            sp.dma_start(bo[:, :], w["bo"].partition_broadcast(P)).then_inc(s_w, 16)
            sp.dma_start(XR[:, :, :].rearrange("p t d -> p (t d)"), dram["x"]).then_inc(s_w, 16)

        @block.tensor
        def _(pe):
            pe.wait_ge(s_w, 48)
            for g in range(TILES // 4):
                if g >= 2:
                    pe.wait_ge(s_tc, g - 1)
                for j in range(4):
                    last = pe.transpose(bank[g % 2][:, j * P:(j + 1) * P], X[:, 4 * g + j, :], con["ident"])
                last.then_inc(s_t, 1)
                pe.wait_ge(s_tc, g + 1)
                if g >= 2:
                    pe.wait_ge(s_x, g - 1)
                for j in range(4):
                    t = 4 * g + j
                    last = pe.matmul(bank[2 + g % 2][:, j * D:(j + 1) * D], CXT[:, t * P:(t + 1) * P], Wo[:, :], start=True, stop=True)
                last.then_inc(s_o, 1)

        @block.scalar
        def _(act):
            for g in range(TILES // 4):
                act.wait_ge(s_t, g + 1)
                act.activation(CXT[:, g * 512:(g + 1) * 512], bank[g % 2][:, :], ACT.Copy).then_inc(s_tc, 1)

        @block.vector
        def _(dve):
            dve.wait_ge(s_w, 48)
            dve.tensor_tensor(XR[:, :, :], XR[:, :, :], bo[:, :].unsqueeze(1).to_broadcast([P, TILES, D]), ALU.add).then_inc(s_b, 1)
            dve.wait_ge(s_b, 1)
            for g in range(TILES // 4):
                dve.wait_ge(s_o, g + 1)
                dve.tensor_tensor(X[:, 4 * g:4 * g + 4, :], bank[2 + g % 2][:, :].rearrange("p (t d) -> p t d", t=4),
                                  XR[:, 4 * g:4 * g + 4, :], ALU.add).then_inc(s_x, 1)


def bucket(rel):
    mid = BUCKETS // 2
    size = np.where(np.abs(rel) < mid, mid - 1, np.abs(rel)).astype(np.float32)
    far = np.ceil(np.log(size / np.float32(mid)) / np.float32(np.log((MAX_REL - 1) / mid)) * np.float32(mid - 1)) + mid
    return np.where(size <= mid, rel, far * np.sign(rel)).astype(np.int64)


def bucket_onehots():
    x = np.arange(OFFS)
    rows = [np.clip(bucket(off) + BUCKETS, 0, 2 * BUCKETS - 1) for off in (SEQ - 1 - x, x - SEQ + 1)]
    return np.concatenate([np.arange(2 * BUCKETS)[:, None] == r[None, :] for r in rows], axis=1)


INPUTS = ["L0_attn_a_x"] + ["L0_attn_a_" + n for n in ("Wq", "Wm", "W1", "W2", "g1", "b1", "g2", "b2")] + \
    ["L0_attn_b_" + n for n in ("Wq", "bq", "Wk", "bk", "Wv", "bv", "Wo", "bo", "rel_emb", "ln_g", "ln_b", "Wpk", "bpk", "Wpq", "bpq")] + \
    ["L0_ffn_" + n for n in ("switch_w", "switch_b", "w1", "b1", "w2", "b2")]


def shape_constants():
    row = np.arange(P)
    return {
        "ident": np.eye(P),
        "ones": np.ones((P, P)),
        "below": row[:, None] < row[None, :],
        "iota_e": np.broadcast_to(np.arange(E), (P, E)),
        "head_block": row[:, None] // DA == row[None, :] // DA,
        "head_of": row[:, None] // DA == np.arange(HA)[None, :],
        "own_pos": 15 - row[:, None] // DB == np.arange(16)[None, :],
        "iota_b": np.broadcast_to(np.arange(BLOCKS), (P, BLOCKS)),
    }


def program(nc, dram, consts, onehots, out):
    x = dram["L0_attn_a_x"].rearrange("b (u p) d -> p (b u) d", p=P)
    y = out.rearrange("b (u p) d -> p (b u) d", p=P)
    with ExitStack() as stack:
        Mem.whole, Mem.sems = stack, {}
        m = Mem(nc, stack, "all")
        X = m.sb("x", [P, TILES, D])
        width = consts.shape[1]
        C = m.sb("constants", [P, width])
        con, at = {}, 0
        for name, v in shape_constants().items():
            con[name] = C[:, at:at + v.shape[1]]
            at += v.shape[1]
        ffn = {n: dram["L0_ffn_" + n] for n in ("switch_w", "switch_b", "w1", "b1", "w2", "b2")}
        s_in = m.sem("in")
        s_done = m.sem("done")
        with nc.Block() as block:
            @block.sync
            def _(sp):
                sp.dma_start(X[:, :, :], x).then_inc(s_in, 16)
                sp.dma_start(C[:, :], consts).then_inc(s_in, 16)
                sp.wait_ge(s_in, 32)
        linear_attention_layer(nc, "a", X, con, {n: dram["L0_attn_a_" + n] for n in ("Wq", "Wm", "W1", "W2", "g1", "b1", "g2", "b2")})
        def experts(layer):
            a = nc.dram_tensor(f"slots_in{layer}", (SLOTS, D), FP32, kind="Internal").ap()
            b = nc.dram_tensor(f"slots_out{layer}", (SLOTS, D), FP32, kind="Internal").ap()
            experts_layer(nc, f"{layer}f", X, con, ffn, a, b)

        experts(0)
        clear_semaphores(nc, [handle for key, handle in Mem.sems.items() if key.startswith("f")])
        scratch = {n: nc.dram_tensor("scratch_" + n, shape, dt, kind="Internal").ap() for n, shape, dt in (
            ("x", (P, TILES * D), FP32), ("qk", (2, P, TOKENS), FP32), ("parts", (2, 3, P, TOKENS), BF16),
            ("tables", (2, P, OFFS), FP32))}
        disentangled_attention_layer(nc, "d", X, con, {n: dram["L0_attn_b_" + n] for n in (
            "Wq", "bq", "Wk", "bk", "Wv", "bv", "Wo", "bo", "rel_emb", "ln_g", "ln_b", "Wpk", "bpk", "Wpq", "bpq")},
            dict(scratch, onehot=onehots))
        experts(1)
        with nc.Block() as block:
            @block.sync
            def _(sp):
                sp.dma_start(y, X[:, :, :]).then_inc(s_done, 16)
                sp.wait_ge(s_done, 16)


def kernel(**inputs):
    import concourse.bacc as bacc
    from concourse.bass_utils import run_bass_kernel_spmd

    nc = bacc.Bacc("TRN2", target_bir_lowering=False, num_devices=1)
    arrays, dram = {}, {}
    for name in INPUTS:
        a = np.ascontiguousarray(inputs[name])
        arrays["in_" + name] = a
        dram[name] = nc.dram_tensor("in_" + name, a.shape, mybir.dt.from_np(a.dtype), kind="ExternalInput").ap()
    c = np.concatenate([np.asarray(v, np.float32) for v in shape_constants().values()], axis=1)
    arrays["shape_constants"] = c
    consts = nc.dram_tensor("shape_constants", c.shape, FP32, kind="ExternalInput").ap()
    out = nc.dram_tensor("out", (BATCH, SEQ, D), FP32, kind="ExternalOutput").ap()
    arrays["bucket_onehots"] = bucket_onehots().astype(np.float32)
    onehots = nc.dram_tensor("bucket_onehots", arrays["bucket_onehots"].shape, FP32, kind="ExternalInput").ap()
    program(nc, dram, consts, onehots, out)
    r = run_bass_kernel_spmd(nc, [arrays], core_ids=[0])
    return r.results[0]["out"]
```

```python
from contextlib import ExitStack

import numpy as np

import concourse.bass as bass
from concourse import mybir

FP32 = mybir.dt.float32
BF16 = mybir.dt.bfloat16
I32 = mybir.dt.int32
U32 = mybir.dt.uint32
ALU = mybir.AluOpType
ACT = mybir.ActivationFunctionType
AX = mybir.AxisListType

P = 128
BATCH, SEQ, D = 16, 256, 128
TOKENS = BATCH * SEQ
TILES = TOKENS // P
EPS = 1e-5
E, F = 8, 512
FC = F // P
BLOCKS = TOKENS // P + E
SLOTS = BLOCKS * P
W1_AT, W2_AT, B1_AT, B2_AT = 0, F, F + FC * D, F + FC * D + FC
EXPERT_COLS = B2_AT + D


class Mem:

    whole = None
    sems = {}

    def __init__(self, nc, stack, prefix):
        self.nc, self.stack, self.prefix = nc, stack, prefix

    def sb(self, name, shape, dt=FP32):
        return self.stack.enter_context(self.nc.sbuf_tensor(f"{self.prefix}_{name}", shape, dt))

    def sem(self, name, own=False):
        key = f"{self.prefix if own else self.prefix.strip('01')}_{name}"
        if key not in Mem.sems:
            Mem.sems[key] = Mem.whole.enter_context(self.nc.semaphore(key))
        return Mem.sems[key]

    def banks(self, n):
        return [self.stack.enter_context(self.nc.psum_tensor(f"{self.prefix}_bank{i}", [P, 512], FP32)) for i in range(n)]


def clear_semaphores(nc, handles):
    with nc.Block() as block:
        for n, engine in enumerate((block.sync, block.gpsimd, block.scalar, block.vector)):
            @engine
            def _(eng, n=n):
                for handle in handles[n::4]:
                    eng.sem_clear(handle)


def layernorm_transposed(nc, prefix, X, ident, XN, XT):
    with ExitStack() as stack:
        m = Mem(nc, stack, prefix)
        stats = m.sb("stats", [P, TILES, 6])
        mv = m.sb("mean_var", [P, TILES, 2])
        std = m.sb("std", [P, TILES])
        rstd = m.sb("rstd", [P, TILES])
        bank = m.banks(4)
        s_stats, s_mv, s_vareps, s_std, s_rstd, s_xn, s_xt_ps, s_xt = (
            m.sem(n) for n in ("stats", "mv", "vareps", "std", "rstd", "xn", "xt_ps", "xt"))
        block = stack.enter_context(nc.Block())

        @block.vector
        def _(dve):
            for t in range(TILES):
                dve.bn_stats(stats[:, t, :], X[:, t, :]).then_inc(s_stats, 1)
            for t in range(TILES):
                dve.wait_ge(s_stats, t + 1)
                dve.bn_aggr(mv[:, t, :], stats[:, t, :]).then_inc(s_mv, 1)
            dve.wait_ge(s_mv, TILES)
            dve.tensor_scalar(std[:, :], mv[:, :, 1], EPS, None, ALU.add).then_inc(s_vareps, 1)
            dve.wait_ge(s_std, 1)
            dve.reciprocal(rstd[:, :], std[:, :]).then_inc(s_rstd, 1)
            dve.wait_ge(s_rstd, 1)
            for t in range(TILES):
                dve.tensor_scalar(XN[:, t, :], X[:, t, :], mv[:, t, 0:1], rstd[:, t:t + 1],
                                  ALU.subtract, ALU.mult).then_inc(s_xn, 1)

        @block.tensor
        def _(pe):
            for t in range(TILES):
                g = t // 4
                pe.wait_ge(s_xn, t + 1)
                if t % 4 == 0 and g >= 4:
                    pe.wait_ge(s_xt, g - 3)
                pe.transpose(bank[g % 4][:, (t % 4) * P:(t % 4 + 1) * P], XN[:, t, :], ident).then_inc(s_xt_ps, 1)

        @block.scalar
        def _(act):
            act.wait_ge(s_vareps, 1)
            act.activation(std[:, :], std[:, :], ACT.Sqrt).then_inc(s_std, 1)
            for g in range(TILES // 4):
                act.wait_ge(s_xt_ps, 4 * g + 4)
                act.activation(XT[:, g * 512:(g + 1) * 512], bank[g % 4][:, :], ACT.Copy).then_inc(s_xt, 1)


def experts_layer(nc, prefix, X, con, w, slots_in, slots_out, s_cleared):
    with ExitStack() as stack:
        m = Mem(nc, stack, prefix)
        XN = m.sb("xn", [P, TILES, D])
        prob = m.sb("prob", [P, TILES])
        slot = m.sb("slot", [P, TILES], U32)
        bexp = m.sb("block_expert", [P, BLOCKS], I32)
        WA = m.sb("weights", [P, E, EXPERT_COLS])
        s_weights = m.sem("weights")
        with nc.Block() as block:
            @block.sync
            def _(sp):
                sp.dma_start(WA[:, :, W1_AT:W2_AT], w["w1"].rearrange("e d f -> d e f")).then_inc(s_weights, 16)
                sp.dma_start(WA[:, :, W2_AT:B1_AT], w["w2"].rearrange("e (p c) d -> p e (c d)", c=FC)).then_inc(s_weights, 16)
                sp.dma_start(WA[:, :, B1_AT:B2_AT], w["b1"].rearrange("e (p c) -> p e c", c=FC)).then_inc(s_weights, 16)
                sp.dma_start(WA[:, :, B2_AT:], w["b2"].partition_broadcast(P)).then_inc(s_weights, 16)
        route_tokens(nc, prefix + "r", X, con, w, XN, prob, slot, bexp)
        run_experts(nc, prefix + "e", X, con, WA, s_weights, XN, prob, slot, bexp, slots_in, slots_out, s_cleared)


def route_tokens(nc, prefix, X, con, w, XN, prob, slot, bexp):
    with ExitStack() as stack:
        m = Mem(nc, stack, prefix)
        XT = m.sb("xt", [P, TOKENS])
        layernorm_transposed(nc, prefix + "n", X, con["ident"], XN, XT)
        PAD = 16
        sw = m.sb("switch_w", [P, E])
        sbias = m.sb("switch_b", [P, E])
        L = m.sb("logits", [P, TILES, E])
        mx = m.sb("max", [P, TILES])
        ex = m.sb("exp", [P, TILES, E])
        es = m.sb("expsum", [P, TILES])
        cand = m.sb("cand", [P, TILES, E])
        ridx = m.sb("route", [P, TILES])
        hot = m.sb("onehot", [P, TILES, E])
        cnt = [m.sb(f"count{i}", [P, PAD + TILES, E]) for i in range(2)]
        cfirst = m.sb("counts", [P, TILES, E])
        nblk_i = m.sb("nblocks_i", [P, E], I32)
        pre = [m.sb(f"blockprefix{i}", [P, 4 + E]) for i in range(2)]
        pos = m.sb("pos", [P, TILES, E])
        offs = m.sb("offs", [P, E])
        slotf = m.sb("slotf", [P, TILES])
        ge = m.sb("ge", [P, BLOCKS, E])
        bexpf = m.sb("bexpf", [P, BLOCKS])
        bank = m.banks(3)
        s_w, s_logit, s_d, s_exp, s_hot, s_rank, s_v = (m.sem(n) for n in ("w", "logit", "d", "exp", "hot", "rank", "v"))
        block = stack.enter_context(nc.Block())
        psl, psr, psc = (bank[i][:, 0:TILES * E].rearrange("p (t e) -> p t e", e=E) for i in range(3))

        @block.sync
        def _(sp):
            sp.dma_start(sw[:, :], w["switch_w"]).then_inc(s_w, 16)
            sp.dma_start(sbias[:, :], w["switch_b"].partition_broadcast(P)).then_inc(s_w, 16)

        @block.tensor
        def _(pe):
            pe.wait_ge(s_w, 32)
            for t in range(TILES):
                last = pe.matmul(bank[0][:, t * E:(t + 1) * E], XT[:, t * P:(t + 1) * P], sw[:, :], start=True, stop=True)
            last.then_inc(s_logit, 1)
            pe.wait_ge(s_hot, 1)
            pe.matmul(bank[1][:, 0:TILES * E], con["below"], hot[:, :, :].rearrange("p t e -> p (t e)"), start=True, stop=True)
            pe.matmul(bank[2][:, 0:TILES * E], con["ones"], hot[:, :, :].rearrange("p t e -> p (t e)"), start=True, stop=True).then_inc(s_rank, 1)

        @block.scalar
        def _(act):
            act.wait_ge(s_d, 1)
            act.activation(ex[:, :, :], L[:, :, :], ACT.Exp).then_inc(s_exp, 1)

        @block.vector
        def _(dve):
            done = [0]

            def then(ins):
                done[0] += 1
                ins.then_inc(s_v, 1)
                dve.wait_ge(s_v, done[0])

            TE = [P, TILES, E]
            dve.wait_ge(s_w, 32)
            dve.wait_ge(s_logit, 1)
            then(dve.tensor_tensor(L[:, :, :], psl, sbias[:, :].unsqueeze(1).to_broadcast(TE), ALU.add))
            then(dve.tensor_reduce(mx[:, :], L[:, :, :], AX.X, ALU.max))
            dve.tensor_tensor(L[:, :, :], L[:, :, :], mx[:, :].unsqueeze(2).to_broadcast(TE), ALU.subtract).then_inc(s_d, 1)
            dve.wait_ge(s_d, 1)
            then(dve.tensor_scalar(cand[:, :, :], L[:, :, :], 0.0, float(E), ALU.is_lt, ALU.mult))
            then(dve.tensor_tensor(cand[:, :, :], cand[:, :, :], con["iota_e"].unsqueeze(1).to_broadcast(TE), ALU.add))
            then(dve.tensor_reduce(ridx[:, :], cand[:, :, :], AX.X, ALU.min))
            dve.tensor_tensor(hot[:, :, :], con["iota_e"].unsqueeze(1).to_broadcast(TE),
                              ridx[:, :].unsqueeze(2).to_broadcast(TE), ALU.is_equal).then_inc(s_hot, 1)
            dve.wait_ge(s_exp, 1)
            then(dve.tensor_reduce(es[:, :], ex[:, :, :], AX.X, ALU.add))
            dve.reciprocal(prob[:, :], es[:, :])
            dve.memset(cnt[0][:, 0:PAD, :], 0.0)
            dve.memset(cnt[1][:, 0:PAD, :], 0.0)
            dve.memset(pre[0][:, 0:4], 0.0)
            then(dve.memset(pre[1][:, 0:4], 0.0))
            dve.wait_ge(s_rank, 1)
            then(dve.tensor_copy(cfirst[:, :, :], psc))
            then(dve.tensor_copy(cnt[0][:, PAD:, :], cfirst[:, :, :]))
            for k in range(5):
                a, b = cnt[k % 2], cnt[(k + 1) % 2]
                then(dve.tensor_tensor(b[:, PAD:, :], a[:, PAD:, :], a[:, PAD - (1 << k):PAD + TILES - (1 << k), :], ALU.add))
            tot = cnt[1]
            then(dve.tensor_scalar(nblk_i[:, :], tot[:, PAD + TILES - 1, :], float(P - 1), None, ALU.add))
            then(dve.tensor_scalar(nblk_i[:, :], nblk_i[:, :], 7, None, ALU.arith_shift_right))
            then(dve.tensor_copy(pre[0][:, 4:], nblk_i[:, :]))
            for k in range(3):
                a, b = pre[k % 2], pre[(k + 1) % 2]
                then(dve.tensor_tensor(b[:, 4:], a[:, 4:], a[:, 4 - (1 << k):4 + E - (1 << k)], ALU.add))
            bend = pre[1]
            then(dve.tensor_scalar(offs[:, :], bend[:, 3:3 + E], float(P), None, ALU.mult))
            then(dve.tensor_tensor(pos[:, :, :], tot[:, PAD:, :], cfirst[:, :, :], ALU.subtract))
            then(dve.tensor_tensor(pos[:, :, :], psr, pos[:, :, :], ALU.add))
            then(dve.tensor_tensor(pos[:, :, :], pos[:, :, :], offs[:, :].unsqueeze(1).to_broadcast(TE), ALU.add))
            then(dve.tensor_tensor(pos[:, :, :], pos[:, :, :], hot[:, :, :], ALU.mult))
            then(dve.tensor_reduce(slotf[:, :], pos[:, :, :], AX.X, ALU.add))
            then(dve.tensor_copy(slot[:, :], slotf[:, :]))
            BE = [P, BLOCKS, E]
            then(dve.tensor_tensor(ge[:, :, :], con["iota_b"].unsqueeze(2).to_broadcast(BE),
                                   bend[:, 4:].unsqueeze(1).to_broadcast(BE), ALU.is_ge))
            then(dve.tensor_reduce(bexpf[:, :], ge[:, :, :], AX.X, ALU.add))
            then(dve.tensor_scalar(bexp[:, :], bexpf[:, :], float(E - 1), None, ALU.min))


def run_experts(nc, prefix, X, con, WA, s_weights, XN, prob, slot, bexp, slots_in, slots_out, s_cleared):
    with ExitStack() as stack:
        m = Mem(nc, stack, prefix)
        UNROLL = 4
        WB = [m.sb(f"expert_{i}", [P, EXPERT_COLS]) for i in range(UNROLL)]
        xb = [m.sb(f"xb_{i}", [P, D]) for i in range(UNROLL)]
        xbt = [m.sb(f"xbt_{i}", [P, P]) for i in range(2)]
        h = [m.sb(f"h_{i}", [P, FC, P]) for i in range(2)]
        y = [m.sb(f"y_{i}", [P, D]) for i in range(UNROLL)]
        G = m.sb("gathered", [P, TILES, D])
        bank = m.banks(6)
        px, ph, py = bank[0:2], bank[2:4], bank[4:6]
        s_wb, s_xt, s_xtc, s_h, s_g, s_yp, s_y = (m.sem(n) for n in ("wb", "xt", "xtc", "h", "gelu", "yp", "y"))
        s_scat = m.sem("scattered", own=True)
        GQ = 8
        s_gath = [m.sem(f"gathered{q}", own=True) for q in range(TILES // GQ)]
        s_x = [m.sem(f"x{i}") for i in range(UNROLL)]
        s_out = [m.sem(f"out{i}") for i in range(UNROLL)]
        GROUPS = BLOCKS // UNROLL
        block = stack.enter_context(nc.Block())

        def over_blocks(engine, step):
            for i in range(UNROLL):
                step(0, i)
            with engine.Fori(1, GROUPS - 1) as g:
                for i in range(UNROLL):
                    step(g, i)
            for i in range(UNROLL):
                step(GROUPS - 1, i)

        def wait_over(engine, semaphore, count):
            if not isinstance(count, int) or count > 0:
                engine.wait_ge(semaphore, count)

        @block.gpsimd
        def _(pool):
            pool.wait_ge(s_cleared, 16)
            for t in range(TILES):
                pool.indirect_dma_start(slots_in, bass.IndirectOffsetOnAxis(ap=slot[:, t:t + 1], axis=0),
                                        XN[:, t, :], None).then_inc(s_scat, 16)
            for i in range(UNROLL):
                pool.wait_ge(s_out[i], 16 * GROUPS)
            for t in range(TILES):
                pool.indirect_dma_start(G[:, t, :], None, slots_out,
                                        bass.IndirectOffsetOnAxis(ap=slot[:, t:t + 1], axis=0)).then_inc(s_gath[t // GQ], 16)

        @block.sync
        def _(sp):
            sp.wait_ge(s_scat, 16 * TILES)

            def rows(g, i):
                wait_over(sp, s_xt, UNROLL * (g - 1) + i + 1)
                sp.dma_start(xb[i][:, :], slots_in[bass.ds((UNROLL * g + i) * P, P), :]).then_inc(s_x[i], 16)

            def store(g, i):
                sp.wait_ge(s_y, UNROLL * g + i + 1)
                sp.dma_start(slots_out[bass.ds((UNROLL * g + i) * P, P), :], y[i][:, :]).then_inc(s_out[i], 16)

            def step(g, i):
                rows(g, i)
                if not isinstance(g, int) or g > 0:
                    store(g - 1, i)

            over_blocks(sp, step)
            for i in range(UNROLL):
                store(GROUPS - 1, i)

        @block.tensor
        def _(pe):
            def transposed(g, i):
                k = UNROLL * g + i
                pe.wait_ge(s_x[i], 16 * (g + 1))
                wait_over(pe, s_xtc, k - 1)
                pe.transpose(px[i % 2][:, 0:P], xb[i][:, :], con["ident"]).then_inc(s_xt, 1)

            def up(g, i):
                k = UNROLL * g + i
                pe.wait_ge(s_wb, k + 1)
                pe.wait_ge(s_xtc, k + 1)
                wait_over(pe, s_g, FC * (k - 1))
                for c in range(FC):
                    last = pe.matmul(ph[i % 2][:, c * P:(c + 1) * P], WB[i][:, W1_AT + c:W2_AT:FC], xbt[i % 2][:, :], start=True, stop=True)
                last.then_inc(s_h, 1)

            def down(g, i):
                k = UNROLL * g + i
                wait_over(pe, s_y, k - 1)
                pe.matmul(py[i % 2][:, 0:D], con["ones"][0:1, :], WB[i][0:1, B2_AT:], start=True, stop=False)
                for c in range(FC):
                    pe.wait_ge(s_g, FC * k + c + 1)
                    last = pe.matmul(py[i % 2][:, 0:D], h[i % 2][:, c, :], WB[i][:, W2_AT + c * D:W2_AT + (c + 1) * D], start=False, stop=(c == FC - 1))
                last.then_inc(s_yp, 1)

            def step(g, i):
                up(g, i)
                if i < UNROLL - 1:
                    transposed(g, i + 1)
                elif not isinstance(g, int) or g < GROUPS - 1:
                    transposed(g + 1, 0)
                if i > 0:
                    down(g, i - 1)
                elif not isinstance(g, int) or g > 0:
                    down(g - 1, UNROLL - 1)

            transposed(0, 0)
            over_blocks(pe, step)
            down(GROUPS - 1, UNROLL - 1)

        @block.scalar
        def _(act):
            def gelu(g, i):
                k = UNROLL * g + i
                act.wait_ge(s_h, k + 1)
                wait_over(act, s_yp, k - 1)
                for c in range(FC):
                    act.activation(h[i % 2][:, c, :], ph[i % 2][:, c * P:(c + 1) * P], ACT.Gelu_apprx_tanh,
                                   bias=WB[i][:, B1_AT + c:B1_AT + c + 1]).then_inc(s_g, 1)

            over_blocks(act, gelu)

        @block.vector
        def _(dve):
            def expert(g, i):
                e = dve.value_load(bexp[0:1, bass.ds(UNROLL * g + i, 1)], min_val=0, max_val=E - 1)
                wait_over(dve, s_yp, UNROLL * (g - 1) + i + 1)
                dve.tensor_copy(WB[i][:, :], WA[:, bass.ds(e, 1), :].rearrange("p a n -> p (a n)")).then_inc(s_wb, 1)

            def rows(g, i):
                k = UNROLL * g + i
                dve.wait_ge(s_xt, k + 1)
                wait_over(dve, s_h, k - 1)
                dve.tensor_copy(xbt[i % 2][:, :], px[i % 2][:, 0:P]).then_inc(s_xtc, 1)

            def result(g, i):
                dve.wait_ge(s_yp, UNROLL * g + i + 1)
                wait_over(dve, s_out[i], 16 * g)
                dve.tensor_copy(y[i][:, :], py[i % 2][:, 0:D]).then_inc(s_y, 1)

            def step(g, i):
                more = not isinstance(g, int) or g < GROUPS - 1
                if i < UNROLL - 2 or more:
                    expert(g + (i + 2) // UNROLL, (i + 2) % UNROLL)
                if i < UNROLL - 1 or more:
                    rows(g + (i + 1) // UNROLL, (i + 1) % UNROLL)
                if i > 0:
                    result(g, i - 1)
                elif not isinstance(g, int) or g > 0:
                    result(g - 1, UNROLL - 1)

            dve.wait_ge(s_weights, 64)
            expert(0, 0)
            expert(0, 1)
            rows(0, 0)
            over_blocks(dve, step)
            result(GROUPS - 1, UNROLL - 1)
            for t in range(TILES):
                if t % GQ == 0:
                    dve.wait_ge(s_gath[t // GQ], 16 * GQ)
                dve.scalar_tensor_tensor(X[:, t, :], G[:, t, :], prob[:, t:t + 1], X[:, t, :], ALU.mult, ALU.add)


HA, DA = 8, D // 8
ATTN_EPS = 1e-6


def linear_attention_layer(nc, prefix, X, con, w):
    with ExitStack() as stack:
        m = Mem(nc, stack, prefix)
        XN = m.sb("xn", [P, TILES, D])
        M2 = m.sb("msg", [P, TILES, D])
        ML = m.sb("mlp", [P, TILES, D])
        with ExitStack() as inner:
            XT = Mem(nc, inner, prefix).sb("xt", [P, TOKENS])
            layernorm_transposed(nc, prefix + "n", X, con["ident"], XN, XT)
            linear_attention(nc, prefix + "l", con, w, XT, M2, ML)
        add_normalised(nc, prefix + "a", X, w, XN, M2, ML)


def linear_attention(nc, prefix, con, w, XT, M2, ML):
    with ExitStack() as stack:
        m = Mem(nc, stack, prefix)
        Wq, Wm = m.sb("wq", [P, D]), m.sb("wm", [P, D])
        W1, W2 = m.sb("w1", [P, 2 * D]), m.sb("w2", [P, 2, D])
        xt = m.sb("xt", [P, SEQ])
        q = m.sb("q", [P, 2, D + 1])
        neg = m.sb("neg", [P, 2, D])
        feat = m.sb("feat", [P, 2, D])
        featT = m.sb("featT", [P, SEQ])
        kv = m.sb("kv", [P, D + HA])
        den = m.sb("den", [P, 2, HA])
        msg = m.sb("msg", [P, 2, D])
        msgT = m.sb("msgT", [P, SEQ])
        m2T = m.sb("m2T", [P, SEQ])
        h1 = m.sb("h1", [P, 2, SEQ])
        bank = m.banks(8)
        (s_w, s_one, s_xt, s_q, s_qc, s_neg, s_exp, s_feat, s_kv, s_ft, s_kvm, s_ftc, s_un, s_den, s_rec, s_msg,
         s_mt, s_mtc, s_m2, s_m2t, s_m2c, s_h, s_relu, s_ml, s_mlc, s_m2s) = (m.sem(n) for n in (
             "w", "one", "xtc", "q", "qc", "neg", "exp", "feat", "kvp", "ft", "kvm", "ftc", "un", "denom", "rec", "msgs",
             "mt", "mtc", "m2", "m2t", "m2c", "h", "relu", "ml", "mlc", "m2s"))
        block = stack.enter_context(nc.Block())
        pq, pkv, pft, pun, pmt, pm2t, pm2, ph = bank
        pml = pq

        @block.sync
        def _(sp):
            sp.dma_start(Wq[:, :], w["Wq"]).then_inc(s_w, 16)
            sp.dma_start(Wm[:, :], w["Wm"]).then_inc(s_w, 16)
            sp.dma_start(W1[:, :], w["W1"]).then_inc(s_w, 16)
            sp.dma_start(W2[:, :, :], w["W2"].rearrange("(c p) d -> p c d", p=P)).then_inc(s_w, 16)

        @block.tensor
        def _(pe):
            pe.wait_ge(s_w, 64)
            with pe.Fori(0, BATCH) as b:
                pe.wait_ge(s_xt, b + 1)
                for u in range(2):
                    last = pe.matmul(pq[:, u * D:(u + 1) * D], xt[:, u * P:(u + 1) * P], Wq[:, :], start=True, stop=True)
                last.then_inc(s_q, 1)
                pe.wait_ge(s_qc, b + 1)
                pe.wait_ge(s_feat, b + 1)
                for u in range(2):
                    last = pe.matmul(pkv[:, 0:D + 1], feat[:, u, :], q[:, u, :], start=(u == 0), stop=(u == 1))
                last.then_inc(s_kv, 1)
                for u in range(2):
                    last = pe.transpose(pft[:, u * P:(u + 1) * P], feat[:, u, :], con["ident"])
                last.then_inc(s_ft, 1)
                pe.wait_ge(s_kvm, b + 1)
                pe.wait_ge(s_ftc, b + 1)
                for u in range(2):
                    last = pe.matmul(pun[:, u * (D + HA):(u + 1) * (D + HA)], featT[:, u * P:(u + 1) * P], kv[:, :], start=True, stop=True)
                last.then_inc(s_un, 1)
                pe.wait_ge(s_msg, b + 1)
                for u in range(2):
                    last = pe.transpose(pmt[:, u * P:(u + 1) * P], msg[:, u, :], con["ident"])
                last.then_inc(s_mt, 1)
                pe.wait_ge(s_mtc, b + 1)
                pe.matmul(pm2t[:, 0:SEQ], Wm[:, :], msgT[:, :], start=True, stop=True).then_inc(s_m2t, 1)
                for u in range(2):
                    last = pe.matmul(pm2[:, u * D:(u + 1) * D], msgT[:, u * P:(u + 1) * P], Wm[:, :], start=True, stop=True)
                last.then_inc(s_m2, 1)
                pe.wait_ge(s_m2c, b + 1)
                for c in range(2):
                    last = pe.matmul(ph[:, c * SEQ:(c + 1) * SEQ], W1[:, c * P:(c + 1) * P], m2T[:, :], start=True, stop=True)
                last.then_inc(s_h, 1)
                pe.wait_ge(s_relu, b + 1)
                for u in range(2):
                    for c in range(2):
                        last = pe.matmul(pml[:, u * D:(u + 1) * D], h1[:, c, u * P:(u + 1) * P], W2[:, c, :], start=(c == 0), stop=(c == 1))
                last.then_inc(s_ml, 1)
                pe.wait_ge(s_mlc, b + 1)

        @block.scalar
        def _(act):
            with act.Fori(0, BATCH) as b:
                act.wait_ge(s_neg, b + 1)
                act.activation(neg[:, :, :], neg[:, :, :], ACT.Exp).then_inc(s_exp, 1)
                act.wait_ge(s_ft, b + 1)
                act.activation(featT[:, :], pft[:, 0:SEQ], ACT.Copy).then_inc(s_ftc, 1)
                act.wait_ge(s_mt, b + 1)
                act.activation(msgT[:, :], pmt[:, 0:SEQ], ACT.Copy).then_inc(s_mtc, 1)
                act.wait_ge(s_m2t, b + 1)
                act.activation(m2T[:, :], pm2t[:, 0:SEQ], ACT.Copy).then_inc(s_m2c, 1)
                act.wait_ge(s_h, b + 1)
                act.activation(h1[:, :, :], ph[:, :].rearrange("p (c s) -> p c s", c=2), ACT.Relu).then_inc(s_relu, 1)

        @block.vector
        def _(dve):
            dve.memset(q[:, :, D:D + 1], 1.0).then_inc(s_one, 1)
            dve.wait_ge(s_one, 1)
            with dve.Fori(0, BATCH) as b:
                dve.tensor_copy(xt[:, :], XT[:, bass.ds(b * SEQ, SEQ)]).then_inc(s_xt, 1)
                dve.wait_ge(s_q, b + 1)
                pq3 = pq[:, 0:SEQ].rearrange("p (u d) -> p u d", u=2)
                dve.tensor_scalar(neg[:, :, :], pq3, 0.0, None, ALU.min).then_inc(s_neg, 1)
                dve.tensor_copy(q[:, :, 0:D], pq3).then_inc(s_qc, 1)
                dve.wait_ge(s_exp, b + 1)
                dve.scalar_tensor_tensor(feat[:, :, :], pq3, 0.0, neg[:, :, :], ALU.max, ALU.add).then_inc(s_feat, 1)
                dve.wait_ge(s_kv, b + 1)
                dve.tensor_tensor(kv[:, 0:D], pkv[:, 0:D], con["head_block"], ALU.mult)
                dve.tensor_scalar(kv[:, D:D + HA], con["head_of"], pkv[:, D:D + 1], None, ALU.mult).then_inc(s_kvm, 1)
                dve.wait_ge(s_un, b + 1)
                un = pun[:, 0:2 * (D + HA)].rearrange("p (u n) -> p u n", u=2)
                dve.tensor_scalar(den[:, :, :], un[:, :, D:], ATTN_EPS, None, ALU.add).then_inc(s_den, 1)
                dve.wait_ge(s_den, b + 1)
                dve.reciprocal(den[:, :, :], den[:, :, :]).then_inc(s_rec, 1)
                dve.wait_ge(s_rec, b + 1)
                for u in range(2):
                    last = dve.tensor_tensor(msg[:, u, :].rearrange("p (h v) -> p h v", h=HA), un[:, u, 0:D].rearrange("p (h v) -> p h v", h=HA),
                                             den[:, u, :].unsqueeze(2).to_broadcast([P, HA, DA]), ALU.mult)
                last.then_inc(s_msg, 1)
                dve.wait_ge(s_m2, b + 1)
                dve.tensor_copy(M2[:, bass.ds(2 * b, 2), :], pm2[:, 0:SEQ].rearrange("p (u d) -> p u d", u=2)).then_inc(s_m2s, 1)
                dve.wait_ge(s_ml, b + 1)
                dve.tensor_copy(ML[:, bass.ds(2 * b, 2), :], pml[:, 0:SEQ].rearrange("p (u d) -> p u d", u=2)).then_inc(s_mlc, 1)


def add_normalised(nc, prefix, X, w, XN, M2, ML):
    with ExitStack() as stack:
        m = Mem(nc, stack, prefix)
        gain = m.sb("gain", [P, 2, D])
        bias = m.sb("bias", [P, 2, D])
        stats = m.sb("stats", [P, 2 * TILES, 6])
        mv = m.sb("mean_var", [P, 2 * TILES, 2])
        std = m.sb("std", [P, 2 * TILES])
        rstd = m.sb("rstd", [P, 2 * TILES])
        s_w, s_stats, s_mv, s_ve, s_std, s_rstd, s_norm, s_gain, s_x, s_b = (m.sem(n) for n in (
            "w", "stats", "mv", "vareps", "std", "rstd", "norm", "gain", "x", "b"))
        block = stack.enter_context(nc.Block())

        @block.sync
        def _(sp):
            for j, n in enumerate(("g1", "g2")):
                sp.dma_start(gain[:, j, :], w[n].partition_broadcast(P)).then_inc(s_w, 16)
            for j, n in enumerate(("b1", "b2")):
                sp.dma_start(bias[:, j, :], w[n].partition_broadcast(P)).then_inc(s_w, 16)

        @block.scalar
        def _(act):
            act.wait_ge(s_ve, 1)
            act.activation(std[:, :], std[:, :], ACT.Sqrt).then_inc(s_std, 1)

        @block.gpsimd
        def _(pool):
            pool.tensor_tensor(X[:, :, :], X[:, :, :], XN[:, :, :], ALU.add).then_inc(s_x, 1)
            pool.wait_ge(s_x, 1)
            pool.wait_ge(s_w, 64)
            n = 1
            for j in range(2):
                pool.tensor_tensor(X[:, :, :], X[:, :, :], bias[:, j, :].unsqueeze(1).to_broadcast([P, TILES, D]), ALU.add).then_inc(s_x, 1)
                n += 1
                pool.wait_ge(s_x, n)
            for j, Y in enumerate((M2, ML)):
                pool.wait_ge(s_gain, 4 * (j + 1))
                pool.tensor_tensor(X[:, :, :], X[:, :, :], Y[:, :, :], ALU.add).then_inc(s_x, 1)
                n += 1
                pool.wait_ge(s_x, n)

        @block.vector
        def _(dve):
            for j, Y in enumerate((M2, ML)):
                for t in range(TILES):
                    dve.bn_stats(stats[:, j * TILES + t, :], Y[:, t, :]).then_inc(s_stats, 1)
            for t in range(2 * TILES):
                dve.wait_ge(s_stats, t + 1)
                dve.bn_aggr(mv[:, t, :], stats[:, t, :]).then_inc(s_mv, 1)
            dve.wait_ge(s_mv, 2 * TILES)
            dve.tensor_scalar(std[:, :], mv[:, :, 1], EPS, None, ALU.add).then_inc(s_ve, 1)
            dve.wait_ge(s_std, 1)
            dve.reciprocal(rstd[:, :], std[:, :]).then_inc(s_rstd, 1)
            dve.wait_ge(s_rstd, 1)
            dve.wait_ge(s_w, 64)
            for j, Y in enumerate((M2, ML)):
                for t in range(TILES):
                    n = j * TILES + t
                    dve.tensor_scalar(Y[:, t, :], Y[:, t, :], mv[:, n, 0:1], rstd[:, n:n + 1], ALU.subtract, ALU.mult).then_inc(s_norm, 1)
                for g in range(4):
                    dve.wait_ge(s_norm, j * TILES + 8 * g + 8)
                    part = Y[:, 8 * g:8 * g + 8, :]
                    dve.tensor_tensor(part, part, gain[:, j, :].unsqueeze(1).to_broadcast([P, 8, D]), ALU.mult).then_inc(s_gain, 1)


HB, DB = 16, D // 16
NB16 = SEQ // 16
BUCKETS, MAX_REL = 32, 64
OFFS = 2 * SEQ
TABLE = OFFS - 16
VW = DB + 1
NEG_HUGE = -3.0e38


def disentangled_attention_layer(nc, prefix, X, con, w, dram):
    with ExitStack() as stack:
        m = Mem(nc, stack, prefix)
        V = m.sb("v", [P, TILES, HB, VW])
        with ExitStack() as inner:
            mi = Mem(nc, inner, prefix)
            XT = mi.sb("xt", [P, TOKENS])
            XN = mi.sb("xn", [P, TILES, D])
            layernorm_transposed(nc, prefix + "n", X, con["ident"], XN, XT)
            project_qkv(nc, prefix + "p", X, con, w, XT, V, dram)
        position_tables(nc, prefix + "t", con, w, dram)
        attend(nc, prefix + "s", con, V, X, dram)
        return_context(nc, prefix + "o", X, con, w, dram)


def project_qkv(nc, prefix, X, con, w, XT, V, dram):
    with ExitStack() as stack:
        m = Mem(nc, stack, prefix)
        W = m.sb("w", [P, 3, D])
        b_col = m.sb("b_col", [P, 2])
        bv = m.sb("bv", [P, D])
        QT = [m.sb(f"qt{i}", [P, TOKENS]) for i in range(2)]
        part = [m.sb(f"part{i}", [P, 3, TOKENS], BF16) for i in range(2)]
        rest = [m.sb(f"rest{i}", [P, 512]) for i in range(3)]
        s_p1, s_rest, s_p2, s_p3 = m.sem("part1"), m.sem("rest"), m.sem("part2"), m.sem("part3")
        bank = m.banks(6)
        s_w, s_bs, s_q, s_qe, s_v, s_ve, s_one, s_out = (m.sem(n) for n in ("w", "bs", "q", "qe", "v", "ve", "one", "out"))
        scale = (1.0 / np.sqrt(3.0 * DB), 1.0)
        G = TOKENS // 512
        block = stack.enter_context(nc.Block())

        @block.sync
        def _(sp):
            for j, n in enumerate(("Wq", "Wk", "Wv")):
                sp.dma_start(W[:, j, :], w[n]).then_inc(s_w, 16)
            for j, n in enumerate(("bq", "bk")):
                sp.dma_start(b_col[:, j:j + 1], w[n].rearrange("(p o) -> p o", o=1)).then_inc(s_w, 16)
            sp.dma_start(bv[:, :], w["bv"].partition_broadcast(P)).then_inc(s_w, 16)
            sp.dma_start(dram["x"], X[:, :, :].rearrange("p t d -> p (t d)")).then_inc(s_out, 16)
            for j in range(2):
                sp.wait_ge(s_qe, G * (j + 1))
                sp.dma_start(dram["qk"][j], QT[j][:, :]).then_inc(s_out, 16)
            for j in range(2):
                sp.wait_ge(s_p3, G * (j + 1))
                sp.dma_start(dram["parts"][j].rearrange("i p n -> p i n"), part[j][:, :, :]).then_inc(s_out, 16)
            sp.wait_ge(s_out, 80)

        @block.tensor
        def _(pe):
            pe.wait_ge(s_w, 96)
            for n in range(2 * G):
                j, g = n // G, n % G
                if n >= 4:
                    pe.wait_ge(s_p1, n - 3)
                pe.matmul(bank[n % 4][:, :], W[:, j, :], XT[:, g * 512:(g + 1) * 512], start=True, stop=True).then_inc(s_q, 1)
            for t in range(TILES):
                if t % 4 == 0 and t >= 8:
                    pe.wait_ge(s_ve, t // 4 - 1)
                pe.matmul(bank[4 + t // 4 % 2][:, t % 4 * D:(t % 4 + 1) * D], XT[:, t * P:(t + 1) * P], W[:, 2, :], start=True, stop=True).then_inc(s_v, 1)

        @block.scalar
        def _(act):
            act.wait_ge(s_bs, 1)
            for n in range(2 * G):
                j, g = n // G, n % G
                act.wait_ge(s_q, n + 1)
                act.activation(QT[j][:, g * 512:(g + 1) * 512], bank[n % 4][:, :], ACT.Identity,
                               bias=b_col[:, j:j + 1], scale=float(scale[j])).then_inc(s_qe, 1)
                act.activation(part[j][:, 0, g * 512:(g + 1) * 512], bank[n % 4][:, :], ACT.Identity,
                               bias=b_col[:, j:j + 1], scale=float(scale[j])).then_inc(s_p1, 1)

        @block.vector
        def _(dve):
            dve.wait_ge(s_w, 96)
            dve.tensor_scalar(b_col[:, 0:1], b_col[:, 0:1], float(scale[0]), None, ALU.mult).then_inc(s_bs, 1)
            dve.memset(V[:, :, :, DB:], 1.0).then_inc(s_one, 1)
            for g in range(TILES // 4):
                dve.wait_ge(s_v, 4 * g + 4)
                for j in range(4):
                    last = dve.tensor_tensor(V[:, 4 * g + j, :, 0:DB], bank[4 + g % 2][:, j * D:(j + 1) * D].rearrange("p (h d) -> p h d", h=HB),
                                             bv[:, :].rearrange("p (h d) -> p h d", h=HB), ALU.add)
                last.then_inc(s_ve, 1)
            for n in range(2 * G + 1):
                if n < 2 * G:
                    j, g = n // G, n % G
                    cols = slice(g * 512, (g + 1) * 512)
                    dve.wait_ge(s_p1, n + 1)
                    dve.wait_ge(s_qe, n + 1)
                    if n >= 3:
                        dve.wait_ge(s_p3, n - 2)
                    dve.tensor_tensor(rest[n % 3][:, :], QT[j][:, cols], part[j][:, 0, cols], ALU.subtract).then_inc(s_rest, 1)
                if n >= 1:
                    j, g = (n - 1) // G, (n - 1) % G
                    cols = slice(g * 512, (g + 1) * 512)
                    dve.wait_ge(s_p2, n)
                    dve.tensor_tensor(part[j][:, 2, cols], rest[(n - 1) % 3][:, :], part[j][:, 1, cols], ALU.subtract).then_inc(s_p3, 1)

        @block.gpsimd
        def _(pool):
            for n in range(2 * G):
                j, g = n // G, n % G
                pool.wait_ge(s_rest, n + 1)
                pool.tensor_copy(part[j][:, 1, g * 512:(g + 1) * 512], rest[n % 3][:, :]).then_inc(s_p2, 1)


def position_tables(nc, prefix, con, w, dram):
    with ExitStack() as stack:
        m = Mem(nc, stack, prefix)
        R = m.sb("rel", [2 * BUCKETS, D])
        gb = m.sb("gb", [2 * BUCKETS, 2, D])
        Wp = m.sb("wp", [P, 2, D])
        bp = m.sb("bp", [2 * BUCKETS, 2, D])
        onehot = m.sb("onehot", [2 * BUCKETS, 2, OFFS])
        RT = m.sb("relt", [P, 2 * BUCKETS])
        PK = m.sb("pk", [2 * BUCKETS, 2, D])
        T = m.sb("tables", [P, 2, OFFS])
        stats, mv, std = m.sb("stats", [2 * BUCKETS, 6]), m.sb("mv", [2 * BUCKETS, 2]), m.sb("std", [2 * BUCKETS, 1])
        bank = m.banks(4)
        s_w, s_v, s_std, s_ve, s_re, s_rt, s_rtc, s_pk, s_pkc, s_t, s_tc, s_out = (m.sem(n) for n in (
            "w", "v", "std", "vareps", "re", "rt", "rtc", "pk", "pkc", "t", "tc", "out"))
        scale = (np.sqrt(3.0 * DB) / np.sqrt(2.0 * DB), 1.0 / np.sqrt(2.0 * DB))
        NBK = 2 * BUCKETS
        block = stack.enter_context(nc.Block())

        @block.sync
        def _(sp):
            sp.dma_start(R[:, :], w["rel_emb"]).then_inc(s_w, 16)
            for j, n in enumerate(("ln_g", "ln_b")):
                sp.dma_start(gb[:, j, :], w[n].partition_broadcast(NBK)).then_inc(s_w, 16)
            for j, n in enumerate(("k", "q")):
                sp.dma_start(Wp[:, j, :], w["Wp" + n]).then_inc(s_w, 16)
                sp.dma_start(bp[:, j, :], w["bp" + n].partition_broadcast(NBK)).then_inc(s_w, 16)
            sp.dma_start(onehot[:, :, :], dram["onehot"].rearrange("a (j x) -> a j x", j=2)).then_inc(s_w, 16)
            sp.wait_ge(s_tc, 1)
            sp.dma_start(dram["tables"].rearrange("j p x -> p j x"), T[:, :, :]).then_inc(s_out, 16)
            sp.wait_ge(s_out, 16)

        @block.scalar
        def _(act):
            act.wait_ge(s_ve, 1)
            act.activation(std[:, :], std[:, :], ACT.Sqrt).then_inc(s_std, 1)

        @block.vector
        def _(dve):
            done = [0]

            def then(ins):
                done[0] += 1
                ins.then_inc(s_v, 1)
                dve.wait_ge(s_v, done[0])

            dve.wait_ge(s_w, 128)
            then(dve.bn_stats(stats[:, :], R[:, :]))
            then(dve.bn_aggr(mv[:, :], stats[:, :]))
            dve.tensor_scalar(std[:, :], mv[:, 1:2], EPS, None, ALU.add).then_inc(s_ve, 1)
            dve.wait_ge(s_std, 1)
            then(dve.reciprocal(std[:, :], std[:, :]))
            then(dve.tensor_scalar(R[:, :], R[:, :], mv[:, 0:1], std[:, :], ALU.subtract, ALU.mult))
            then(dve.tensor_tensor(R[:, :], R[:, :], gb[:, 0, :], ALU.mult))
            dve.tensor_tensor(R[:, :], R[:, :], gb[:, 1, :], ALU.add).then_inc(s_re, 1)
            dve.wait_ge(s_rt, 1)
            dve.tensor_copy(RT[:, :], bank[0][:, 0:NBK]).then_inc(s_rtc, 1)
            dve.wait_ge(s_pk, 1)
            then(dve.tensor_tensor(PK[:, :, :], bank[1][0:NBK, 0:2 * D].rearrange("p (j d) -> p j d", j=2), bp[:, :, :], ALU.add))
            for j in range(2):
                last = dve.tensor_scalar(PK[:, j, :], PK[:, j, :], float(scale[j]), None, ALU.mult)
            last.then_inc(s_pkc, 1)
            dve.wait_ge(s_t, 1)
            for j in range(2):
                last = dve.tensor_copy(T[:, j, :], bank[2 + j][:, :])
            last.then_inc(s_tc, 1)

        @block.tensor
        def _(pe):
            pe.wait_ge(s_re, 1)
            pe.transpose(bank[0][:, 0:NBK], R[:, :], con["ident"][0:NBK, 0:NBK]).then_inc(s_rt, 1)
            pe.wait_ge(s_rtc, 1)
            for j in range(2):
                last = pe.matmul(bank[1][0:NBK, j * D:(j + 1) * D], RT[:, :], Wp[:, j, :], start=True, stop=True)
            last.then_inc(s_pk, 1)
            pe.wait_ge(s_pkc, 1)
            for j in range(2):
                last = pe.matmul(bank[2 + j][:, :], PK[:, j, :], onehot[:, j, :], start=True, stop=True)
            last.then_inc(s_t, 1)


def stacked_views(dram):
    n, part = TOKENS, P * TOKENS
    tab, qk, parts = (dram[name].tensor for name in ("tables", "qk", "parts"))
    return {
        "tables": [bass.AP(tensor=tab, offset=j * P * OFFS, ap=[[1, 16], [OFFS, P], [1, TABLE]]) for j in range(2)],
        "qk": [bass.AP(tensor=qk, offset=j * P * n, ap=[[0, 16], [n, P], [1, n]]) for j in range(2)],
        "q_parts": [bass.AP(tensor=parts, offset=i * part, ap=[[0, 3], [n, P], [1, n]]) for i in range(3)],
        "k_parts": bass.AP(tensor=parts, offset=3 * part, ap=[[part, 3], [n, P], [1, n]]),
    }


def attend(nc, prefix, con, V, CTX, dram):
    with ExitStack() as stack:
        m = Mem(nc, stack, prefix)
        QR = m.sb("qr", [P, TOKENS])
        KR = m.sb("kr", [P, TOKENS])
        QS = m.sb("qs", [9 * DB, TOKENS], BF16)
        KS = m.sb("ks", [9 * DB, TOKENS], BF16)
        TAB = m.sb("tab", [P, 2, TABLE])
        CT = m.sb("c2p_t", [P, 2, BATCH, SEQ])
        PC = m.sb("p2c", [P, 2, BATCH, SEQ])
        NS = 4
        S = [m.sb(f"scores{i}", [P, 2, SEQ]) for i in range(NS)]
        PT = [m.sb(f"probs_t{i}", [P, 2, SEQ]) for i in range(2)]
        mx = m.sb("max", [P, 2 * BATCH])
        rec = m.sb("rec", [P, 2 * BATCH])
        bank = m.banks(8)
        pb, pt1, pqk, pt2, pav = bank[0:2], bank[2:4], bank[4:6], bank[6], bank[7]
        (s_masked, s_bm, s_be, s_t1, s_z, s_qk, s_sc, s_sub0, s_sub1, s_t2, s_exp, s_av, s_rec, s_ctx,
         s_q, s_tab, s_stack, s_go_dve, s_go_pool, s_go_sp) = (m.sem(n) for n in (
             "masked", "bias_mm", "bias_copied", "t1", "z", "qk", "scores", "shifted0", "shifted1", "t2", "exp", "av", "rec", "ctx",
             "q", "tab", "stack", "go_dve", "go_pool", "go_sp"))
        PAIRS = NB16 // 2
        BM = 2 * PAIRS * 2
        views = stacked_views(dram)
        LAG = 3
        block = stack.enter_context(nc.Block())

        @block.sync
        def _(sp):
            with sp.Fori(0, HB) as head:
                rows = bass.ds(head * DB, DB)
                sp.wait_ge(s_be, head * BM + 2)
                sp.sem_inc(s_go_sp, 1)
                for j in range(2):
                    sp.dma_start(TAB[:, j, :], views["tables"][j][:, rows, :]).then_inc(s_tab, 16)
                for j, R in enumerate((QR, KR)):
                    sp.dma_start(R[:, :], views["qk"][j][:, rows, :]).then_inc(s_q, 16)
                sp.wait_ge(s_sc, head * BATCH + 2)
                sp.sem_inc(s_go_sp, 1)
                for i in range(3):
                    three = slice(i * 3 * DB, (i + 1) * 3 * DB)
                    sp.dma_start(QS[three, :], views["q_parts"][i][:, rows, :]).then_inc(s_stack, 16)
                    sp.dma_start(KS[three, :], views["k_parts"][:, rows, :]).then_inc(s_stack, 16)

        @block.gpsimd
        def _(pool):
            with pool.Fori(0, HB) as head:
                for b in range(BATCH):
                    pool.wait_ge(s_sc, head * BATCH + b + 3)
                    pool.sem_inc(s_go_pool, 1)
                    pool.tensor_scalar(S[b % NS][:, 1, :], S[b % NS][:, 1, :], mx[:, 2 * b + 1:2 * b + 2], None,
                                       ALU.subtract).then_inc(s_sub1, 1)

        @block.tensor
        def _(pe):
            pe.sem_inc(s_t2, NS)
            pe.sem_inc(s_av, 2)
            with pe.Fori(0, HB) as head:
                pe.wait_ge(s_tab, 16 * 2 * (head + 1))
                n = 0
                for kind, mov in ((0, QR), (1, KR)):
                    for pair in range(PAIRS):
                        pe.wait_ge(s_masked, head * 2 * PAIRS + kind * PAIRS + pair + 1)
                        for side in range(2):
                            pe.wait_ge(s_be, head * BM + n + 1)
                            for a in range(2):
                                grp = 2 * pair + a
                                c = TABLE - SEQ + P * side - 16 * grp
                                last = pe.matmul(pb[n % 2][:, a * 256:(a + 1) * 256], TAB[:, kind, c:c + P],
                                                 mov[:, :].rearrange("p (b g s) -> p g b s", b=BATCH, s=16)[:, grp, :, :],
                                                 start=True, stop=True)
                            last.then_inc(s_bm, 1)
                            n += 1
                pe.wait_ge(s_be, head * BM + BM + 2)
                pe.wait_ge(s_stack, 16 * 6 * (head + 1))

                def t1(b):
                    pe.wait_ge(s_z, head * BATCH + b + 1)
                    for st in range(2):
                        for kt in range(2):
                            last = pe.transpose(pt1[b % 2][:, st * SEQ + kt * P:st * SEQ + (kt + 1) * P],
                                                CT[:, kt, b, st * P:(st + 1) * P], con["ident"])
                    last.then_inc(s_t1, 1)

                def qk(b):
                    pe.wait_ge(s_sc, head * BATCH + b + 1)
                    for st in range(2):
                        last = pe.matmul(pqk[b % 2][:, st * SEQ:(st + 1) * SEQ], QS[:, b * SEQ + st * P:b * SEQ + (st + 1) * P],
                                         KS[:, b * SEQ:(b + 1) * SEQ], start=True, stop=True)
                    last.then_inc(s_qk, 1)

                def t2(b):
                    pe.wait_ge(s_sub0, head * BATCH + b + 1)
                    pe.wait_ge(s_sub1, head * BATCH + b + 1)
                    pe.wait_ge(s_exp, head * BATCH + b + 1)
                    for kt in range(2):
                        for st in range(2):
                            last = pe.transpose(pt2[:, kt * SEQ + st * P:kt * SEQ + (st + 1) * P],
                                                S[b % NS][:, st, kt * P:(kt + 1) * P], con["ident"])
                    last.then_inc(s_t2, 1)

                def av(b):
                    pe.wait_ge(s_exp, head * BATCH + b + 2)
                    if b == 0:
                        pe.wait_ge(s_ctx, head + 1)
                    for st in range(2):
                        for kt in range(2):
                            last = pe.matmul(pav[:, (2 * b + st) * VW:(2 * b + st + 1) * VW], PT[b % 2][:, kt, st * P:(st + 1) * P],
                                             V[:, 2 * b + kt, bass.ds(head, 1), :].rearrange("p a v -> p (a v)"),
                                             start=(kt == 0), stop=(kt == 1))
                    last.then_inc(s_av, 1)

                for n in range(BATCH + LAG + 1):
                    if n < BATCH:
                        t1(n)
                        qk(n)
                    if LAG <= n < BATCH + LAG:
                        t2(n - LAG)
                    if n >= LAG + 1:
                        av(n - LAG - 1)

        @block.scalar
        def _(act):
            act.sem_inc(s_be, 2)
            act.sem_inc(s_exp, 1)
            with act.Fori(0, HB) as head:
                n = 0
                for dst in (CT, PC):
                    for pair in range(PAIRS):
                        for side in range(2):
                            act.wait_ge(s_bm, head * BM + n + 1)
                            o = dst[:, side, :, pair * 32:(pair + 1) * 32].rearrange("p b (a s) -> p a b s", a=2)
                            act.activation(o, pb[n % 2][:, :].rearrange("p (a b s) -> p a b s", a=2, b=BATCH), ACT.Copy).then_inc(s_be, 1)
                            n += 1
                for b in range(BATCH):
                    act.wait_ge(s_t2, head * BATCH + b + NS + 1)
                    act.wait_ge(s_av, head * BATCH + b + 1)
                    act.activation(PT[b % 2][:, :, :], pt2[:, :].rearrange("p (k s) -> p k s", k=2), ACT.Exp).then_inc(s_exp, 1)

        @block.vector
        def _(dve):
            dve.sem_inc(s_z, 2)
            dve.sem_inc(s_sc, 2)
            dve.sem_inc(s_ctx, 1)
            with dve.Fori(0, HB) as head:
                dve.wait_ge(s_q, 16 * 2 * (head + 1))
                for R in (QR, KR):
                    for pair in range(PAIRS):
                        for a in range(2):
                            part = R[:, :].rearrange("p (b g s) -> p g b s", b=BATCH, s=16)[:, 2 * pair + a, :, :]
                            last = dve.tensor_tensor(part, part, con["own_pos"].unsqueeze(1).to_broadcast([P, BATCH, 16]), ALU.mult)
                        last.then_inc(s_masked, 1)
                dve.wait_ge(s_be, head * BM + BM + 2)
                for b in range(BATCH):
                    dve.wait_ge(s_t1, head * BATCH + b + 1)
                    z = PC[:, :, b, :]
                    dve.tensor_tensor(z, pt1[b % 2][:, :].rearrange("p (a k) -> p a k", a=2), z, ALU.add).then_inc(s_z, 1)
                    dve.wait_ge(s_z, head * BATCH + b + 3)
                    dve.wait_ge(s_qk, head * BATCH + b + 1)
                    dve.wait_ge(s_t2, head * BATCH + b + 1)
                    dve.sem_inc(s_go_dve, 1)
                    for st in range(2):
                        last = dve.tensor_tensor_reduce(out=S[b % NS][:, st, :], in0=pqk[b % 2][:, st * SEQ:(st + 1) * SEQ], in1=PC[:, st, b, :],
                                                        scale=1.0, scalar=NEG_HUGE, op0=ALU.add, op1=ALU.max,
                                                        accum_out=mx[:, 2 * b + st:2 * b + st + 1])
                    last.then_inc(s_sc, 1)
                    dve.wait_ge(s_sc, head * BATCH + b + 3)
                    dve.tensor_scalar(S[b % NS][:, 0, :], S[b % NS][:, 0, :], mx[:, 2 * b:2 * b + 1], None, ALU.subtract).then_inc(s_sub0, 1)
                dve.wait_ge(s_av, head * BATCH + BATCH + 2)
                o = pav[:, 0:2 * BATCH * VW].rearrange("p (t v) -> p t v", v=VW)
                dve.reciprocal(rec[:, :], o[:, :, DB]).then_inc(s_rec, 1)
                dve.wait_ge(s_rec, head + 1)
                dve.tensor_tensor(CTX[:, :, bass.ds(head * DB, DB)], o[:, :, 0:DB],
                                  rec[:, :].unsqueeze(2).to_broadcast([P, TILES, DB]), ALU.mult).then_inc(s_ctx, 1)


def return_context(nc, prefix, X, con, w, dram):
    with ExitStack() as stack:
        m = Mem(nc, stack, prefix)
        Wo = m.sb("wo", [P, D])
        bo = m.sb("bo", [P, D])
        XR = m.sb("x", [P, TILES, D])
        CXT = m.sb("ctx_t", [P, TOKENS])
        bank = m.banks(4)
        s_w, s_t, s_tc, s_o, s_x, s_b = (m.sem(n) for n in ("w", "t", "tc", "o", "x", "b"))
        block = stack.enter_context(nc.Block())

        @block.sync
        def _(sp):
            sp.dma_start(Wo[:, :], w["Wo"]).then_inc(s_w, 16)
            sp.dma_start(bo[:, :], w["bo"].partition_broadcast(P)).then_inc(s_w, 16)
            sp.dma_start(XR[:, :, :].rearrange("p t d -> p (t d)"), dram["x"]).then_inc(s_w, 16)

        @block.tensor
        def _(pe):
            pe.wait_ge(s_w, 48)
            for g in range(TILES // 4):
                if g >= 2:
                    pe.wait_ge(s_tc, g - 1)
                for j in range(4):
                    last = pe.transpose(bank[g % 2][:, j * P:(j + 1) * P], X[:, 4 * g + j, :], con["ident"])
                last.then_inc(s_t, 1)
                pe.wait_ge(s_tc, g + 1)
                if g >= 2:
                    pe.wait_ge(s_x, g - 1)
                for j in range(4):
                    t = 4 * g + j
                    last = pe.matmul(bank[2 + g % 2][:, j * D:(j + 1) * D], CXT[:, t * P:(t + 1) * P], Wo[:, :], start=True, stop=True)
                last.then_inc(s_o, 1)

        @block.scalar
        def _(act):
            for g in range(TILES // 4):
                act.wait_ge(s_t, g + 1)
                act.activation(CXT[:, g * 512:(g + 1) * 512], bank[g % 2][:, :], ACT.Copy).then_inc(s_tc, 1)

        @block.vector
        def _(dve):
            dve.wait_ge(s_w, 48)
            dve.tensor_tensor(XR[:, :, :], XR[:, :, :], bo[:, :].unsqueeze(1).to_broadcast([P, TILES, D]), ALU.add).then_inc(s_b, 1)
            dve.wait_ge(s_b, 1)
            for g in range(TILES // 4):
                dve.wait_ge(s_o, g + 1)
                dve.tensor_tensor(X[:, 4 * g:4 * g + 4, :], bank[2 + g % 2][:, :].rearrange("p (t d) -> p t d", t=4),
                                  XR[:, 4 * g:4 * g + 4, :], ALU.add).then_inc(s_x, 1)


def bucket(rel):
    mid = BUCKETS // 2
    size = np.where(np.abs(rel) < mid, mid - 1, np.abs(rel)).astype(np.float32)
    far = np.ceil(np.log(size / np.float32(mid)) / np.float32(np.log((MAX_REL - 1) / mid)) * np.float32(mid - 1)) + mid
    return np.where(size <= mid, rel, far * np.sign(rel)).astype(np.int64)


def bucket_onehots():
    x = np.arange(OFFS)
    rows = [np.clip(bucket(off) + BUCKETS, 0, 2 * BUCKETS - 1) for off in (SEQ - 1 - x, x - SEQ + 1)]
    return np.concatenate([np.arange(2 * BUCKETS)[:, None] == r[None, :] for r in rows], axis=1)


INPUTS = ["L0_attn_a_x"] + ["L0_attn_a_" + n for n in ("Wq", "Wm", "W1", "W2", "g1", "b1", "g2", "b2")] + \
    ["L0_attn_b_" + n for n in ("Wq", "bq", "Wk", "bk", "Wv", "bv", "Wo", "bo", "rel_emb", "ln_g", "ln_b", "Wpk", "bpk", "Wpq", "bpq")] + \
    ["L0_ffn_" + n for n in ("switch_w", "switch_b", "w1", "b1", "w2", "b2")]


def shape_constants():
    row = np.arange(P)
    return {
        "ident": np.eye(P),
        "ones": np.ones((P, P)),
        "below": row[:, None] < row[None, :],
        "iota_e": np.broadcast_to(np.arange(E), (P, E)),
        "head_block": row[:, None] // DA == row[None, :] // DA,
        "head_of": row[:, None] // DA == np.arange(HA)[None, :],
        "own_pos": 15 - row[:, None] // DB == np.arange(16)[None, :],
        "iota_b": np.broadcast_to(np.arange(BLOCKS), (P, BLOCKS)),
    }


def program(nc, dram, consts, onehots, out):
    x = dram["L0_attn_a_x"].rearrange("b (u p) d -> p (b u) d", p=P)
    y = out.rearrange("b (u p) d -> p (b u) d", p=P)
    with ExitStack() as stack:
        Mem.whole, Mem.sems = stack, {}
        m = Mem(nc, stack, "all")
        X = m.sb("x", [P, TILES, D])
        width = consts.shape[1]
        C = m.sb("constants", [P, width])
        con, at = {}, 0
        for name, v in shape_constants().items():
            con[name] = C[:, at:at + v.shape[1]]
            at += v.shape[1]
        ffn = {n: dram["L0_ffn_" + n] for n in ("switch_w", "switch_b", "w1", "b1", "w2", "b2")}
        s_in = m.sem("in")
        s_done = m.sem("done")
        zero = m.sb("zero", [P, D])
        s_zero = m.sem("zero")
        slots_in = [nc.dram_tensor(f"slots_in{layer}", (SLOTS, D), FP32, kind="Internal").ap() for layer in range(2)]
        s_clear = [m.sem(f"cleared{layer}") for layer in range(2)]
        with nc.Block() as block:
            @block.sync
            def _(sp):
                sp.dma_start(X[:, :, :], x).then_inc(s_in, 16)
                sp.dma_start(C[:, :], consts).then_inc(s_in, 16)
                sp.wait_ge(s_zero, 1)
                for slots, s_cleared in zip(slots_in, s_clear):
                    sp.dma_start(slots.rearrange("(p b) d -> p b d", p=P), zero[:, :].unsqueeze(1).to_broadcast([P, BLOCKS, D])).then_inc(s_cleared, 16)
                sp.wait_ge(s_in, 32)

            @block.vector
            def _(dve):
                dve.memset(zero[:, :], 0.0).then_inc(s_zero, 1)
        linear_attention_layer(nc, "a", X, con, {n: dram["L0_attn_a_" + n] for n in ("Wq", "Wm", "W1", "W2", "g1", "b1", "g2", "b2")})
        def experts(layer):
            b = nc.dram_tensor(f"slots_out{layer}", (SLOTS, D), FP32, kind="Internal").ap()
            experts_layer(nc, f"{layer}f", X, con, ffn, slots_in[layer], b, s_clear[layer])

        experts(0)
        clear_semaphores(nc, [handle for key, handle in Mem.sems.items() if key.startswith("f")])
        scratch = {n: nc.dram_tensor("scratch_" + n, shape, dt, kind="Internal").ap() for n, shape, dt in (
            ("x", (P, TILES * D), FP32), ("qk", (2, P, TOKENS), FP32), ("parts", (2, 3, P, TOKENS), BF16),
            ("tables", (2, P, OFFS), FP32))}
        disentangled_attention_layer(nc, "d", X, con, {n: dram["L0_attn_b_" + n] for n in (
            "Wq", "bq", "Wk", "bk", "Wv", "bv", "Wo", "bo", "rel_emb", "ln_g", "ln_b", "Wpk", "bpk", "Wpq", "bpq")},
            dict(scratch, onehot=onehots))
        experts(1)
        with nc.Block() as block:
            @block.sync
            def _(sp):
                sp.dma_start(y, X[:, :, :]).then_inc(s_done, 16)
                sp.wait_ge(s_done, 16)


def kernel(**inputs):
    import concourse.bacc as bacc
    from concourse.bass_utils import run_bass_kernel_spmd

    nc = bacc.Bacc("TRN2", target_bir_lowering=False, num_devices=1)
    arrays, dram = {}, {}
    for name in INPUTS:
        a = np.ascontiguousarray(inputs[name])
        arrays["in_" + name] = a
        dram[name] = nc.dram_tensor("in_" + name, a.shape, mybir.dt.from_np(a.dtype), kind="ExternalInput").ap()
    c = np.concatenate([np.asarray(v, np.float32) for v in shape_constants().values()], axis=1)
    arrays["shape_constants"] = c
    consts = nc.dram_tensor("shape_constants", c.shape, FP32, kind="ExternalInput").ap()
    out = nc.dram_tensor("out", (BATCH, SEQ, D), FP32, kind="ExternalOutput").ap()
    arrays["bucket_onehots"] = bucket_onehots().astype(np.float32)
    onehots = nc.dram_tensor("bucket_onehots", arrays["bucket_onehots"].shape, FP32, kind="ExternalInput").ap()
    program(nc, dram, consts, onehots, out)
    r = run_bass_kernel_spmd(nc, [arrays], core_ids=[0])
    return r.results[0]["out"]
```

```python
from contextlib import ExitStack

import numpy as np

import concourse.bass as bass
from concourse import mybir

FP32 = mybir.dt.float32
BF16 = mybir.dt.bfloat16
I32 = mybir.dt.int32
U32 = mybir.dt.uint32
ALU = mybir.AluOpType
ACT = mybir.ActivationFunctionType
AX = mybir.AxisListType

P = 128
BATCH, SEQ, D = 16, 256, 128
TOKENS = BATCH * SEQ
TILES = TOKENS // P
EPS = 1e-5
E, F = 8, 512
FC = F // P
BLOCKS = TOKENS // P + E
SLOTS = BLOCKS * P
W1_AT, W2_AT, B1_AT, B2_AT = 0, F, F + FC * D, F + FC * D + FC
EXPERT_COLS = B2_AT + D


class Mem:

    whole = None
    sems = {}

    def __init__(self, nc, stack, prefix):
        self.nc, self.stack, self.prefix = nc, stack, prefix

    def sb(self, name, shape, dt=FP32):
        return self.stack.enter_context(self.nc.sbuf_tensor(f"{self.prefix}_{name}", shape, dt))

    def sem(self, name, own=False):
        key = f"{self.prefix if own else self.prefix.strip('01')}_{name}"
        if key not in Mem.sems:
            Mem.sems[key] = Mem.whole.enter_context(self.nc.semaphore(key))
        return Mem.sems[key]

    def banks(self, n):
        return [self.stack.enter_context(self.nc.psum_tensor(f"{self.prefix}_bank{i}", [P, 512], FP32)) for i in range(n)]


def clear_semaphores(nc, handles):
    with nc.Block() as block:
        for n, engine in enumerate((block.sync, block.gpsimd, block.scalar, block.vector)):
            @engine
            def _(eng, n=n):
                for handle in handles[n::4]:
                    eng.sem_clear(handle)


class TransposedNorm:

    GT = 8
    GROUPS = TILES // GT

    def __init__(self, nc, stack, X, XN, XT, ident):
        m = Mem(nc, stack, "norm")
        self.X, self.XN, self.XT, self.ident = X, XN, XT, ident
        self.stats = m.sb("stats", [P, TILES, 6])
        self.mv = m.sb("mean_var", [P, TILES, 2])
        self.std = m.sb("std", [P, TILES])
        self.rstd = m.sb("rstd", [P, TILES])
        self.s_stats, self.s_mv, self.s_vareps, self.s_std, self.s_rstd, self.s_xn, self.s_xt_ps, self.s_xt = (
            m.sem(n) for n in ("stats", "mv", "vareps", "std", "rstd", "xn", "xt_ps", "xt"))
        self.s_logit_ps, self.s_logit = m.sem("logit_ps"), m.sem("logit")
        self.use, self.routed, self.bank, self.logit_bank, self.switch = -1, 0, None, None, None

    def begin(self, bank, switch=None):
        self.use += 1
        self.bank, self.switch = bank[0:2], switch
        if switch:
            self.logit_bank = bank[2]
            self.routed += 1

    def vector(self, dve, g):
        tiles, groups = self.use * TILES, self.use * self.GROUPS
        if g < self.GROUPS:
            own = range(g * self.GT, (g + 1) * self.GT)
            cols = slice(own.start, own.stop)
            for t in own:
                dve.bn_stats(self.stats[:, t, :], self.X[:, t, :]).then_inc(self.s_stats, 1)
            for t in own:
                dve.wait_ge(self.s_stats, tiles + t + 1)
                dve.bn_aggr(self.mv[:, t, :], self.stats[:, t, :]).then_inc(self.s_mv, 1)
            dve.wait_ge(self.s_mv, tiles + own.stop)
            dve.tensor_scalar(self.std[:, cols], self.mv[:, cols, 1], EPS, None, ALU.add).then_inc(self.s_vareps, 1)
        if g > 0:
            own = range((g - 1) * self.GT, g * self.GT)
            cols = slice(own.start, own.stop)
            dve.wait_ge(self.s_std, groups + g)
            dve.reciprocal(self.rstd[:, cols], self.std[:, cols]).then_inc(self.s_rstd, 1)
            dve.wait_ge(self.s_rstd, groups + g)
            for t in own:
                dve.tensor_scalar(self.XN[:, t, :], self.X[:, t, :], self.mv[:, t, 0:1], self.rstd[:, t:t + 1],
                                  ALU.subtract, ALU.mult).then_inc(self.s_xn, 1)

    def tensor(self, pe, g):
        tiles, banks = self.use * TILES, self.use * TILES // 4
        for half in range(2 if g < self.GROUPS else 0):
            if g > 0:
                pe.wait_ge(self.s_xt, banks + 2 * (g - 1) + half + 1)
            for j in range(4):
                t = g * self.GT + half * 4 + j
                pe.wait_ge(self.s_xn, tiles + t + 1)
                last = pe.transpose(self.bank[half][:, j * P:(j + 1) * P], self.XN[:, t, :], self.ident)
            last.then_inc(self.s_xt_ps, 1)
        if self.switch and g > 0:
            pe.wait_ge(self.s_xt, banks + 2 * g)
            for t in range((g - 1) * self.GT, g * self.GT):
                last = pe.matmul(self.logit_bank[:, t * E:(t + 1) * E], self.XT[:, t * P:(t + 1) * P], self.switch[0], start=True, stop=True)
            if g == self.GROUPS:
                last.then_inc(self.s_logit_ps, 1)

    def scalar(self, act, g):
        groups, banks = self.use * self.GROUPS, self.use * TILES // 4
        if g < self.GROUPS:
            cols = slice(g * self.GT, (g + 1) * self.GT)
            act.wait_ge(self.s_vareps, groups + g + 1)
            act.activation(self.std[:, cols], self.std[:, cols], ACT.Sqrt).then_inc(self.s_std, 1)
        if g > 0:
            for n in range(2 * (g - 1), 2 * g):
                act.wait_ge(self.s_xt_ps, banks + n + 1)
                act.activation(self.XT[:, n * 512:(n + 1) * 512], self.bank[n % 2][:, :], ACT.Copy).then_inc(self.s_xt, 1)
        if self.switch and g == self.GROUPS:
            act.wait_ge(self.s_logit_ps, self.routed)
            act.activation(self.switch[1], self.logit_bank[:, 0:TILES * E].rearrange("p (t e) -> p t e", e=E), ACT.Copy).then_inc(self.s_logit, 1)


def experts_layer(nc, prefix, X, norm, con, L, sbias, w, slots_in, slots_out, s_cleared, finish):
    with ExitStack() as stack:
        m = Mem(nc, stack, prefix)
        prob = m.sb("prob", [P, TILES])
        slot = m.sb("slot", [P, TILES], U32)
        bexp = m.sb("block_expert", [P, BLOCKS], I32)
        WA = m.sb("weights", [P, E, EXPERT_COLS])
        s_weights = m.sem("weights")
        route_tokens(nc, prefix + "r", norm, con, L, sbias, w, WA, s_weights, prob, slot, bexp)
        run_experts(nc, prefix + "e", X, norm, con, WA, s_weights, prob, slot, bexp, slots_in, slots_out, s_cleared, finish)


def route_tokens(nc, prefix, norm, con, L, sbias, w, WA, s_weights, prob, slot, bexp):
    with ExitStack() as stack:
        m = Mem(nc, stack, prefix)
        PAD = 16
        mx = m.sb("max", [P, TILES])
        ex = m.sb("exp", [P, TILES, E])
        es = m.sb("expsum", [P, TILES])
        cand = m.sb("cand", [P, TILES, E])
        ridx = m.sb("route", [P, TILES])
        hot = m.sb("onehot", [P, TILES, E])
        cnt = [m.sb(f"count{i}", [P, PAD + TILES, E]) for i in range(2)]
        cfirst = m.sb("counts", [P, TILES, E])
        nblk_i = m.sb("nblocks_i", [P, E], I32)
        pre = [m.sb(f"blockprefix{i}", [P, 4 + E]) for i in range(2)]
        pos = m.sb("pos", [P, TILES, E])
        offs = m.sb("offs", [P, E])
        slotf = m.sb("slotf", [P, TILES])
        ge = m.sb("ge", [P, BLOCKS, E])
        bexpf = m.sb("bexpf", [P, BLOCKS])
        bank = m.banks(2)
        s_d, s_exp, s_hot, s_rank, s_v = (m.sem(n) for n in ("d", "exp", "hot", "rank", "v"))
        block = stack.enter_context(nc.Block())
        psr, psc = (bank[i][:, 0:TILES * E].rearrange("p (t e) -> p t e", e=E) for i in range(2))

        @block.sync
        def _(sp):
            sp.dma_start(WA[:, :, W1_AT:W2_AT], w["w1"].rearrange("e d f -> d e f")).then_inc(s_weights, 16)
            sp.dma_start(WA[:, :, W2_AT:B1_AT], w["w2"].rearrange("e (p c) d -> p e (c d)", c=FC)).then_inc(s_weights, 16)
            sp.dma_start(WA[:, :, B1_AT:B2_AT], w["b1"].rearrange("e (p c) -> p e c", c=FC)).then_inc(s_weights, 16)
            sp.dma_start(WA[:, :, B2_AT:], w["b2"].partition_broadcast(P)).then_inc(s_weights, 16)

        @block.tensor
        def _(pe):
            pe.wait_ge(s_hot, 1)
            pe.matmul(bank[0][:, 0:TILES * E], con["below"], hot[:, :, :].rearrange("p t e -> p (t e)"), start=True, stop=True)
            pe.matmul(bank[1][:, 0:TILES * E], con["ones"], hot[:, :, :].rearrange("p t e -> p (t e)"), start=True, stop=True).then_inc(s_rank, 1)

        @block.scalar
        def _(act):
            act.wait_ge(s_d, 1)
            act.activation(ex[:, :, :], L[:, :, :], ACT.Exp).then_inc(s_exp, 1)

        @block.vector
        def _(dve):
            done = [0]

            def then(ins):
                done[0] += 1
                ins.then_inc(s_v, 1)
                dve.wait_ge(s_v, done[0])

            TE = [P, TILES, E]
            dve.wait_ge(norm.s_logit, norm.routed)
            then(dve.tensor_tensor(L[:, :, :], L[:, :, :], sbias[:, :].unsqueeze(1).to_broadcast(TE), ALU.add))
            then(dve.tensor_reduce(mx[:, :], L[:, :, :], AX.X, ALU.max))
            dve.tensor_tensor(L[:, :, :], L[:, :, :], mx[:, :].unsqueeze(2).to_broadcast(TE), ALU.subtract).then_inc(s_d, 1)
            dve.wait_ge(s_d, 1)
            then(dve.tensor_scalar(cand[:, :, :], L[:, :, :], 0.0, float(E), ALU.is_lt, ALU.mult))
            then(dve.tensor_tensor(cand[:, :, :], cand[:, :, :], con["iota_e"].unsqueeze(1).to_broadcast(TE), ALU.add))
            then(dve.tensor_reduce(ridx[:, :], cand[:, :, :], AX.X, ALU.min))
            dve.tensor_tensor(hot[:, :, :], con["iota_e"].unsqueeze(1).to_broadcast(TE),
                              ridx[:, :].unsqueeze(2).to_broadcast(TE), ALU.is_equal).then_inc(s_hot, 1)
            dve.wait_ge(s_exp, 1)
            then(dve.tensor_reduce(es[:, :], ex[:, :, :], AX.X, ALU.add))
            dve.reciprocal(prob[:, :], es[:, :])
            dve.memset(cnt[0][:, 0:PAD, :], 0.0)
            dve.memset(cnt[1][:, 0:PAD, :], 0.0)
            dve.memset(pre[0][:, 0:4], 0.0)
            then(dve.memset(pre[1][:, 0:4], 0.0))
            dve.wait_ge(s_rank, 1)
            then(dve.tensor_copy(cfirst[:, :, :], psc))
            then(dve.tensor_copy(cnt[0][:, PAD:, :], cfirst[:, :, :]))
            for k in range(5):
                a, b = cnt[k % 2], cnt[(k + 1) % 2]
                then(dve.tensor_tensor(b[:, PAD:, :], a[:, PAD:, :], a[:, PAD - (1 << k):PAD + TILES - (1 << k), :], ALU.add))
            tot = cnt[1]
            then(dve.tensor_scalar(nblk_i[:, :], tot[:, PAD + TILES - 1, :], float(P - 1), None, ALU.add))
            then(dve.tensor_scalar(nblk_i[:, :], nblk_i[:, :], 7, None, ALU.arith_shift_right))
            then(dve.tensor_copy(pre[0][:, 4:], nblk_i[:, :]))
            for k in range(3):
                a, b = pre[k % 2], pre[(k + 1) % 2]
                then(dve.tensor_tensor(b[:, 4:], a[:, 4:], a[:, 4 - (1 << k):4 + E - (1 << k)], ALU.add))
            bend = pre[1]
            then(dve.tensor_scalar(offs[:, :], bend[:, 3:3 + E], float(P), None, ALU.mult))
            then(dve.tensor_tensor(pos[:, :, :], tot[:, PAD:, :], cfirst[:, :, :], ALU.subtract))
            then(dve.tensor_tensor(pos[:, :, :], psr, pos[:, :, :], ALU.add))
            then(dve.tensor_tensor(pos[:, :, :], pos[:, :, :], offs[:, :].unsqueeze(1).to_broadcast(TE), ALU.add))
            then(dve.tensor_tensor(pos[:, :, :], pos[:, :, :], hot[:, :, :], ALU.mult))
            then(dve.tensor_reduce(slotf[:, :], pos[:, :, :], AX.X, ALU.add))
            then(dve.tensor_copy(slot[:, :], slotf[:, :]))
            BE = [P, BLOCKS, E]
            then(dve.tensor_tensor(ge[:, :, :], con["iota_b"].unsqueeze(2).to_broadcast(BE),
                                   bend[:, 4:].unsqueeze(1).to_broadcast(BE), ALU.is_ge))
            then(dve.tensor_reduce(bexpf[:, :], ge[:, :, :], AX.X, ALU.add))
            then(dve.tensor_scalar(bexp[:, :], bexpf[:, :], float(E - 1), None, ALU.min))


def run_experts(nc, prefix, X, norm, con, WA, s_weights, prob, slot, bexp, slots_in, slots_out, s_cleared, finish):
    with ExitStack() as stack:
        m = Mem(nc, stack, prefix)
        UNROLL = 4
        WB = [m.sb(f"expert_{i}", [P, EXPERT_COLS]) for i in range(UNROLL)]
        xb = [m.sb(f"xb_{i}", [P, D]) for i in range(UNROLL)]
        xbt = [m.sb(f"xbt_{i}", [P, P]) for i in range(2)]
        h = [m.sb(f"h_{i}", [P, FC, P]) for i in range(2)]
        y = [m.sb(f"y_{i}", [P, D]) for i in range(UNROLL)]
        G = m.sb("gathered", [P, TILES, D])
        bank = m.banks(8)
        px, ph, py = bank[0:2], bank[2:4], bank[4:6]
        if finish is None:
            norm.begin(bank[6:8])
        s_fin, s_stored = m.sem("finished"), m.sem("stored")
        s_wb, s_xt, s_xtc, s_h, s_g, s_yp, s_y = (m.sem(n) for n in ("wb", "xt", "xtc", "h", "gelu", "yp", "y"))
        s_scat = m.sem("scattered", own=True)
        GQ = norm.GT
        s_gath = [m.sem(f"gathered{q}", own=True) for q in range(TILES // GQ)]
        s_x = [m.sem(f"x{i}") for i in range(UNROLL)]
        s_out = [m.sem(f"out{i}") for i in range(UNROLL)]
        GROUPS = BLOCKS // UNROLL
        block = stack.enter_context(nc.Block())

        def over_blocks(engine, step):
            for i in range(UNROLL):
                step(0, i)
            with engine.Fori(1, GROUPS - 1) as g:
                for i in range(UNROLL):
                    step(g, i)
            for i in range(UNROLL):
                step(GROUPS - 1, i)

        def wait_over(engine, semaphore, count):
            if not isinstance(count, int) or count > 0:
                engine.wait_ge(semaphore, count)

        @block.gpsimd
        def _(pool):
            pool.wait_ge(s_cleared, 16)
            for t in range(TILES):
                pool.indirect_dma_start(slots_in, bass.IndirectOffsetOnAxis(ap=slot[:, t:t + 1], axis=0),
                                        norm.XN[:, t, :], None).then_inc(s_scat, 16)
            for i in range(UNROLL):
                pool.wait_ge(s_out[i], 16 * GROUPS)
            for t in range(TILES):
                pool.indirect_dma_start(G[:, t, :], None, slots_out,
                                        bass.IndirectOffsetOnAxis(ap=slot[:, t:t + 1], axis=0)).then_inc(s_gath[t // GQ], 16)

        @block.sync
        def _(sp):
            sp.wait_ge(s_scat, 16 * TILES)

            def rows(g, i):
                wait_over(sp, s_xt, UNROLL * (g - 1) + i + 1)
                sp.dma_start(xb[i][:, :], slots_in[bass.ds((UNROLL * g + i) * P, P), :]).then_inc(s_x[i], 16)

            def store(g, i):
                sp.wait_ge(s_y, UNROLL * g + i + 1)
                sp.dma_start(slots_out[bass.ds((UNROLL * g + i) * P, P), :], y[i][:, :]).then_inc(s_out[i], 16)

            def step(g, i):
                rows(g, i)
                if not isinstance(g, int) or g > 0:
                    store(g - 1, i)

            over_blocks(sp, step)
            for i in range(UNROLL):
                store(GROUPS - 1, i)
            if finish is not None:
                for q in range(TILES // GQ):
                    sp.wait_ge(s_fin, GQ * (q + 1))
                    sp.dma_start(finish[:, q * GQ:(q + 1) * GQ, :], X[:, q * GQ:(q + 1) * GQ, :]).then_inc(s_stored, 16)
                sp.wait_ge(s_stored, 16 * (TILES // GQ))

        @block.tensor
        def _(pe):
            def transposed(g, i):
                k = UNROLL * g + i
                pe.wait_ge(s_x[i], 16 * (g + 1))
                wait_over(pe, s_xtc, k - 1)
                pe.transpose(px[i % 2][:, 0:P], xb[i][:, :], con["ident"]).then_inc(s_xt, 1)

            def up(g, i):
                k = UNROLL * g + i
                pe.wait_ge(s_wb, k + 1)
                pe.wait_ge(s_xtc, k + 1)
                wait_over(pe, s_g, FC * (k - 1))
                for c in range(FC):
                    last = pe.matmul(ph[i % 2][:, c * P:(c + 1) * P], WB[i][:, W1_AT + c:W2_AT:FC], xbt[i % 2][:, :], start=True, stop=True)
                last.then_inc(s_h, 1)

            def down(g, i):
                k = UNROLL * g + i
                wait_over(pe, s_y, k - 1)
                for c in range(FC):
                    pe.wait_ge(s_g, FC * k + c + 1)
                    last = pe.matmul(py[i % 2][:, 0:D], h[i % 2][:, c, :], WB[i][:, W2_AT + c * D:W2_AT + (c + 1) * D], start=(c == 0), stop=(c == FC - 1))
                last.then_inc(s_yp, 1)

            def step(g, i):
                up(g, i)
                if i < UNROLL - 1:
                    transposed(g, i + 1)
                elif not isinstance(g, int) or g < GROUPS - 1:
                    transposed(g + 1, 0)
                if i > 0:
                    down(g, i - 1)
                elif not isinstance(g, int) or g > 0:
                    down(g - 1, UNROLL - 1)

            transposed(0, 0)
            over_blocks(pe, step)
            down(GROUPS - 1, UNROLL - 1)
            if finish is None:
                for q in range(norm.GROUPS):
                    norm.tensor(pe, q)

        @block.scalar
        def _(act):
            def gelu(g, i):
                k = UNROLL * g + i
                act.wait_ge(s_h, k + 1)
                wait_over(act, s_yp, k - 1)
                for c in range(FC):
                    act.activation(h[i % 2][:, c, :], ph[i % 2][:, c * P:(c + 1) * P], ACT.Gelu_apprx_tanh,
                                   bias=WB[i][:, B1_AT + c:B1_AT + c + 1]).then_inc(s_g, 1)

            over_blocks(act, gelu)
            if finish is None:
                for q in range(norm.GROUPS + 1):
                    norm.scalar(act, q)

        @block.vector
        def _(dve):
            def expert(g, i):
                e = dve.value_load(bexp[0:1, bass.ds(UNROLL * g + i, 1)], min_val=0, max_val=E - 1)
                wait_over(dve, s_y, UNROLL * (g - 1) + i + 1)
                dve.tensor_copy(WB[i][:, :], WA[:, bass.ds(e, 1), :].rearrange("p a n -> p (a n)")).then_inc(s_wb, 1)

            def rows(g, i):
                k = UNROLL * g + i
                dve.wait_ge(s_xt, k + 1)
                wait_over(dve, s_h, k - 1)
                dve.tensor_copy(xbt[i % 2][:, :], px[i % 2][:, 0:P]).then_inc(s_xtc, 1)

            def result(g, i):
                dve.wait_ge(s_yp, UNROLL * g + i + 1)
                wait_over(dve, s_out[i], 16 * g)
                dve.tensor_tensor(y[i][:, :], py[i % 2][:, 0:D], WB[i][:, B2_AT:], ALU.add).then_inc(s_y, 1)

            def step(g, i):
                more = not isinstance(g, int) or g < GROUPS - 1
                if i < UNROLL - 2 or more:
                    expert(g + (i + 2) // UNROLL, (i + 2) % UNROLL)
                if i < UNROLL - 1 or more:
                    rows(g + (i + 1) // UNROLL, (i + 1) % UNROLL)
                if i > 0:
                    result(g, i - 1)
                elif not isinstance(g, int) or g > 0:
                    result(g - 1, UNROLL - 1)

            dve.wait_ge(s_weights, 64)
            expert(0, 0)
            expert(0, 1)
            rows(0, 0)
            over_blocks(dve, step)
            result(GROUPS - 1, UNROLL - 1)
            for t in range(TILES):
                if t % GQ == 0:
                    dve.wait_ge(s_gath[t // GQ], 16 * GQ)
                dve.scalar_tensor_tensor(X[:, t, :], G[:, t, :], prob[:, t:t + 1], X[:, t, :], ALU.mult, ALU.add).then_inc(s_fin, 1)
                if finish is None and t % GQ == GQ - 1:
                    dve.wait_ge(s_fin, t + 1)
                    norm.vector(dve, t // GQ)
            if finish is None:
                norm.vector(dve, norm.GROUPS)


HA, DA = 8, D // 8
ATTN_EPS = 1e-6


def linear_attention_layer(nc, prefix, X, norm, con, w, switch):
    with ExitStack() as stack:
        m = Mem(nc, stack, prefix)
        M2 = m.sb("msg", [P, TILES, D])
        ML = m.sb("mlp", [P, TILES, D])
        gain = m.sb("gain", [P, 2, D])
        stats = m.sb("stats", [P, 2, TILES, 6])
        linear_attention(nc, prefix + "l", con, w, norm.XT, X, norm.XN, M2, ML, gain, stats)
        add_normalised(nc, prefix + "a", X, norm, M2, ML, gain, stats, switch)


def linear_attention(nc, prefix, con, w, XT, X, XN, M2, ML, gain, stats):
    with ExitStack() as stack:
        m = Mem(nc, stack, prefix)
        Wq, Wm = m.sb("wq", [P, D]), m.sb("wm", [P, D])
        W1, W2 = m.sb("w1", [P, 2 * D]), m.sb("w2", [P, 2, D])
        bias = m.sb("bias", [P, 2, D])
        xt = m.sb("xt", [P, SEQ])
        q = m.sb("q", [P, 2, D + 1])
        neg = m.sb("neg", [P, 2, D])
        feat = m.sb("feat", [P, 2, D])
        featT = m.sb("featT", [P, SEQ])
        kv = m.sb("kv", [P, D + HA])
        den = m.sb("den", [P, 2, HA])
        msg = m.sb("msg", [P, 2, D])
        msgT = m.sb("msgT", [P, SEQ])
        m2T = m.sb("m2T", [P, SEQ])
        h1 = m.sb("h1", [P, 2, SEQ])
        bank = m.banks(8)
        (s_w, s_gb, s_one, s_x, s_xt, s_q, s_qc, s_neg, s_exp, s_feat, s_kv, s_ft, s_kvm, s_ftc, s_un, s_den, s_rec, s_msg,
         s_mt, s_mtc, s_m2, s_m2t, s_m2c, s_h, s_relu, s_ml, s_mlc, s_m2s) = (m.sem(n) for n in (
             "w", "gb", "one", "x", "xtc", "q", "qc", "neg", "exp", "feat", "kvp", "ft", "kvm", "ftc", "un", "denom", "rec", "msgs",
             "mt", "mtc", "m2", "m2t", "m2c", "h", "relu", "ml", "mlc", "m2s"))
        block = stack.enter_context(nc.Block())
        pq, pkv, pft, pun, pmt, pm2t, ph, pml = bank
        pq3, un, m23, ml3 = (p[:, 0:n].rearrange("p (u d) -> p u d", u=2) for p, n in (
            (pq, SEQ), (pun, 2 * (D + HA)), (pmt[:, SEQ:], SEQ), (pml, SEQ)))

        def over_steps(engine, step):
            step(0, (0,))
            step(1, (0, 1))
            with engine.Fori(2, BATCH - 1) as n:
                step(n, (0, 1, 2))
            step(BATCH - 1, (0, 1, 2))
            step(BATCH, (1, 2))
            step(BATCH + 1, (2,))

        def wait_over(engine, semaphore, count):
            if not isinstance(count, int) or count > 0:
                engine.wait_ge(semaphore, count)

        @block.sync
        def _(sp):
            sp.dma_start(Wq[:, :], w["Wq"]).then_inc(s_w, 16)
            sp.dma_start(Wm[:, :], w["Wm"]).then_inc(s_w, 16)
            sp.dma_start(W1[:, :], w["W1"]).then_inc(s_w, 16)
            sp.dma_start(W2[:, :, :], w["W2"].rearrange("(c p) d -> p c d", p=P)).then_inc(s_w, 16)
            for j in range(2):
                sp.dma_start(gain[:, j, :], w[f"g{j + 1}"].partition_broadcast(P)).then_inc(s_gb, 16)
                sp.dma_start(bias[:, j, :], w[f"b{j + 1}"].partition_broadcast(P)).then_inc(s_gb, 16)

        @block.gpsimd
        def _(pool):
            pool.wait_ge(s_gb, 64)
            pool.tensor_tensor(X[:, :, :], X[:, :, :], XN[:, :, :], ALU.add).then_inc(s_x, 1)
            for j in range(2):
                pool.wait_ge(s_x, j + 1)
                pool.tensor_tensor(X[:, :, :], X[:, :, :], bias[:, j, :].unsqueeze(1).to_broadcast([P, TILES, D]), ALU.add).then_inc(s_x, 1)

        @block.tensor
        def _(pe):
            def step(n, stages):
                if 0 in stages:
                    pe.wait_ge(s_xt, n + 1)
                    wait_over(pe, s_feat, n)
                    for u in range(2):
                        last = pe.matmul(pq[:, u * D:(u + 1) * D], xt[:, u * P:(u + 1) * P], Wq[:, :], start=True, stop=True)
                    last.then_inc(s_q, 1)
                if 1 in stages:
                    pe.wait_ge(s_kvm, n)
                    pe.wait_ge(s_ftc, n)
                    for u in range(2):
                        last = pe.matmul(pun[:, u * (D + HA):(u + 1) * (D + HA)], featT[:, u * P:(u + 1) * P], kv[:, :], start=True, stop=True)
                    last.then_inc(s_un, 1)
                if 2 in stages:
                    pe.wait_ge(s_m2c, n - 1)
                    for c in range(2):
                        last = pe.matmul(ph[:, c * SEQ:(c + 1) * SEQ], W1[:, c * P:(c + 1) * P], m2T[:, :], start=True, stop=True)
                    last.then_inc(s_h, 1)
                    for u in range(2):
                        last = pe.matmul(pmt[:, SEQ + u * D:SEQ + (u + 1) * D], msgT[:, u * P:(u + 1) * P], Wm[:, :], start=True, stop=True)
                    last.then_inc(s_m2, 1)
                if 0 in stages:
                    pe.wait_ge(s_qc, n + 1)
                    pe.wait_ge(s_feat, n + 1)
                    for u in range(2):
                        last = pe.matmul(pkv[:, 0:D + 1], feat[:, u, :], q[:, u, :], start=(u == 0), stop=(u == 1))
                    last.then_inc(s_kv, 1)
                    for u in range(2):
                        last = pe.transpose(pft[:, u * P:(u + 1) * P], feat[:, u, :], con["ident"])
                    last.then_inc(s_ft, 1)
                if 1 in stages:
                    pe.wait_ge(s_msg, n)
                    wait_over(pe, s_m2s, n - 1)
                    for u in range(2):
                        last = pe.transpose(pmt[:, u * P:(u + 1) * P], msg[:, u, :], con["ident"])
                    last.then_inc(s_mt, 1)
                if 2 in stages:
                    pe.wait_ge(s_relu, n - 1)
                    wait_over(pe, s_mlc, n - 2)
                    for u in range(2):
                        for c in range(2):
                            last = pe.matmul(pml[:, u * D:(u + 1) * D], h1[:, c, u * P:(u + 1) * P], W2[:, c, :], start=(c == 0), stop=(c == 1))
                    last.then_inc(s_ml, 1)
                if 1 in stages:
                    pe.wait_ge(s_mtc, n)
                    pe.matmul(pm2t[:, 0:SEQ], Wm[:, :], msgT[:, :], start=True, stop=True).then_inc(s_m2t, 1)

            pe.wait_ge(s_w, 64)
            over_steps(pe, step)

        @block.scalar
        def _(act):
            def step(n, stages):
                if 2 in stages:
                    act.wait_ge(s_m2t, n - 1)
                    act.activation(m2T[:, :], pm2t[:, 0:SEQ], ACT.Copy).then_inc(s_m2c, 1)
                if 0 in stages:
                    act.wait_ge(s_neg, n + 1)
                    act.activation(neg[:, :, :], neg[:, :, :], ACT.Exp).then_inc(s_exp, 1)
                if 2 in stages:
                    act.wait_ge(s_m2, n - 1)
                    act.activation(M2[:, bass.ds(2 * (n - 2), 2), :], m23, ACT.Copy).then_inc(s_m2s, 1)
                if 0 in stages:
                    act.wait_ge(s_ft, n + 1)
                    act.activation(featT[:, :], pft[:, 0:SEQ], ACT.Copy).then_inc(s_ftc, 1)
                if 1 in stages:
                    act.wait_ge(s_mt, n)
                    act.activation(msgT[:, :], pmt[:, 0:SEQ], ACT.Copy).then_inc(s_mtc, 1)

            over_steps(act, step)

        @block.vector
        def _(dve):
            def step(n, stages):
                if 0 in stages:
                    dve.wait_ge(s_q, n + 1)
                    wait_over(dve, s_feat, n)
                    dve.tensor_scalar(neg[:, :, :], pq3, 0.0, None, ALU.min).then_inc(s_neg, 1)
                    wait_over(dve, s_kv, n)
                    dve.tensor_copy(q[:, :, 0:D], pq3).then_inc(s_qc, 1)
                if 1 in stages:
                    dve.wait_ge(s_un, n)
                    wait_over(dve, s_msg, n - 1)
                    dve.tensor_scalar(den[:, :, :], un[:, :, D:], ATTN_EPS, None, ALU.add).then_inc(s_den, 1)
                    dve.wait_ge(s_den, n)
                    dve.reciprocal(den[:, :, :], den[:, :, :]).then_inc(s_rec, 1)
                if 0 in stages:
                    dve.wait_ge(s_exp, n + 1)
                    wait_over(dve, s_ft, n)
                    dve.scalar_tensor_tensor(feat[:, :, :], pq3, 0.0, neg[:, :, :], ALU.max, ALU.add).then_inc(s_feat, 1)
                if 1 in stages:
                    dve.wait_ge(s_rec, n)
                    wait_over(dve, s_mt, n - 1)
                    for u in range(2):
                        last = dve.tensor_tensor(msg[:, u, :].rearrange("p (h v) -> p h v", h=HA), un[:, u, 0:D].rearrange("p (h v) -> p h v", h=HA),
                                                 den[:, u, :].unsqueeze(2).to_broadcast([P, HA, DA]), ALU.mult)
                    last.then_inc(s_msg, 1)
                if 2 in stages:
                    dve.wait_ge(s_h, n - 1)
                    dve.tensor_scalar(h1[:, :, :], ph[:, :].rearrange("p (c s) -> p c s", c=2), 0.0, None, ALU.max).then_inc(s_relu, 1)
                if 0 in stages:
                    if not (isinstance(n, int) and n == BATCH - 1):
                        dve.tensor_copy(xt[:, :], XT[:, bass.ds(n * SEQ + SEQ, SEQ)]).then_inc(s_xt, 1)
                    dve.wait_ge(s_kv, n + 1)
                    dve.tensor_tensor(kv[:, 0:D], pkv[:, 0:D], con["head_block"], ALU.mult)
                    dve.tensor_scalar(kv[:, D:D + HA], con["head_of"], pkv[:, D:D + 1], None, ALU.mult).then_inc(s_kvm, 1)
                if 2 in stages:
                    dve.wait_ge(s_m2s, n - 1)
                    for u in range(2):
                        dve.bn_stats(stats[:, 0, bass.ds(2 * (n - 2) + u, 1), :].rearrange("p a s -> p (a s)"),
                                     M2[:, bass.ds(2 * (n - 2) + u, 1), :].rearrange("p a d -> p (a d)"))
                    dve.wait_ge(s_ml, n - 1)
                    for u in range(2):
                        dve.bn_stats(stats[:, 1, bass.ds(2 * (n - 2) + u, 1), :].rearrange("p a s -> p (a s)"), ml3[:, u, :])
                    dve.tensor_copy(ML[:, bass.ds(2 * (n - 2), 2), :], ml3).then_inc(s_mlc, 1)

            dve.memset(q[:, :, D:D + 1], 1.0).then_inc(s_one, 1)
            dve.wait_ge(s_one, 1)
            dve.tensor_copy(xt[:, :], XT[:, 0:SEQ]).then_inc(s_xt, 1)
            over_steps(dve, step)


def add_normalised(nc, prefix, X, norm, M2, ML, gain, stats, switch):
    with ExitStack() as stack:
        m = Mem(nc, stack, prefix)
        mv = m.sb("mean_var", [P, 2, TILES, 2])
        std = m.sb("std", [P, 2 * TILES])
        rstd = m.sb("rstd", [P, 2 * TILES])
        shift = m.sb("shift", [P, 2 * TILES])
        s_mv, s_ve, s_std, s_rstd, s_neg, s_shift, s_norm, s_gain, s_x = (m.sem(n) for n in (
            "mv", "vareps", "std", "rstd", "neg", "shift", "norm", "gain", "x"))
        GT = norm.GT
        norm.begin(m.banks(3), switch)
        block = stack.enter_context(nc.Block())

        @block.scalar
        def _(act):
            act.wait_ge(s_ve, 1)
            act.activation(std[:, :], std[:, :], ACT.Sqrt).then_inc(s_std, 1)
            act.wait_ge(s_shift, 1)
            for g in range(norm.GROUPS + 2):
                if g < norm.GROUPS:
                    for t in range(GT * g, GT * (g + 1)):
                        for j, Y in enumerate((M2, ML)):
                            n = j * TILES + t
                            act.activation(Y[:, t, :], Y[:, t, :], ACT.Identity, bias=shift[:, n:n + 1], scale=rstd[:, n:n + 1]).then_inc(s_norm, 1)
                if g >= 1:
                    norm.scalar(act, g - 1)

        @block.tensor
        def _(pe):
            for g in range(norm.GROUPS + 1):
                norm.tensor(pe, g)

        @block.gpsimd
        def _(pool):
            for g in range(TILES // GT):
                pool.wait_ge(s_norm, 2 * GT * (g + 1))
                part = ML[:, GT * g:GT * (g + 1), :]
                pool.tensor_tensor(part, part, gain[:, 1, :].unsqueeze(1).to_broadcast([P, GT, D]), ALU.mult).then_inc(s_gain, 1)

        @block.vector
        def _(dve):
            for t in range(TILES):
                for j in range(2):
                    last = dve.bn_aggr(mv[:, j, t, :], stats[:, j, t, :])
            last.then_inc(s_mv, 1)
            dve.wait_ge(s_mv, 1)
            mean, var = (mv[:, :, :, i].rearrange("p j t -> p (j t)") for i in range(2))
            dve.tensor_scalar(std[:, :], var, EPS, None, ALU.add).then_inc(s_ve, 1)
            dve.tensor_scalar(shift[:, :], mean, -1.0, None, ALU.mult).then_inc(s_neg, 1)
            dve.wait_ge(s_std, 1)
            dve.reciprocal(rstd[:, :], std[:, :]).then_inc(s_rstd, 1)
            dve.wait_ge(s_rstd, 1)
            dve.wait_ge(s_neg, 1)
            dve.tensor_tensor(shift[:, :], shift[:, :], rstd[:, :], ALU.mult).then_inc(s_shift, 1)
            done = 0
            for g in range(TILES // GT):
                x, a, b = (Y[:, GT * g:GT * (g + 1), :] for Y in (X, M2, ML))
                dve.wait_ge(s_norm, 2 * GT * (g + 1))
                for part, what in ((a, None), (x, a)):
                    other = gain[:, 0, :].unsqueeze(1).to_broadcast([P, GT, D]) if what is None else what
                    dve.tensor_tensor(part, part, other, ALU.mult if what is None else ALU.add).then_inc(s_x, 1)
                    done += 1
                    dve.wait_ge(s_x, done)
                dve.wait_ge(s_gain, g + 1)
                dve.tensor_tensor(x, x, b, ALU.add).then_inc(s_x, 1)
                done += 1
                dve.wait_ge(s_x, done)
                norm.vector(dve, g)
            norm.vector(dve, norm.GROUPS)


HB, DB = 16, D // 16
NB16 = SEQ // 16
BUCKETS, MAX_REL = 32, 64
OFFS = 2 * SEQ
TABLE = OFFS - 16
VW = DB + 1
NEG_HUGE = -3.0e38
FAR = P


def disentangled_attention_layer(nc, prefix, X, norm, con, w, dram, switch):
    with ExitStack() as stack:
        m = Mem(nc, stack, prefix)
        V = m.sb("v", [P, TILES, HB, VW])
        Wo = m.sb("wo", [P, D])
        with ExitStack() as inner:
            mi = Mem(nc, inner, prefix)
            QT = [mi.sb(f"qt{i}", [P, TOKENS]) for i in range(2)]
            part = [mi.sb(f"part{i}", [P, 3, TOKENS], BF16) for i in range(2)]
            NBK = 2 * BUCKETS
            rel = {"R": mi.sb("rel", [NBK, D]), "gb": mi.sb("gb", [NBK, 2, D]), "Wp": mi.sb("wp", [P, 2, D]),
                   "bp": mi.sb("bp", [NBK, 2, D]), "onehot": mi.sb("onehot", [NBK, 2, OFFS])}
            s_rel, s_stored = mi.sem("rel"), mi.sem("stored")
            project_qkv(nc, prefix + "p", X, w, norm.XT, V, QT, part, rel, s_rel, s_stored, dram)
            position_tables(nc, prefix + "t", con, rel, s_rel, s_stored, dram)
        CTX = norm.XN
        attend(nc, prefix + "s", con, w, V, CTX, Wo, dram)
        return_context(nc, prefix + "o", X, norm, CTX, Wo, con, switch)


def project_qkv(nc, prefix, X, w, XT, V, QT, part, rel, s_rel, s_stored, dram):
    with ExitStack() as stack:
        m = Mem(nc, stack, prefix)
        W = m.sb("w", [P, 3, D])
        b_col = m.sb("b_col", [P, 2])
        bv = m.sb("bv", [P, D])
        bo = m.sb("bo", [P, D])
        s_bo, s_x = m.sem("bo"), m.sem("x")
        rest = [m.sb(f"rest{i}", [P, 512]) for i in range(3)]
        s_p1, s_rest, s_p2, s_p3 = m.sem("part1"), m.sem("rest"), m.sem("part2"), m.sem("part3")
        bank = m.banks(6)
        s_w, s_bs, s_q, s_qe, s_v, s_ve, s_one = (m.sem(n) for n in ("w", "bs", "q", "qe", "v", "ve", "one"))
        scale = (1.0 / np.sqrt(3.0 * DB), 1.0)
        G = TOKENS // 512
        block = stack.enter_context(nc.Block())

        @block.sync
        def _(sp):
            for j, n in enumerate(("Wq", "Wk", "Wv")):
                sp.dma_start(W[:, j, :], w[n]).then_inc(s_w, 16)
            for j, n in enumerate(("bq", "bk")):
                sp.dma_start(b_col[:, j:j + 1], w[n].rearrange("(p o) -> p o", o=1)).then_inc(s_w, 16)
            sp.dma_start(bv[:, :], w["bv"].partition_broadcast(P)).then_inc(s_w, 16)
            sp.dma_start(bo[:, :], w["bo"].partition_broadcast(P)).then_inc(s_bo, 16)
            sp.dma_start(rel["R"][:, :], w["rel_emb"]).then_inc(s_rel, 16)
            for j, n in enumerate(("ln_g", "ln_b")):
                sp.dma_start(rel["gb"][:, j, :], w[n].partition_broadcast(2 * BUCKETS)).then_inc(s_rel, 16)
            for j, n in enumerate(("k", "q")):
                sp.dma_start(rel["Wp"][:, j, :], w["Wp" + n]).then_inc(s_rel, 16)
                sp.dma_start(rel["bp"][:, j, :], w["bp" + n].partition_broadcast(2 * BUCKETS)).then_inc(s_rel, 16)
            sp.dma_start(rel["onehot"][:, :, :], dram["onehot"].rearrange("a (j x) -> a j x", j=2)).then_inc(s_rel, 16)
            for c in range(5):
                if c < 4:
                    cols = slice(c % 2 * TOKENS // 2, (c % 2 + 1) * TOKENS // 2)
                    sp.wait_ge(s_qe, G // 2 * (c + 1))
                    sp.dma_start(dram["qk"][c // 2][:, cols], QT[c // 2][:, cols]).then_inc(s_stored, 16)
                if c >= 1:
                    j, h = (c - 1) // 2, (c - 1) % 2
                    cols = slice(h * TOKENS // 2, (h + 1) * TOKENS // 2)
                    sp.wait_ge(s_p3, G // 2 * c)
                    sp.dma_start(dram["parts"][j].rearrange("i p n -> p i n")[:, :, cols], part[j][:, :, cols]).then_inc(s_stored, 16)

        @block.gpsimd
        def _(pool):
            pool.wait_ge(s_bo, 16)
            pool.tensor_tensor(X[:, :, :], X[:, :, :], bo[:, :].unsqueeze(1).to_broadcast([P, TILES, D]), ALU.add).then_inc(s_x, 1)

        @block.tensor
        def _(pe):
            pe.wait_ge(s_w, 96)
            for n in range(2 * G):
                j, g = n // G, n % G
                if n >= 4:
                    pe.wait_ge(s_p1, n - 3)
                pe.matmul(bank[n % 4][:, :], W[:, j, :], XT[:, g * 512:(g + 1) * 512], start=True, stop=True).then_inc(s_q, 1)
                if n < TILES // 4:
                    if n >= 2:
                        pe.wait_ge(s_ve, n - 1)
                    for t in range(4 * n, 4 * n + 4):
                        last = pe.matmul(bank[4 + n % 2][:, t % 4 * D:(t % 4 + 1) * D], XT[:, t * P:(t + 1) * P], W[:, 2, :], start=True, stop=True)
                    last.then_inc(s_v, 1)

        @block.scalar
        def _(act):
            act.wait_ge(s_bs, 1)
            for n in range(2 * G + 1):
                if n < 2 * G:
                    j, g = n // G, n % G
                    act.wait_ge(s_q, n + 1)
                    act.activation(QT[j][:, g * 512:(g + 1) * 512], bank[n % 4][:, :], ACT.Identity,
                                   bias=b_col[:, j:j + 1], scale=float(scale[j])).then_inc(s_qe, 1)
                    act.activation(part[j][:, 0, g * 512:(g + 1) * 512], bank[n % 4][:, :], ACT.Identity,
                                   bias=b_col[:, j:j + 1], scale=float(scale[j])).then_inc(s_p1, 1)
                if n >= 1:
                    j, g = (n - 1) // G, (n - 1) % G
                    act.wait_ge(s_rest, n)
                    act.activation(part[j][:, 1, g * 512:(g + 1) * 512], rest[(n - 1) % 3][:, :], ACT.Copy).then_inc(s_p2, 1)

        @block.vector
        def _(dve):
            dve.wait_ge(s_w, 96)
            dve.tensor_scalar(b_col[:, 0:1], b_col[:, 0:1], float(scale[0]), None, ALU.mult).then_inc(s_bs, 1)
            dve.memset(V[:, :, :, DB:], 1.0).then_inc(s_one, 1)
            for n in range(2 * G + 1):
                if n < 2 * G:
                    j, g = n // G, n % G
                    cols = slice(g * 512, (g + 1) * 512)
                    dve.wait_ge(s_p1, n + 1)
                    dve.wait_ge(s_qe, n + 1)
                    if n >= 3:
                        dve.wait_ge(s_p3, n - 2)
                    dve.tensor_tensor(rest[n % 3][:, :], QT[j][:, cols], part[j][:, 0, cols], ALU.subtract).then_inc(s_rest, 1)
                if n < TILES // 4:
                    dve.wait_ge(s_v, n + 1)
                    SHAPE = [P, 4, HB, DB]
                    dve.tensor_tensor(V[:, 4 * n:4 * n + 4, :, 0:DB], bank[4 + n % 2][:, :].rearrange("p (t h d) -> p t h d", t=4, h=HB),
                                      bv[:, :].rearrange("p (h d) -> p h d", h=HB).unsqueeze(1).to_broadcast(SHAPE), ALU.add).then_inc(s_ve, 1)
                if n >= 1:
                    j, g = (n - 1) // G, (n - 1) % G
                    cols = slice(g * 512, (g + 1) * 512)
                    dve.wait_ge(s_p2, n)
                    dve.tensor_tensor(part[j][:, 2, cols], rest[(n - 1) % 3][:, :], part[j][:, 1, cols], ALU.subtract).then_inc(s_p3, 1)


def position_tables(nc, prefix, con, rel, s_rel, s_stored, dram):
    with ExitStack() as stack:
        m = Mem(nc, stack, prefix)
        R, gb, Wp, bp, onehot = (rel[n] for n in ("R", "gb", "Wp", "bp", "onehot"))
        RT = m.sb("relt", [P, 2 * BUCKETS])
        PK = m.sb("pk", [2 * BUCKETS, 2, D])
        T = m.sb("tables", [P, 2, OFFS])
        stats, mv, std = m.sb("stats", [2 * BUCKETS, 6]), m.sb("mv", [2 * BUCKETS, 2]), m.sb("std", [2 * BUCKETS, 1])
        far = m.sb("far", [P, 2, 2, FAR])
        far_rest = m.sb("far_rest", [P, 2, 2, FAR])
        far_parts = m.sb("far_parts", [P, 2, 3, 2, FAR], BF16)
        bank = m.banks(4)
        s_v, s_std, s_ve, s_re, s_rt, s_rtc, s_pk, s_pkc, s_t, s_tc, s_far, s_out = (m.sem(n) for n in (
            "v", "std", "vareps", "re", "rt", "rtc", "pk", "pkc", "t", "tc", "far", "out"))
        scale = (np.sqrt(3.0 * DB) / np.sqrt(2.0 * DB), 1.0 / np.sqrt(2.0 * DB))
        NBK = 2 * BUCKETS
        block = stack.enter_context(nc.Block())

        @block.sync
        def _(sp):
            sp.wait_ge(s_tc, 1)
            sp.dma_start(dram["tables"].rearrange("j p x -> p j x"), T[:, :, :]).then_inc(s_out, 16)
            sp.wait_ge(s_far, 1)
            sp.dma_start(dram["far"].rearrange("j i p x -> p (j i) x"), far_parts[:, :, :, :, :].rearrange("p j i e x -> p (j i) (e x)")).then_inc(s_out, 16)
            sp.wait_ge(s_out, 32)
            sp.wait_ge(s_stored, 16 * 8)

        @block.scalar
        def _(act):
            act.wait_ge(s_ve, 1)
            act.activation(std[:, :], std[:, :], ACT.Sqrt).then_inc(s_std, 1)

        @block.vector
        def _(dve):
            done = [0]

            def then(ins):
                done[0] += 1
                ins.then_inc(s_v, 1)
                dve.wait_ge(s_v, done[0])

            dve.wait_ge(s_rel, 128)
            then(dve.bn_stats(stats[:, :], R[:, :]))
            then(dve.bn_aggr(mv[:, :], stats[:, :]))
            dve.tensor_scalar(std[:, :], mv[:, 1:2], EPS, None, ALU.add).then_inc(s_ve, 1)
            dve.wait_ge(s_std, 1)
            then(dve.reciprocal(std[:, :], std[:, :]))
            then(dve.tensor_scalar(R[:, :], R[:, :], mv[:, 0:1], std[:, :], ALU.subtract, ALU.mult))
            then(dve.tensor_tensor(R[:, :], R[:, :], gb[:, 0, :], ALU.mult))
            dve.tensor_tensor(R[:, :], R[:, :], gb[:, 1, :], ALU.add).then_inc(s_re, 1)
            dve.wait_ge(s_rt, 1)
            dve.tensor_copy(RT[:, :], bank[0][:, 0:NBK]).then_inc(s_rtc, 1)
            dve.wait_ge(s_pk, 1)
            then(dve.tensor_tensor(PK[:, :, :], bank[1][0:NBK, 0:2 * D].rearrange("p (j d) -> p j d", j=2), bp[:, :, :], ALU.add))
            for j in range(2):
                last = dve.tensor_scalar(PK[:, j, :], PK[:, j, :], float(scale[j]), None, ALU.mult)
            last.then_inc(s_pkc, 1)
            dve.wait_ge(s_t, 1)
            for j in range(2):
                last = dve.tensor_copy(T[:, j, :], bank[2 + j][:, :])
            last.then_inc(s_tc, 1)
            dve.wait_ge(s_tc, 1)
            for end in range(2):
                last = dve.tensor_copy(far[:, :, end, :], T[:, :, end * (OFFS - FAR):end * (OFFS - FAR) + FAR])
            then(last)
            then(dve.tensor_copy(far_parts[:, :, 0, :, :], far[:, :, :, :]))
            then(dve.tensor_tensor(far_rest[:, :, :, :], far[:, :, :, :], far_parts[:, :, 0, :, :], ALU.subtract))
            then(dve.tensor_copy(far_parts[:, :, 1, :, :], far_rest[:, :, :, :]))
            dve.tensor_tensor(far_parts[:, :, 2, :, :], far_rest[:, :, :, :], far_parts[:, :, 1, :, :], ALU.subtract).then_inc(s_far, 1)

        @block.tensor
        def _(pe):
            pe.wait_ge(s_re, 1)
            pe.transpose(bank[0][:, 0:NBK], R[:, :], con["ident"][0:NBK, 0:NBK]).then_inc(s_rt, 1)
            pe.wait_ge(s_rtc, 1)
            for j in range(2):
                last = pe.matmul(bank[1][0:NBK, j * D:(j + 1) * D], RT[:, :], Wp[:, j, :], start=True, stop=True)
            last.then_inc(s_pk, 1)
            pe.wait_ge(s_pkc, 1)
            for j in range(2):
                last = pe.matmul(bank[2 + j][:, :], PK[:, j, :], onehot[:, j, :], start=True, stop=True)
            last.then_inc(s_t, 1)


def stacked_views(dram):
    n, part = TOKENS, P * TOKENS
    tab, qk, parts, far = (dram[name].tensor for name in ("tables", "qk", "parts", "far"))
    fn, fpart = 2 * FAR, P * 2 * FAR
    return {
        "tables": [bass.AP(tensor=tab, offset=j * P * OFFS, ap=[[1, 16], [OFFS, P], [1, TABLE]]) for j in range(2)],
        "qk": [bass.AP(tensor=qk, offset=j * P * n, ap=[[0, 16], [n, P], [1, n]]) for j in range(2)],
        "q_parts": [bass.AP(tensor=parts, offset=i * part, ap=[[0, 3], [n, P], [1, n]]) for i in range(3)],
        "k_parts": bass.AP(tensor=parts, offset=3 * part, ap=[[part, 3], [n, P], [1, n]]),
        "far_e": bass.AP(tensor=far, offset=0, ap=[[fpart, 3], [fn, P], [1, fn]]),
        "far_f": [bass.AP(tensor=far, offset=(3 + i) * fpart, ap=[[0, 3], [fn, P], [1, fn]]) for i in range(3)],
    }


def attend(nc, prefix, con, w, V, CTX, Wo, dram):
    with ExitStack() as stack:
        m = Mem(nc, stack, prefix)
        s_wo = m.sem("wo")
        HALF = BATCH // 2
        HT = HALF * SEQ
        QR = [m.sb(f"qr{i}", [P, HT]) for i in range(2)]
        KR = [m.sb(f"kr{i}", [P, HT]) for i in range(2)]
        QS = [m.sb(f"qs{i}", [9 * DB, HT], BF16) for i in range(2)]
        KS = [m.sb(f"ks{i}", [9 * DB, HT], BF16) for i in range(2)]
        TAB = [m.sb(f"tab{i}", [P, 2, TABLE]) for i in range(2)]
        ENDS = [m.sb(f"ends{i}", [9 * DB, 2, 2 * FAR], BF16) for i in range(2)]
        CT = [m.sb(f"c2p_t{i}", [P, 2, HALF, SEQ]) for i in range(2)]
        PC = [m.sb(f"p2c{i}", [P, 2, HALF, SEQ]) for i in range(2)]
        NS = 4
        S = [m.sb(f"scores{i}", [P, 2, SEQ]) for i in range(NS)]
        PT = [m.sb(f"probs_t{i}", [P, 2, SEQ]) for i in range(2)]
        mx = m.sb("max", [P, 2 * HALF])
        VS = [m.sb(f"values{i}", [P, 2 * HALF, VW]) for i in range(2)]
        rec = [m.sb(f"rec{i}", [P, 2 * HALF]) for i in range(2)]
        bank = m.banks(8)
        pb, pt1, pqk, pt2, pav = bank[0:2], bank[2:4], bank[4:6], bank[6], bank[7]
        (s_masked, s_bm, s_be, s_t1, s_z, s_qk, s_sc, s_sub0, s_sub1, s_t2, s_exp, s_av, s_vs, s_rec, s_ctx,
         s_go_dve, s_go_pool, s_go_sp) = (m.sem(n) for n in (
             "masked", "bias_mm", "bias_copied", "t1", "z", "qk", "scores", "shifted0", "shifted1", "t2", "exp", "av", "values", "rec", "ctx",
             "go_dve", "go_pool", "go_sp"))
        s_q, s_tab, s_stack = ([m.sem(f"{n}{i}") for i in range(2)] for n in ("q", "tab", "stack"))
        QUADS = NB16 // 4
        assert (bucket(np.arange(SEQ // 4 + 1, SEQ)) >= BUCKETS - 1).all() and (bucket(-np.arange(SEQ // 4 + 1, SEQ)) <= -BUCKETS).all()
        FILLS = [(kind, quad, side) for kind in range(2) for quad in range(QUADS) for side in range(2)]
        is_far = lambda quad, side: (quad, side) in ((QUADS - 1, 0), (0, 1))
        FILLS.sort(key=lambda f: is_far(*f[1:]))
        BM = len(FILLS)
        views = stacked_views(dram)
        LAG = 3
        SHARE = [BM // HALF + (n == 1) - (n == HALF - 1) for n in range(HALF)]
        block = stack.enter_context(nc.Block())

        def over_heads(engine, head_body):
            head_body(0, False)
            with engine.Fori(1, HB - 1) as head:
                head_body(head, False)
            head_body(HB - 1, True)

        def following(head, half):
            return (head, 1) if half == 0 else (head + 1, 0)

        def steps_before(head, half, n, lag):
            if n >= lag:
                return head, half, n - lag
            if half == 1:
                return head, 0, n - lag + HALF
            return None if isinstance(head, int) and head == 0 else (head - 1, 1, n - lag + HALF)

        def number(head, half, b):
            return head * BATCH + (half * HALF + b)

        @block.sync
        def _(sp):
            def load_rows(head, half):
                rows, cols = bass.ds(head * DB, DB), slice(half * HT, (half + 1) * HT)
                for j in range(2):
                    sp.dma_start(TAB[half][:, j, :], views["tables"][j][:, rows, :]).then_inc(s_tab[half], 16)
                for j, R in enumerate((QR, KR)):
                    sp.dma_start(R[half][:, :], views["qk"][j][:, rows, cols]).then_inc(s_q[half], 16)

            def load_parts(head, half):
                rows, cols = bass.ds(head * DB, DB), slice(half * HT, (half + 1) * HT)
                for i in range(3):
                    three = slice(i * 3 * DB, (i + 1) * 3 * DB)
                    sp.dma_start(QS[half][three, :], views["q_parts"][i][:, rows, cols]).then_inc(s_stack[half], 16)
                    sp.dma_start(KS[half][three, :], views["k_parts"][:, rows, cols]).then_inc(s_stack[half], 16)
                    sp.dma_start(ENDS[half][three, 0, :], views["far_e"][:, rows, :]).then_inc(s_stack[half], 16)
                    sp.dma_start(ENDS[half][three, 1, :], views["far_f"][i][:, rows, :]).then_inc(s_stack[half], 16)

            def heads(head, last):
                for half in range(2):
                    u = 2 * head + half
                    if not last:
                        sp.wait_ge(s_bm, BM * (u + 1))
                        sp.sem_inc(s_go_sp, 1)
                        load_rows(head + 1, half)
                    if not (last and half == 1):
                        sp.wait_ge(s_sc, HALF * u + 2)
                        sp.sem_inc(s_go_sp, 1)
                        load_parts(*following(head, half))

            load_rows(0, 0)
            load_parts(0, 0)
            load_rows(0, 1)
            sp.dma_start(Wo[:, :], w["Wo"]).then_inc(s_wo, 16)
            over_heads(sp, heads)
            sp.wait_ge(s_wo, 16)

        @block.gpsimd
        def _(pool):
            def heads(head, last):
                for half in range(2):
                    for b in range(HALF):
                        pool.wait_ge(s_sc, head * BATCH + half * HALF + b + 3)
                        pool.sem_inc(s_go_pool, 1)
                        pool.tensor_scalar(S[b % NS][:, 1, :], S[b % NS][:, 1, :], mx[:, 2 * b + 1:2 * b + 2], None,
                                           ALU.subtract).then_inc(s_sub1, 1)

            over_heads(pool, heads)

        @block.tensor
        def _(pe):
            def fill(head, half, n):
                kind, quad, side = FILLS[n]
                f = (2 * head + half) * BM + n
                if n == 0:
                    pe.wait_ge(s_tab[half], 32 * (head + 1))
                pe.wait_ge(s_masked, 2 * (2 * head + half) + kind + 1)
                pe.wait_ge(s_be, f + 1)
                mov = (QR, KR)[kind][half]
                if is_far(quad, side):
                    pe.wait_ge(s_stack[half], 16 * 12 * (head + 1))
                    pe.matmul(pb[n % 2][:, :], ENDS[half][:, kind, side * FAR:(side + 1) * FAR],
                              (QS, KS)[kind][half][:, :].rearrange("p (b s) -> p b s", b=HALF)[:, :, quad * 64:(quad + 1) * 64],
                              start=True, stop=True).then_inc(s_bm, 1)
                    return
                for a in range(4):
                    grp = 4 * quad + a
                    c = TABLE - SEQ + P * side - 16 * grp
                    last = pe.matmul(pb[n % 2][:, a * P:(a + 1) * P], TAB[half][:, kind, c:c + P],
                                     mov[:, :].rearrange("p (b g s) -> p g b s", b=HALF, s=16)[:, grp, :, :],
                                     start=True, stop=True)
                last.then_inc(s_bm, 1)

            def t1(step, half, b):
                pe.wait_ge(s_z, step + 1)
                for st in range(2):
                    for kt in range(2):
                        last = pe.transpose(pt1[b % 2][:, st * SEQ + kt * P:st * SEQ + (kt + 1) * P],
                                            CT[half][:, kt, b, st * P:(st + 1) * P], con["ident"])
                last.then_inc(s_t1, 1)

            def qk(step, half, b):
                pe.wait_ge(s_sc, step + 1)
                for st in range(2):
                    last = pe.matmul(pqk[b % 2][:, st * SEQ:(st + 1) * SEQ], QS[half][:, b * SEQ + st * P:b * SEQ + (st + 1) * P],
                                     KS[half][:, b * SEQ:(b + 1) * SEQ], start=True, stop=True)
                last.then_inc(s_qk, 1)

            def t2(head, half, b):
                step = number(head, half, b)
                pe.wait_ge(s_sub0, step + 1)
                pe.wait_ge(s_sub1, step + 1)
                pe.wait_ge(s_exp, step + 1)
                for kt in range(2):
                    for st in range(2):
                        last = pe.transpose(pt2[:, kt * SEQ + st * P:kt * SEQ + (st + 1) * P],
                                            S[b % NS][:, st, kt * P:(kt + 1) * P], con["ident"])
                last.then_inc(s_t2, 1)

            def av(head, half, b):
                step = number(head, half, b)
                pe.wait_ge(s_exp, step + 2)
                if b == 0:
                    pe.wait_ge(s_vs, 2 * head + half + 1)
                for st in range(2):
                    t = 2 * b + st
                    for kt in range(2):
                        last = pe.matmul(pav[:, t * VW:(t + 1) * VW], PT[b % 2][:, kt, st * P:(st + 1) * P],
                                         V[:, 2 * (half * HALF + b) + kt, bass.ds(head, 1), :].rearrange("p a v -> p (a v)"),
                                         start=(kt == 0), stop=(kt == 1))
                last.then_inc(s_av, 1)

            def heads(head, last):
                for half in range(2):
                    u = 2 * head + half
                    pe.wait_ge(s_be, BM * (u + 1) + 2)
                    pe.wait_ge(s_stack[half], 16 * 12 * (head + 1))
                    done = 0
                    for n in range(HALF):
                        t1(HALF * u + n, half, n)
                        qk(HALF * u + n, half, n)
                        if before := steps_before(head, half, n, LAG):
                            t2(*before)
                        if not (last and half == 1):
                            for _ in range(SHARE[n]):
                                fill(*following(head, half), done)
                                done += 1
                        if before := steps_before(head, half, n, LAG + 1):
                            av(*before)

            pe.sem_inc(s_t2, NS)
            pe.sem_inc(s_av, 2)
            for n in range(BM):
                fill(0, 0, n)
            over_heads(pe, heads)
            for b in range(HALF - LAG - 1, HALF):
                if b >= HALF - LAG:
                    t2(HB - 1, 1, b)
                av(HB - 1, 1, b)

        @block.scalar
        def _(act):
            def copy(head, half, n):
                kind, quad, side = FILLS[n]
                act.wait_ge(s_bm, (2 * head + half) * BM + n + 1)
                dst, src = (CT, PC)[kind][half][:, side, :, quad * 64:(quad + 1) * 64], pb[n % 2][:, :]
                if is_far(quad, side):
                    src = src.rearrange("p (b s) -> p b s", b=HALF)
                else:
                    dst, src = dst.rearrange("p b (a s) -> p a b s", a=4), src.rearrange("p (a b s) -> p a b s", a=4, b=HALF)
                act.activation(dst, src, ACT.Copy).then_inc(s_be, 1)

            def values(head, half):
                u = 2 * head + half
                act.wait_ge(s_av, HALF * (u + 1) + 2)
                act.wait_ge(s_ctx, u + 1)
                act.activation(VS[half][:, :, :], pav[:, 0:2 * HALF * VW].rearrange("p (t v) -> p t v", v=VW), ACT.Copy).then_inc(s_vs, 1)

            def exponentials(head, half, b):
                act.wait_ge(s_t2, number(head, half, b) + NS + 1)
                act.wait_ge(s_av, number(head, half, b) + 1)
                act.activation(PT[b % 2][:, :, :], pt2[:, :].rearrange("p (k s) -> p k s", k=2), ACT.Exp).then_inc(s_exp, 1)

            def heads(head, last):
                for half in range(2):
                    u = 2 * head + half
                    act.wait_ge(s_sc, HALF * u + 2)
                    done = 0
                    for n in range(HALF):
                        if n == LAG + 1 and (before := steps_before(head, half, 0, 1)):
                            values(*before[:2])
                        if not (last and half == 1):
                            for _ in range(SHARE[n]):
                                copy(*following(head, half), done)
                                done += 1
                        if before := steps_before(head, half, n, LAG):
                            exponentials(*before)

            act.sem_inc(s_be, 2)
            act.sem_inc(s_exp, 1)
            act.sem_inc(s_vs, 1)
            for n in range(BM):
                copy(0, 0, n)
            over_heads(act, heads)
            for b in range(HALF - LAG, HALF):
                exponentials(HB - 1, 1, b)
            values(HB - 1, 1)

        @block.vector
        def _(dve):
            def mask(head, half, R):
                dve.wait_ge(s_q[half], 32 * (head + 1))
                rows = R[half][:, :].rearrange("p (n s) -> p n s", s=16)
                dve.tensor_tensor(rows, rows, con["own_pos"].unsqueeze(1).to_broadcast([P, HT // 16, 16]), ALU.mult).then_inc(s_masked, 1)

            def results(head, half):
                u = 2 * head + half
                dve.wait_ge(s_vs, u + 2)
                dve.wait_ge(s_ctx, u + 1)
                o = VS[half]
                dve.reciprocal(rec[half][:, :], o[:, :, DB]).then_inc(s_rec, 1)
                dve.wait_ge(s_rec, u + 1)
                dve.tensor_tensor(CTX[:, half * 2 * HALF:(half + 1) * 2 * HALF, bass.ds(head * DB, DB)], o[:, :, 0:DB],
                                  rec[half][:, :].unsqueeze(2).to_broadcast([P, 2 * HALF, DB]), ALU.mult).then_inc(s_ctx, 1)

            def scores(step, half, b):
                dve.wait_ge(s_t1, step + 1)
                z = PC[half][:, :, b, :]
                dve.tensor_tensor(z, pt1[b % 2][:, :].rearrange("p (a k) -> p a k", a=2), z, ALU.add).then_inc(s_z, 1)
                dve.wait_ge(s_z, step + 3)
                dve.wait_ge(s_qk, step + 1)
                dve.wait_ge(s_t2, step + 1)
                dve.sem_inc(s_go_dve, 1)
                for st in range(2):
                    last = dve.tensor_tensor_reduce(out=S[b % NS][:, st, :], in0=pqk[b % 2][:, st * SEQ:(st + 1) * SEQ], in1=PC[half][:, st, b, :],
                                                    scale=1.0, scalar=NEG_HUGE, op0=ALU.add, op1=ALU.max,
                                                    accum_out=mx[:, 2 * b + st:2 * b + st + 1])
                last.then_inc(s_sc, 1)
                dve.wait_ge(s_sc, step + 3)
                dve.tensor_scalar(S[b % NS][:, 0, :], S[b % NS][:, 0, :], mx[:, 2 * b:2 * b + 1], None, ALU.subtract).then_inc(s_sub0, 1)

            def heads(head, last):
                for half in range(2):
                    u = 2 * head + half
                    dve.wait_ge(s_be, BM * (u + 1) + 2)
                    for b in range(HALF):
                        scores(HALF * u + b, half, b)
                        if b == LAG + 1 and (before := steps_before(head, half, 0, 1)):
                            results(*before[:2])
                        if b in (3, 5) and not last:
                            mask(head + 1, half, QR if b == 3 else KR)

            dve.sem_inc(s_z, 2)
            dve.sem_inc(s_sc, 2)
            dve.sem_inc(s_ctx, 2)
            for half in range(2):
                for R in (QR, KR):
                    mask(0, half, R)
            over_heads(dve, heads)
            results(HB - 1, 1)


def return_context(nc, prefix, X, norm, CTX, Wo, con, switch):
    with ExitStack() as stack:
        m = Mem(nc, stack, prefix)
        CXT = m.sb("ctx_t", [P, TOKENS])
        bank = m.banks(8)
        pt, po = bank[0:3], bank[3:5]
        norm.begin(bank[5:8], switch)
        s_t, s_tc, s_o, s_x = (m.sem(n) for n in ("t", "tc", "o", "x"))
        G = TILES // 4
        block = stack.enter_context(nc.Block())

        @block.tensor
        def _(pe):
            for g in range(G + 2):
                if g < G:
                    if g >= 3:
                        pe.wait_ge(s_tc, g - 2)
                    for j in range(4):
                        last = pe.transpose(pt[g % 3][:, j * P:(j + 1) * P], CTX[:, 4 * g + j, :], con["ident"])
                    last.then_inc(s_t, 1)
                if g >= 2:
                    pe.wait_ge(s_tc, g - 1)
                    if g >= 4:
                        pe.wait_ge(s_x, g - 3)
                    for j in range(4):
                        t = 4 * (g - 2) + j
                        last = pe.matmul(po[g % 2][:, j * D:(j + 1) * D], CXT[:, t * P:(t + 1) * P], Wo[:, :], start=True, stop=True)
                    last.then_inc(s_o, 1)
                if g >= 6 and g % 2 == 0:
                    norm.tensor(pe, (g - 6) // 2)
            for q in range(2, norm.GROUPS + 1):
                norm.tensor(pe, q)

        @block.scalar
        def _(act):
            for g in range(G):
                act.wait_ge(s_t, g + 1)
                act.activation(CXT[:, g * 512:(g + 1) * 512], pt[g % 3][:, :], ACT.Copy).then_inc(s_tc, 1)
                if g >= 3 and g % 2 == 1:
                    norm.scalar(act, (g - 3) // 2)
            for q in range(3, norm.GROUPS + 1):
                norm.scalar(act, q)

        @block.vector
        def _(dve):
            for g in range(G):
                dve.wait_ge(s_o, g + 1)
                x = X[:, 4 * g:4 * g + 4, :]
                dve.tensor_tensor(x, po[g % 2][:, :].rearrange("p (t d) -> p t d", t=4), x, ALU.add).then_inc(s_x, 1)
                if g % 2 == 1:
                    dve.wait_ge(s_x, g + 1)
                    norm.vector(dve, g // 2)
            norm.vector(dve, norm.GROUPS)


def bucket(rel):
    mid = BUCKETS // 2
    size = np.where(np.abs(rel) < mid, mid - 1, np.abs(rel)).astype(np.float32)
    far = np.ceil(np.log(size / np.float32(mid)) / np.float32(np.log((MAX_REL - 1) / mid)) * np.float32(mid - 1)) + mid
    return np.where(size <= mid, rel, far * np.sign(rel)).astype(np.int64)


def bucket_onehots():
    x = np.arange(OFFS)
    rows = [np.clip(bucket(off) + BUCKETS, 0, 2 * BUCKETS - 1) for off in (SEQ - 1 - x, x - SEQ + 1)]
    return np.concatenate([np.arange(2 * BUCKETS)[:, None] == r[None, :] for r in rows], axis=1)


INPUTS = ["L0_attn_a_x"] + ["L0_attn_a_" + n for n in ("Wq", "Wm", "W1", "W2", "g1", "b1", "g2", "b2")] + \
    ["L0_attn_b_" + n for n in ("Wq", "bq", "Wk", "bk", "Wv", "bv", "Wo", "bo", "rel_emb", "ln_g", "ln_b", "Wpk", "bpk", "Wpq", "bpq")] + \
    ["L0_ffn_" + n for n in ("switch_w", "switch_b", "w1", "b1", "w2", "b2")]


def shape_constants():
    row = np.arange(P)
    return {
        "ident": np.eye(P),
        "ones": np.ones((P, P)),
        "below": row[:, None] < row[None, :],
        "iota_e": np.broadcast_to(np.arange(E), (P, E)),
        "head_block": row[:, None] // DA == row[None, :] // DA,
        "head_of": row[:, None] // DA == np.arange(HA)[None, :],
        "own_pos": 15 - row[:, None] // DB == np.arange(16)[None, :],
        "iota_b": np.broadcast_to(np.arange(BLOCKS), (P, BLOCKS)),
    }


def program(nc, dram, consts, onehots, out):
    x = dram["L0_attn_a_x"].rearrange("b (u p) d -> p (b u) d", p=P)
    y = out.rearrange("b (u p) d -> p (b u) d", p=P)
    with ExitStack() as stack:
        Mem.whole, Mem.sems = stack, {}
        m = Mem(nc, stack, "all")
        X = m.sb("x", [P, TILES, D])
        width = consts.shape[1]
        C = m.sb("constants", [P, width])
        con, at = {}, 0
        for name, v in shape_constants().items():
            con[name] = C[:, at:at + v.shape[1]]
            at += v.shape[1]
        ffn = {n: dram["L0_ffn_" + n] for n in ("switch_w", "switch_b", "w1", "b1", "w2", "b2")}
        XN = m.sb("xn", [P, TILES, D])
        XT = m.sb("xt", [P, TOKENS])
        norm = TransposedNorm(nc, stack, X, XN, XT, con["ident"])
        s_in = [m.sem(f"in{g}") for g in range(norm.GROUPS)]
        s_con = m.sem("con")
        switch_w = m.sb("switch_w", [P, E])
        switch_b = m.sb("switch_b", [P, E])
        logits = m.sb("logits", [P, TILES, E])
        zero = m.sb("zero", [P, D])
        s_zero = m.sem("zero")
        slots_in = [nc.dram_tensor(f"slots_in{layer}", (SLOTS, D), FP32, kind="Internal").ap() for layer in range(2)]
        s_clear = [m.sem(f"cleared{layer}") for layer in range(2)]
        with ExitStack() as first:
            norm.begin(Mem(nc, first, "first").banks(2))
            block = first.enter_context(nc.Block())

            @block.sync
            def _(sp):
                for g, s_group in enumerate(s_in):
                    tiles = slice(g * norm.GT, (g + 1) * norm.GT)
                    sp.dma_start(X[:, tiles, :], x[:, tiles, :]).then_inc(s_group, 16)
                sp.dma_start(C[:, :], consts).then_inc(s_con, 16)
                sp.dma_start(switch_w[:, :], ffn["switch_w"]).then_inc(s_con, 16)
                sp.dma_start(switch_b[:, :], ffn["switch_b"].partition_broadcast(P)).then_inc(s_con, 16)
                sp.wait_ge(s_zero, 1)
                for slots, s_cleared in zip(slots_in, s_clear):
                    sp.dma_start(slots.rearrange("(p b) d -> p b d", p=P), zero[:, :].unsqueeze(1).to_broadcast([P, BLOCKS, D])).then_inc(s_cleared, 16)

            @block.vector
            def _(dve):
                dve.memset(zero[:, :], 0.0).then_inc(s_zero, 1)
                for g in range(norm.GROUPS):
                    dve.wait_ge(s_in[g], 16)
                    norm.vector(dve, g)
                norm.vector(dve, norm.GROUPS)

            @block.scalar
            def _(act):
                for g in range(norm.GROUPS + 1):
                    norm.scalar(act, g)

            @block.tensor
            def _(pe):
                pe.wait_ge(s_con, 48)
                for g in range(norm.GROUPS):
                    norm.tensor(pe, g)

        linear_attention_layer(nc, "a", X, norm, con, {n: dram["L0_attn_a_" + n] for n in ("Wq", "Wm", "W1", "W2", "g1", "b1", "g2", "b2")},
                               (switch_w[:, :], logits[:, :, :]))

        def experts(layer, finish):
            b = nc.dram_tensor(f"slots_out{layer}", (SLOTS, D), FP32, kind="Internal").ap()
            experts_layer(nc, f"{layer}f", X, norm, con, logits, switch_b, ffn, slots_in[layer], b, s_clear[layer], finish)

        experts(0, None)
        clear_semaphores(nc, [handle for key, handle in Mem.sems.items() if key.startswith("f")])
        scratch = {n: nc.dram_tensor("scratch_" + n, shape, dt, kind="Internal").ap() for n, shape, dt in (
            ("qk", (2, P, TOKENS), FP32), ("parts", (2, 3, P, TOKENS), BF16),
            ("tables", (2, P, OFFS), FP32), ("far", (2, 3, P, 2 * FAR), BF16))}
        disentangled_attention_layer(nc, "d", X, norm, con, {n: dram["L0_attn_b_" + n] for n in (
            "Wq", "bq", "Wk", "bk", "Wv", "bv", "Wo", "bo", "rel_emb", "ln_g", "ln_b", "Wpk", "bpk", "Wpq", "bpq")},
            dict(scratch, onehot=onehots), (switch_w[:, :], logits[:, :, :]))
        experts(1, y)


def kernel(**inputs):
    import concourse.bacc as bacc
    from concourse.bass_utils import run_bass_kernel_spmd

    nc = bacc.Bacc("TRN2", target_bir_lowering=False, num_devices=1)
    arrays, dram = {}, {}
    for name in INPUTS:
        a = np.ascontiguousarray(inputs[name])
        arrays["in_" + name] = a
        dram[name] = nc.dram_tensor("in_" + name, a.shape, mybir.dt.from_np(a.dtype), kind="ExternalInput").ap()
    c = np.concatenate([np.asarray(v, np.float32) for v in shape_constants().values()], axis=1)
    arrays["shape_constants"] = c
    consts = nc.dram_tensor("shape_constants", c.shape, FP32, kind="ExternalInput").ap()
    out = nc.dram_tensor("out", (BATCH, SEQ, D), FP32, kind="ExternalOutput").ap()
    arrays["bucket_onehots"] = bucket_onehots().astype(np.float32)
    onehots = nc.dram_tensor("bucket_onehots", arrays["bucket_onehots"].shape, FP32, kind="ExternalInput").ap()
    program(nc, dram, consts, onehots, out)
    r = run_bass_kernel_spmd(nc, [arrays], core_ids=[0])
    return r.results[0]["out"]
```
